# Optimizing a Trainium2 kernel written in Bass

```python
import numpy as np
import jax
import jax.numpy as jnp

def _softmax(x, axis=-1):
    return jax.nn.softmax(x, axis=axis)

def _gelu(x):
    return jax.nn.gelu(x, approximate=True)

def _silu(x):
    return jax.nn.silu(x)

def _sigmoid(x):
    return jax.nn.sigmoid(x)

def _layernorm(x, axis=-1, eps=1e-05):
    m = jnp.mean(x, axis=axis, keepdims=True)
    v = jnp.var(x, axis=axis, keepdims=True)
    return (x - m) / jnp.sqrt(v + eps)

def _scatter_add(tgt, idx, src, axis=0):
    return tgt.at[idx].add(src)

def _segment_sum(src, seg, n):
    return jax.ops.segment_sum(src, seg, n)
kernel_name = 'mk_gnn_preln_d2_gnn_r8_a77a34'

def setup_inputs(seed: int=0):
    np.random.seed(seed)
    _w = jnp.asarray

    def _rec_inputs():
        import jax
        import jax.numpy as jnp
        _gk = jax.random.key(seed)
        x = -0.000202 + 1 * jax.random.normal(jax.random.fold_in(_gk, 1), (12500, 64), jnp.float32)
        _s = jax.random.randint(jax.random.fold_in(_gk, 2), (200000,), 0, 12500, jnp.int32)
        _d = jax.random.randint(jax.random.fold_in(_gk, 3), (200000,), 0, 12500, jnp.int32)
        _loop = jnp.arange(12500, dtype=jnp.int32)
        src = jnp.concatenate([_s, _d, _loop])
        dst = jnp.concatenate([_d, _s, _loop])
        _o = jnp.argsort(dst, stable=True)
        src = src[_o]
        dst = dst[_o]
        edge_attr_16 = 0.000254156 + 0.999948 * jax.random.normal(jax.random.fold_in(_gk, 11), (412500, 16), jnp.float32)
        return (x, src, dst, edge_attr_16)
    x, src, dst, edge_attr_16 = _rec_inputs()

    def _L0_gnn_setup():
        import jax, jax.numpy as jnp
        import numpy as np
        N = 12500
        E = 200000
        D_IN = 64
        D_OUT = 64
        key = jax.random.key(seed)
        k1, k2, k3 = jax.random.split(key, 3)
        x = jax.random.normal(k1, (N, D_IN), dtype=jnp.float32)
        edge_index = jax.random.randint(k2, (2, E), 0, N, dtype=jnp.int32)
        W = jax.random.normal(k3, (D_IN, D_OUT), dtype=jnp.float32) * (1.0 / np.sqrt(D_IN))
        b = jnp.zeros((D_OUT,), dtype=jnp.float32)
        return {'x': x, 'edge_index': edge_index, 'W': W, 'b': b}
    _L0_gnn_all = _L0_gnn_setup()
    _L0_gnn_in = {k: v for k, v in _L0_gnn_all.items() if k in ('W', 'b')}
    del _L0_gnn_all

    def _L1_gnn_setup():
        import jax, jax.numpy as jnp
        import numpy as np
        N, E = (6250, 100000)
        NODE_DIM, EDGE_DIM, HEADS = (64, 16, 4)
        C = NODE_DIM // HEADS
        NEG_SLOPE = 0.2
        BN_EPS = 1e-05
        key = jax.random.key(seed)
        ks = jax.random.split(key, 12)
        glorot = lambda k, shape: jax.random.normal(k, shape, jnp.float32) * np.sqrt(2.0 / (shape[0] + shape[-1]))
        return {'x': jax.random.normal(ks[0], (N, NODE_DIM), jnp.float32), 'edge_index': jax.random.randint(ks[1], (2, E), 0, N, jnp.int32), 'edge_attr': jax.random.normal(ks[2], (E, EDGE_DIM), jnp.float32), 'W_l': glorot(ks[3], (NODE_DIM, HEADS * C)), 'b_l': jnp.zeros((HEADS * C,), jnp.float32), 'W_r': glorot(ks[4], (NODE_DIM, HEADS * C)), 'b_r': jnp.zeros((HEADS * C,), jnp.float32), 'W_e': glorot(ks[5], (EDGE_DIM, HEADS * C)), 'att': glorot(ks[6], (HEADS, C)), 'bias': jnp.zeros((HEADS * C,), jnp.float32), 'gamma': jnp.ones((NODE_DIM,), jnp.float32), 'beta': jnp.zeros((NODE_DIM,), jnp.float32)}
    _L1_gnn_all = _L1_gnn_setup()
    _L1_gnn_in = {k: v for k, v in _L1_gnn_all.items() if k in ('W_l', 'b_l', 'W_r', 'b_r', 'W_e', 'att', 'bias', 'gamma', 'beta')}
    del _L1_gnn_all
    return {'x': x, 'src': src, 'dst': dst, 'edge_attr_16': edge_attr_16, 'L0_gnn_W': _L0_gnn_in['W'], 'L0_gnn_b': _L0_gnn_in['b'], 'L1_gnn_W_l': _L1_gnn_in['W_l'], 'L1_gnn_b_l': _L1_gnn_in['b_l'], 'L1_gnn_W_r': _L1_gnn_in['W_r'], 'L1_gnn_b_r': _L1_gnn_in['b_r'], 'L1_gnn_W_e': _L1_gnn_in['W_e'], 'L1_gnn_att': _L1_gnn_in['att'], 'L1_gnn_bias': _L1_gnn_in['bias'], 'L1_gnn_gamma': _L1_gnn_in['gamma'], 'L1_gnn_beta': _L1_gnn_in['beta']}

def reference(x, src, dst, edge_attr_16, L0_gnn_W, L0_gnn_b, L1_gnn_W_l, L1_gnn_b_l, L1_gnn_W_r, L1_gnn_b_r, L1_gnn_W_e, L1_gnn_att, L1_gnn_bias, L1_gnn_gamma, L1_gnn_beta):
    import jax
    import jax.numpy as jnp

    def _L0_gnn_ref(x, edge_index, W, b):
        import jax, jax.numpy as jnp
        import numpy as np
        N = 12500
        E = 200000
        D_IN = 64
        D_OUT = 64
        loop = jnp.arange(N, dtype=edge_index.dtype)
        row = jnp.concatenate([edge_index[0], loop])
        col = jnp.concatenate([edge_index[1], loop])
        ew = jnp.ones(row.shape[0], dtype=x.dtype)
        deg = jax.ops.segment_sum(ew, col, num_segments=N)
        dinv = jnp.where(deg > 0, jax.lax.rsqrt(deg), 0.0)
        norm = dinv[row] * dinv[col]
        h = x @ W
        msg = h[row] * norm[:, None]
        out = jax.ops.segment_sum(msg, col, num_segments=N)
        return out + b

    def _L1_gnn_ref(x, edge_index, edge_attr, W_l, b_l, W_r, b_r, W_e, att, bias, gamma, beta):
        import jax, jax.numpy as jnp
        import numpy as np
        N, E = (6250, 100000)
        NODE_DIM, EDGE_DIM, HEADS = (64, 16, 4)
        C = NODE_DIM // HEADS
        NEG_SLOPE = 0.2
        BN_EPS = 1e-05
        src, dst = (edge_index[0], edge_index[1])
        n = x.shape[0]
        xl = (x @ W_l + b_l).reshape(n, HEADS, C)
        xr = (x @ W_r + b_r).reshape(n, HEADS, C)
        e = (edge_attr @ W_e).reshape(-1, HEADS, C)
        g = jax.nn.leaky_relu(xl[src] + xr[dst] + e, NEG_SLOPE)
        logits = jnp.einsum('ehc,hc->eh', g, att)
        amax = jax.ops.segment_max(logits, dst, num_segments=n)
        ex = jnp.exp(logits - amax[dst])
        denom = jax.ops.segment_sum(ex, dst, num_segments=n)
        alpha = ex / (denom[dst] + 1e-16)
        msg = xl[src] * alpha[..., None]
        out = jax.ops.segment_sum(msg, dst, num_segments=n).reshape(n, HEADS * C) + bias
        mean = out.mean(axis=0)
        var = out.var(axis=0)
        out = (out - mean) * jax.lax.rsqrt(var + BN_EPS) * gamma + beta
        return jax.nn.gelu(out + x, approximate=False)
    edge_index = jnp.stack([src, dst])
    h = jnp.maximum(_layernorm(x, axis=-1), 0.0)
    x = x + _L0_gnn_ref(h, edge_index, L0_gnn_W, L0_gnn_b)
    h = jnp.maximum(_layernorm(x, axis=-1), 0.0)
    x = x + _L1_gnn_ref(h, edge_index, edge_attr_16, L1_gnn_W_l, L1_gnn_b_l, L1_gnn_W_r, L1_gnn_b_r, L1_gnn_W_e, L1_gnn_att, L1_gnn_bias, L1_gnn_gamma, L1_gnn_beta)
    return x

_drawn_inputs = setup_inputs


def setup_inputs(seed=0):
    import zlib

    import numpy as np

    out = dict(_drawn_inputs(seed))
    spreads = {'L0_gnn_b': (0.0, 0.1),
     'L1_gnn_b_l': (0.0, 0.487),
     'L1_gnn_b_r': (0.0, 0.423),
     'L1_gnn_bias': (0.0, 0.8),
     'L1_gnn_gamma': (1.0, 0.2),
     'L1_gnn_beta': (0.0, 0.1)}
    factors = {}
    for name, (base, spread) in spreads.items():
        noise = np.random.default_rng([zlib.crc32(name.encode()), seed]).standard_normal(out[name].shape)
        drawn = base * np.exp(spread * noise) if base else spread * noise
        out[name] = jnp.asarray(drawn.astype(out[name].dtype))
    for name, factor in factors.items():
        out[name] = (out[name] * factor).astype(out[name].dtype)
    return out
```

```python
import concourse.bass as bass
from concourse import mybir
from contextlib import ExitStack

F32 = mybir.dt.float32
BF16 = mybir.dt.bfloat16
I32 = mybir.dt.int32
I16 = mybir.dt.int16
ALU = mybir.AluOpType
ACT = mybir.ActivationFunctionType
AX = mybir.AxisListType
ENG = mybir.EngineType

N = 12500
E = 412500
C = 64
H = 4
HC = C // H
ED = 16
T = 128
GT = 8
SLOTS = 4
GE = GT * T
BODIES = -(-E // (SLOTS * GE))
GROUPS = BODIES * SLOTS
BLK = -(-(GROUPS * GT) // T)
TILES = BLK * T
NP, NJ = 125, 100
JC = 4
CHUNKS = NJ // JC
NW = N + T
CD = C + H
BIG = 1.0e38
SLOPE = 0.2
LN_EPS = 1e-5
BN_EPS = 1e-5
DEN_EPS = 1e-16
PARTS = 5
JP = NJ // PARTS
JE = 10
ENDS = NJ // JE


def gnn_kernel(nc, x, src_cols, dst_rows, dst_cols, first_dst, last_dst, edge_rows, w0, b0, w_l, b_l, w_r, b_r, w_e,
               att, bias, gamma, beta, out):
    ctx = ExitStack()
    with ctx:
        def sb(name, shape, dt=F32):
            return ctx.enter_context(nc.sbuf_tensor(name, shape, dt))

        def pb(name, shape, dt=F32):
            return ctx.enter_context(nc.psum_tensor(name, shape, dt))

        def sem(name):
            return ctx.enter_context(nc.semaphore(name))

        def dram(name, shape, dt=F32):
            return nc.dram_tensor(name, shape, dt, kind="Internal").ap()

        loc_rows = dram("loc_rows", [TILES, T], BF16)
        start_rows = dram("start_rows", [TILES, H, T], BF16)
        agg_table = dram("agg_table", [N, C])
        xl_table = dram("xl_table", [N, C])
        xr_table = dram("xr_table", [NW, 3, C], BF16)

        xs = sb("xs", [NP, NJ * C])
        hs_all = sb("hs", [T, NJ * C])
        hs = hs_all[0:NP, :]
        arena = sb("arena", [T, NW])
        acc0 = arena[0:C, :]
        acc1 = arena[0:CD, :]
        loc = sb("loc", [T, TILES], BF16)
        lastm = sb("lastm", [T, TILES], BF16)
        cont = sb("cont", [CD, TILES], BF16)
        single_prev = sb("single_prev", [CD, TILES], BF16)
        wide = sb("wide", [CD, TILES], BF16)
        by_tiles = sb("by_tiles", [C + 1, TILES], BF16)
        chain = by_tiles[0:H, :]
        base_row = by_tiles[C:C + 1, :].bitcast(I16)

        sizes = dict(g=SLOTS * GT * C, xrw=SLOTS * GT * 3 * C // 2, oht=GE, oh=2 * GE, msg=2 * GT * CD,
                     lr=GT * C, locr=SLOTS * GE // 2, ea=SLOTS * T, start=SLOTS * (T + 2) // 2)
        ring = sb("ring", [T, sum(sizes.values())])
        offs, at = {}, 0
        for key, size in sizes.items():
            offs[key] = at
            at += size

        def piece(key):
            return ring[:, offs[key]:offs[key] + sizes[key]]

        gbuf = piece("g").rearrange("p (s t c) -> p s t c", s=SLOTS, t=GT)
        xrw = piece("xrw").bitcast(BF16).rearrange("p (s t k c) -> p s t k c", s=SLOTS, t=GT, k=3)
        oht = piece("oht").bitcast(BF16).rearrange("p (b e) -> p b e", b=2)
        oh = piece("oh").rearrange("p (b t n) -> p b t n", b=2, t=GT)
        msg = piece("msg").rearrange("p (b t c) -> p b t c", b=2, t=GT)
        lr = piece("lr")
        locr = piece("locr").bitcast(BF16).rearrange("p (s e) -> p s e", s=SLOTS)
        eat = piece("ea").rearrange("p (s e) -> p s e", s=SLOTS)
        start = piece("start").bitcast(BF16).rearrange("p (s e) -> p s e", s=SLOTS)

        idx = sb("idx", [T, SLOTS, GT], I32)
        lg = sb("lg", [T, GT * H])
        fwd = sb("fwd", [GT * H, T])
        segmax = sb("segmax", [GT * H, T])
        diff = sb("diff", [GT * H, T + 1])
        expt = sb("expt", [GT * H, T + 1])
        tails = sb("tails", [GT * H, GT])
        resc = sb("resc", [GT * H, GT])
        hist = sb("hist", [GT * H, 1])
        runmax = sb("runmax", [H, GT + 1])
        before = sb("before", [H, GT])
        beforex = sb("beforex", [H, GT * H])
        keep = sb("keep", [CD, 2, 2, GT])
        lastsum = sb("lastsum", [CD, 2, GT + 1])
        joined = sb("joined", [CD, GT])
        firsts = sb("firsts", [CD, 2, GT])

        iota_f = sb("iota_f", [T, T])
        iota_b = sb("iota_b", [T, T], BF16)
        part_i = sb("part_i", [T, 1], I32)
        part_f = sb("part_f", [T, 1])
        ident = sb("ident", [T, T])
        ones = sb("ones", [T, T])
        ones_b = sb("ones_b", [T, T], BF16)
        node_f = sb("node_f", [NP, NJ + 1])
        head_i = sb("head_i", [GT * H, 1], I32)
        head_f = sb("head_f", [GT * H, 1])
        tile_i = sb("tile_i", [GT * H, 1], I32)
        tile_f = sb("tile_f", [GT * H, 1])
        chan_f = sb("chan_f", [GT * H, CD])
        by_tile = sb("by_tile", [GT * H, GT])
        by_head = sb("by_head", [GT * H, H])
        by_chan = sb("by_chan", [GT * H, CD])
        w0_s = sb("w0_s", [C, C])
        wlr = sb("wlr", [C, 2 * C])
        blr = sb("blr", [1, 2 * C])
        web = sb("web", [T, GT * C])
        att_s = sb("att_s", [T, C])
        b0_s = sb("b0_s", [NP, C])
        bias_s = sb("bias_s", [NP, C])
        gam_s = sb("gam_s", [NP, C])
        bet_s = sb("bet_s", [NP, C])
        eps_ln = sb("eps_ln", [NP, 1])
        eps_bn = sb("eps_bn", [NP, 1])
        rowblk = sb("rowblk", [NP, NJ + 1])
        rowidx = sb("rowidx", [NP, NJ + 1], I32)
        below = sb("below", [NP, NJ + 1])
        dinv = sb("dinv", [NP, NJ])
        mean = sb("mean", [NP, NJ])
        rstd = sb("rstd", [NP, NJ])
        stat = sb("stat", [NP, 3, C])
        pa = sb("pa", [T, BLK])
        jb = sb("jb", [T, BLK])

        ps_g = pb("ps_g", [T, 2, GT * C])
        ps_s = pb("ps_s", [T, 2, GE])
        ps_e = pb("ps_e", [T, 512])
        rows_to = ps_g[:, 0, :]
        ext_ps = ps_g[:, 1, 0:GT * H]
        resc_ps = ps_g[0:CD, 1, T:T + GT]
        lt_ps = ps_e[0:GT * H, 0:T]
        tails_ps = ps_e[0:H, 2 * T:2 * T + GT]
        hist_ps = ps_e[0:GT * H, 3 * T:3 * T + 1]

        def blocks(ap):
            return ap.rearrange("p (b e) -> p b e", e=T)

        dst_i = arena[:, 0:TILES].bitcast(I32)
        dst_f = arena[:, 0:TILES]
        first_all = arena[:, TILES:2 * TILES].bitcast(I32)
        last_all = arena[:, 2 * TILES:3 * TILES].bitcast(I32)
        squares = arena[0:NP, 3 * TILES:3 * TILES + NJ * C // 4].rearrange("p (j c) -> p j c", c=C)
        found = ring[0:NP, 0:2 * GE].bitcast(I32).rearrange("p (b t e) -> p b t e", b=2, t=GT)
        less = ring[0:NP, 2 * GE:3 * GE].rearrange("p (t e) -> p t e", t=GT)
        h_turn = ring[0:C, 3 * GE:3 * GE + 2 * JC * NP].rearrange("p (b k q) -> p b k q", b=2, k=JC)
        dst_t = ring[:, offs["oht"]:offs["oht"] + TILES].bitcast(I32)
        stages = sum(sizes.values()) - TILES
        loc_b = ring[:, stages:stages + TILES // 2].bitcast(BF16)
        start_b = ring[:, stages + TILES // 2:stages + TILES].bitcast(BF16)
        equal_all = ring[0:CD, offs["oht"]:offs["oht"] + TILES]
        ge_b = hs_all[:, 0:BLK * (NP + 1) // 2].bitcast(BF16).rearrange("p (b q) -> p b q", b=BLK)
        in_b = hs_all[:, 1700:1700 + BLK * NP // 2].bitcast(BF16).rearrange("p (b q) -> p b q", b=BLK)
        jlt = hs_all[:, 3400:3400 + BLK * (NJ + 1) // 2].bitcast(BF16).rearrange("p (b j) -> p b j", b=BLK)
        iota_i = hs_all[:, 4800:4800 + T].bitcast(I32)
        node_i = hs_all[0:NP, 4960:4960 + NJ + 1].bitcast(I32)
        hund_i = hs_all[:, 5100:5100 + NP + 1].bitcast(I32)
        chan_i = hs_all[0:GT * H, 5260:5260 + CD].bitcast(I32)
        hund_f = hs_all[:, 5360:5360 + NP + 1]
        zeros = hs_all[:, 5600:5600 + 3 * C // 2].bitcast(BF16)

        def acc_to(c):
            return ps_s[0:NP, c % 2, GE // 2:GE // 2 + JC * C]

        lr_keep = ring[0:NP, offs["oht"]:offs["oht"] + 2 * JC * C].rearrange("p (b j c) -> p b j c", b=2, j=JC)
        xr_rest = ring[0:NP, offs["oht"] + 2 * JC * C:offs["oht"] + 4 * JC * C].rearrange("p (b j c) -> p b j c", b=2, j=JC)
        xr_parts = ring[0:NP, offs["oh"]:offs["oh"] + 3 * JC * C].bitcast(BF16).rearrange(
            "p (b j k c) -> p b j k c", b=2, j=JC, k=3)
        squares1 = ring[0:NP, offs["msg"]:offs["msg"] + 2 * JP * C].rearrange("p (b j c) -> p b j c", b=2, c=C)
        y = ring[0:NP, 0:NJ * C]
        y3 = y.rearrange("p (j c) -> p j c", c=C)
        rden = ring[0:NP, 6400:6400 + 2 * JE * H].rearrange("p (b j h) -> p b j h", b=2, j=JE)
        sq = ring[0:NP, 6656:6656 + 2 * JP * C].rearrange("p (b k) -> p b k", b=2)
        sq_sum = ring[0:NP, 9600:9600 + PARTS * C].rearrange("p (q c) -> p q c", c=C)

        xs3 = xs[:, :].rearrange("p (j c) -> p j c", c=C)
        hs3 = hs[:, :].rearrange("p (j c) -> p j c", c=C)
        acc0_n = acc0[:, 0:N].rearrange("c (p j) -> c j p", j=NJ)
        acc1_n = acc1[:, 0:N].rearrange("c (p j) -> c j p", j=NJ)
        agg_n, xl_n, out_n = (t.rearrange("(p j) c -> p j c", j=NJ) for t in (agg_table, xl_table, out))
        xr_n = xr_table[0:N].rearrange("(p j) k c -> p j k c", j=NJ)

        dst_in, ends_in, dstt_in, x_in, w_in = sem("dst_in"), sem("ends_in"), sem("dstt_in"), sem("x_in"), sem("w_in")
        consts_set, consts_f = sem("consts_set"), sem("consts_f")
        v_step = sem("v_step")
        dstf_set, loc_set, start_set, flags_set = sem("dstf_set"), sem("loc_set"), sem("start_set"), sem("flags_set")
        loc_out, start_out, pad_out = sem("loc_out"), sem("start_out"), sem("pad_out")
        onehots_set, rows_ps, rows_set = sem("onehots_set"), sem("rows_ps"), sem("rows_set")
        found_in = [sem("found_in0"), sem("found_in1")]
        counted, deg_set, root_set, table_set, table_out = (
            sem("counted"), sem("deg_set"), sem("root_set"), sem("table_set"), sem("table_out"))
        var_set, std_set, h_set = sem("var_set"), sem("std_set"), sem("h_set")
        h_t, ht_set, lin_ps, lin_kept = sem("h_t"), sem("ht_set"), sem("lin_ps"), sem("lin_kept")
        idx_in = [[sem(f"idx{k}_in{s}") for s in range(SLOTS)] for k in range(2)]
        gathered = [[sem(f"gathered{k}_{s}") for s in range(SLOTS)] for k in range(2)]
        slot_free = sem("slot_free")
        oh_set = [sem("oh_set0"), sem("oh_set1")]
        summed = [sem("summed0"), sem("summed1")]
        lastsum_set, prior_set, joined_set, firsts_sb, firsts_set, acc_set = (
            [sem(f"{n}{k}") for k in range(2)] for n in
            ("lastsum_set", "prior_set", "joined_set", "firsts_sb", "firsts_set", "acc_set"))
        keep_set, drop_set = [sem("keep_set0"), sem("keep_set1")], [sem("drop_set0"), sem("drop_set1")]
        acc_t, x1_set, cent1_set, sq1_set = sem("acc_t"), sem("x1_set"), sem("cent1_set"), sem("sq1_set")
        h1_t, h1t_set, lr_ps, parts_set, rest_set, xl_kept, xr_kept = (
            sem("h1_t"), sem("h1t_set"), sem("lr_ps"), sem("parts_set"), sem("rest_set"), sem("xl_kept"), sem("xr_kept"))
        lr_out = [sem("lr_out0"), sem("lr_out1")]
        xrw_in = [sem(f"xrw_in{s}") for s in range(SLOTS)]
        edge_in = [sem(f"edge_in{s}") for s in range(SLOTS)]
        oht_set, g_made, row_set, leaky_set, prod_set, logits_set = (
            sem("oht_set"), sem("g_made"), sem("row_set"), sem("leaky_set"), sem("prod_set"), sem("logits_set"))
        lt_made, fwd_set, tails_set, tails_made, carry_set, runmax_set, before_set, beforex_set = (
            sem("lt_made"), sem("fwd_set"), sem("tails_set"), sem("tails_made"), sem("carry_set"),
            sem("runmax_set"), sem("before_set"), sem("beforex_set"))
        hist_made, hist_set, fwdh_set, segmax_set, diff_set, exp_set, ext_made, resc_set, msg_set = (
            sem("hist_made"), sem("hist_set"), sem("fwdh_set"), sem("segmax_set"), sem("diff_set"), sem("exp_set"),
            sem("ext_made"), sem("resc_set"), sem("msg_set"))
        num_t, y_set, sum_ps, cent_set, sq_set, sqsum_set, sqsum_ps, gelu_in, gelu_set, y_done, out_done = (
            sem("num_t"), sem("y_set"), sem("sum_ps"), sem("cent_set"), sem("sq_set"), sem("sqsum_set"),
            sem("sqsum_ps"), sem("gelu_in"), sem("gelu_set"), sem("y_done"), sem("out_done"))

        N_CONST = 12
        N_W = 10 + GT
        COUNTS = -(-(NJ + 1) // GT)

        def wait(eng, s, value):
            if not isinstance(value, int) or value > 0:
                eng.wait_ge(s, value)

        def each_body(eng, body):
            body(0)
            with eng.Fori(1, BODIES - 1) as i:
                body(i)
            body(BODIES - 1)

        def behind(i, s, lag):
            g = i * SLOTS + s - lag
            if isinstance(i, int) and not 0 <= g < GROUPS:
                return None
            return g, (s - lag) % SLOTS, i + (s - lag) // SLOTS

        def chunks_of(q):
            return range(q * JP // JC, (q + 1) * JP // JC) if 0 <= q < PARTS else ()

        def tile_bases(engine, g):
            return nc.values_load_multi_w_load_instructions(
                base_row[0:1, bass.ds(g * GT, GT)], engines=[engine], min_val=0, max_val=N,
                skip_runtime_bounds_check_because="dst holds node numbers")[1]

        block = ctx.enter_context(nc.Block())

        @block.sync
        def _(sp):
            sp.dma_start(blocks(dst_i), dst_rows.rearrange("(b p) e -> p b e", p=T)).then_inc(dst_in, 16)
            sp.dma_start(xs[:, :], x.rearrange("(p j) c -> p (j c)", j=NJ)).then_inc(x_in, 16)
            sp.dma_start(dst_t, dst_cols).then_inc(dstt_in, 16)
            sp.dma_start(first_all, first_dst.partition_broadcast(T)).then_inc(ends_in, 16)
            sp.dma_start(last_all, last_dst.partition_broadcast(T)).then_inc(ends_in, 16)

            def layer0(i):
                for s in range(SLOTS):
                    wait(sp, gathered[0][s], i * (16 * GT))
                    sp.dma_start(idx[:, s, :], src_cols[:, bass.ds((i * SLOTS + s) * GT, GT)]).then_inc(idx_in[0][s], 16)

            layer0(0)
            for q in range(PARTS):
                sp.wait_ge(table_set, q + 1)
                sp.dma_start(agg_n[:, q * JP:(q + 1) * JP, :], hs3[:, q * JP:(q + 1) * JP, :]).then_inc(table_out, 16)
            sp.wait_ge(loc_set, 1)
            sp.dma_start(loc_rows.rearrange("(b p) e -> p b e", p=T), blocks(loc_b)).then_inc(loc_out, 16)
            sp.wait_ge(start_set, 1)
            for h in range(H):
                sp.dma_start(start_rows[:, h, :].rearrange("(b p) e -> p b e", p=T), blocks(start_b)).then_inc(start_out, 16)
            with sp.Fori(1, BODIES - 1) as i:
                layer0(i)
            layer0(BODIES - 1)

            for c in range(CHUNKS):
                sp.wait_ge(xl_kept, c + 1)
                sp.wait_ge(xr_kept, c + 1)
                sp.dma_start(xl_n[:, c * JC:(c + 1) * JC, :], lr_keep[:, c % 2]).then_inc(lr_out[c % 2], 16)
                sp.dma_start(xr_n[:, c * JC:(c + 1) * JC], xr_parts[:, c % 2]).then_inc(lr_out[c % 2], 16)
            sp.wait_ge(pad_out, 16)
            sp.wait_ge(loc_out, 16)
            sp.wait_ge(start_out, 16 * H)
            for b in range(2):
                sp.wait_ge(lr_out[b], 32 * len(range(b, CHUNKS, 2)))

            def layer1(i):
                for s in range(SLOTS):
                    g = i * SLOTS + s
                    wait(sp, gathered[1][s], i * (16 * GT))
                    if isinstance(i, int) and i == 0:
                        sp.wait_ge(gathered[0][s], BODIES * 16 * GT)
                    sp.dma_start(idx[:, s, :], src_cols[:, bass.ds(g * GT, GT)]).then_inc(idx_in[1][s], 16)
                    bases = tile_bases(ENG.SP, g)
                    wait(sp, g_made, g - SLOTS + 1)
                    wait(sp, segmax_set, g - SLOTS + 1)
                    sp.dma_start(eat[:, s, :], edge_rows[bass.ds(g * T, T), :]).then_inc(edge_in[s], 16)
                    sp.dma_start(locr[:, s, :], loc_rows[bass.ds(g * GT, GT), :].rearrange(
                        "t e -> (t e)").partition_broadcast(T)).then_inc(edge_in[s], 16)
                    sp.dma_start(start[0:GT * H, s, 0:T], start_rows[bass.ds(g * GT, GT), :, :].rearrange(
                        "t h e -> (t h) e")).then_inc(edge_in[s], 16)
                    for t in range(GT):
                        sp.dma_start(xrw[:, s, t], xr_table[bass.ds(bases[t], T)]).then_inc(xrw_in[s], 16)

            each_body(sp, layer1)

            for q in range(PARTS):
                sp.wait_ge(y_done, q + 1)
                at = slice(q * JP, (q + 1) * JP)
                sp.dma_start(out_n[:, at, :], hs3[:, at, :]).then_inc(out_done, 16)
            sp.wait_ge(out_done, 16 * PARTS)

        @block.gpsimd
        def _(pool):
            g = nc.gpsimd
            g.iota(iota_i[:], [[1, T]], base=0, channel_multiplier=0).then_inc(consts_set, 1)
            g.iota(part_i[:], [[1, 1]], base=0, channel_multiplier=1).then_inc(consts_set, 1)
            g.iota(node_i[:], [[1, NJ + 1]], base=0, channel_multiplier=NJ).then_inc(consts_set, 1)
            g.iota(hund_i[:], [[NJ, NP + 1]], base=0, channel_multiplier=0).then_inc(consts_set, 1)
            g.iota(chan_i[:, 0:C], [[1, H], [0, HC]], base=0, channel_multiplier=0).then_inc(consts_set, 1)
            g.iota(chan_i[:, C:CD], [[1, H]], base=0, channel_multiplier=0).then_inc(consts_set, 1)
            g.memset(ones[:], 1.0).then_inc(consts_set, 1)
            g.memset(ones_b[:], 1.0).then_inc(consts_set, 1)
            g.memset(eps_ln[:], LN_EPS).then_inc(consts_set, 1)
            g.memset(eps_bn[:], BN_EPS).then_inc(consts_set, 1)
            g.memset(zeros, 0.0).then_inc(consts_set, 1)
            g.memset(web[:], 0.0).then_inc(consts_set, 1)

            pool.wait_ge(rows_set, 1)
            for k in range(COUNTS):
                wait(pool, counted, k - 1)
                for t in range(min(GT, NJ + 1 - k * GT)):
                    j = k * GT + t
                    g.indirect_dma_start(out=found[:, k % 2, t, :], out_offset=None, in_=dst_rows,
                                         in_offset=bass.IndirectOffsetOnAxis(ap=rowidx[:, j:j + 1], axis=0)
                                         ).then_inc(found_in[k % 2], 16)

            def gathers(layer, table, ready, used):
                def body(i):
                    for s in range(SLOTS):
                        wait(pool, used, i * SLOTS + s - SLOTS + 1)
                        pool.wait_ge(idx_in[layer][s], 16 * (i + 1))
                        ready()
                        pool.sem_inc(slot_free, 1)
                        for t in range(GT):
                            g.indirect_dma_start(out=gbuf[:, s, t, :], out_offset=None, in_=table,
                                                 in_offset=bass.IndirectOffsetOnAxis(ap=idx[:, s, t:t + 1], axis=0)
                                                 ).then_inc(gathered[layer][s], 16)
                each_body(pool, body)

            pool.wait_ge(counted, COUNTS)
            gathers(0, agg_table, lambda: pool.wait_ge(table_out, 16 * PARTS), summed[0])
            for b in range(2):
                pool.wait_ge(lr_out[b], 32 * len(range(b, CHUNKS, 2)))
            gathers(1, xl_table, lambda: pool.wait_ge(lr_out[0], 32 * len(range(0, CHUNKS, 2))), msg_set)

        @block.vector
        def _(dve):
            v = nc.vector
            steps = [0]

            def link(ins):
                steps[0] += 1
                ins.then_inc(v_step, 1)
                dve.wait_ge(v_step, steps[0])

            dve.wait_ge(consts_set, N_CONST)
            v.tensor_copy(iota_f[:], iota_i[:])
            v.tensor_copy(iota_b[:], iota_i[:])
            v.tensor_copy(part_f[:], part_i[:])
            v.tensor_copy(node_f[:], node_i[:])
            v.tensor_copy(hund_f[:], hund_i[:])
            v.tensor_copy(chan_f[:], chan_i[:])
            v.tensor_scalar(head_i[:], part_i[0:GT * H, :], H - 1, None, ALU.bitwise_and)
            link(v.tensor_scalar(tile_i[:], part_i[0:GT * H, :], H.bit_length() - 1, None, ALU.arith_shift_right))
            v.tensor_copy(head_f[:], head_i[:])
            link(v.tensor_copy(tile_f[:], tile_i[:]))
            v.tensor_scalar(ident[:], iota_f[:], part_f[:, 0:1], None, ALU.is_equal)
            v.tensor_scalar(by_tile[:], iota_f[0:GT * H, 0:GT], tile_f[:, 0:1], None, ALU.is_equal)
            v.tensor_scalar(by_head[:], iota_f[0:GT * H, 0:H], head_f[:, 0:1], None, ALU.is_equal)
            v.tensor_scalar(by_chan[:], chan_f[:], head_f[:, 0:1], None, ALU.is_equal)
            v.memset(lastsum[:], 0.0)
            v.memset(firsts[:], 0.0)
            v.memset(runmax[:], -BIG).then_inc(consts_f, 1)

            dve.wait_ge(dst_in, 16)
            v.tensor_copy(dst_f, dst_i).then_inc(dstf_set, 1)
            dve.wait_ge(dstf_set, 1)
            base = blocks(dst_f)[:, :, 0]
            base_q = base.unsqueeze(2).to_broadcast([T, BLK, NP + 1])
            hund = hund_f[:].unsqueeze(1).to_broadcast([T, BLK, NP + 1])
            link(v.tensor_tensor(ge_b, base_q, hund, ALU.is_ge))
            link(v.tensor_reduce(pa[:], ge_b[:, :, 1:NP + 1], AX.X, ALU.add))
            v.tensor_tensor(in_b, ge_b[:, :, 0:NP], ge_b[:, :, 1:NP + 1], ALU.subtract)
            link(v.scalar_tensor_tensor(jb[:], pa[:], -float(NJ), base, ALU.mult, ALU.add))
            v.tensor_tensor(jlt, jb[:].unsqueeze(2).to_broadcast([T, BLK, NJ + 1]),
                            iota_f[:, 0:NJ + 1].unsqueeze(1).to_broadcast([T, BLK, NJ + 1]), ALU.is_lt)
            v.tensor_tensor(ge_b, base_q, hund, ALU.is_lt).then_inc(onehots_set, 1)
            dve.wait_ge(rows_ps, 1)
            link(v.tensor_scalar(rowblk[:], ps_g[0:NP, 0, 0:NJ + 1], -1.0, 0.0, ALU.add, ALU.max))
            v.tensor_copy(rowidx[:], rowblk[:]).then_inc(rows_set, 1)

            def count(k):
                n = min(GT, NJ + 1 - k * GT)
                at = slice(k * GT, k * GT + n)
                dve.wait_ge(found_in[k % 2], sum(16 * min(GT, NJ + 1 - r * GT) for r in range(k % 2, k + 1, 2)))
                wait(dve, counted, k)
                link(v.tensor_tensor(less[:, 0:n, :], found[:, k % 2, 0:n, :],
                                     node_f[:, at].unsqueeze(2).to_broadcast([NP, n, T]), ALU.is_lt))
                v.tensor_reduce(below[:, at], less[:, 0:n, :], AX.X, ALU.add).then_inc(counted, 1)

            dve.wait_ge(x_in, 16)
            dve.wait_ge(w_in, 16 * N_W)
            dve.wait_ge(pad_out, 16)
            link(v.tensor_reduce(mean[:], xs3, AX.X, ALU.add))
            link(v.tensor_scalar(mean[:], mean[:], 1.0 / C, None, ALU.mult))
            link(v.tensor_tensor(hs3, xs3, mean[:].unsqueeze(2).to_broadcast([NP, NJ, C]), ALU.subtract))
            for q in range(4):
                at = slice(q * NJ // 4, (q + 1) * NJ // 4)
                if q % 2 == 0:
                    count(q // 2)
                link(v.tensor_tensor(squares, hs3[:, at, :], hs3[:, at, :], ALU.mult))
                link(v.tensor_reduce(rstd[:, at], squares, AX.X, ALU.add))
            v.tensor_scalar(rstd[:], rstd[:], 1.0 / C, None, ALU.mult).then_inc(var_set, 1)
            count(2)
            dve.wait_ge(std_set, 1)
            link(v.reciprocal(rstd[:], rstd[:]))
            v.scalar_tensor_tensor(hs3, hs3, 0.0, rstd[:].unsqueeze(2).to_broadcast([NP, NJ, C]),
                                   ALU.max, ALU.mult).then_inc(h_set, 1)
            count(3)
            dve.wait_ge(dstt_in, 16)
            dve.wait_ge(ends_in, 32)
            v.tensor_tensor(loc[:], dst_t, first_all, ALU.subtract)
            v.tensor_tensor(lastm[:], dst_t, last_all, ALU.is_equal)
            count(4)
            v.tensor_copy(base_row, first_all[C:C + 1, :])
            v.tensor_tensor(blocks(loc_b), blocks(dst_f), base.unsqueeze(2).to_broadcast([T, BLK, T]),
                            ALU.subtract).then_inc(loc_set, 1)
            v.memset(blocks(start_b)[:, :, 0:1], 0.0)
            link(v.tensor_tensor(blocks(start_b)[:, :, 1:T], blocks(dst_f)[:, :, 1:T], blocks(dst_f)[:, :, 0:T - 1],
                                 ALU.not_equal))
            count(5)
            v.tensor_scalar(start_b, start_b, -BIG, None, ALU.mult).then_inc(start_set, 1)
            v.memset(cont[:, 0:1], -BIG)
            v.memset(single_prev[:, 0:1], 0.0)
            link(v.tensor_tensor(equal_all[:, 1:TILES], first_all[0:CD, 1:TILES], last_all[0:CD, 0:TILES - 1], ALU.is_equal))
            count(6)
            link(v.tensor_scalar(cont[:, 1:TILES], equal_all[:, 1:TILES], 2 * BIG, -BIG, ALU.mult, ALU.add))
            link(v.tensor_tensor(equal_all, last_all[0:CD, :], first_all[0:CD, :], ALU.subtract))
            count(7)
            v.tensor_scalar(single_prev[:, 1:TILES], equal_all[:, 0:TILES - 1], 0.0, None, ALU.is_equal)
            link(v.tensor_scalar(wide[:], equal_all, float(T - 1), None, ALU.is_equal))
            count(8)
            link(v.tensor_scalar(equal_all[0:H, :], equal_all[0:H, :], 0.0, None, ALU.is_equal))
            link(v.tensor_scalar(equal_all[0:H, :], equal_all[0:H, :], 2 * BIG, -BIG, ALU.mult, ALU.add))
            v.tensor_tensor(chain, cont[0:H, :], equal_all[0:H, :], ALU.min).then_inc(flags_set, 1)
            for k in range(9, COUNTS):
                count(k)

            dve.wait_ge(counted, COUNTS)
            link(v.scalar_tensor_tensor(below[:], rowblk[:], float(T), below[:], ALU.mult, ALU.add))
            v.tensor_tensor(dinv[:], below[:, 1:NJ + 1], below[:, 0:NJ], ALU.subtract).then_inc(deg_set, 1)
            dve.wait_ge(root_set, 1)
            link(v.reciprocal(dinv[:], dinv[:]))
            dve.wait_ge(lin_kept, CHUNKS)
            for q in range(PARTS):
                at = slice(q * JP, (q + 1) * JP)
                v.tensor_tensor(hs3[:, at, :], hs3[:, at, :], dinv[:, at].unsqueeze(2).to_broadcast([NP, JP, C]),
                                ALU.mult).then_inc(table_set, 1)
            link(v.tensor_tensor(xs3, xs3, b0_s[:].unsqueeze(1).to_broadcast([NP, NJ, C]), ALU.add))
            dve.wait_ge(table_out, 16 * PARTS)
            link(v.tensor_tensor(hs3, hs3, dinv[:].unsqueeze(2).to_broadcast([NP, NJ, C]), ALU.mult))
            link(v.tensor_tensor(xs3, xs3, hs3, ALU.add))
            dve.wait_ge(flags_set, 1)
            dve.wait_ge(loc_out, 16)
            dve.wait_ge(start_out, 16 * H)

            def onehot(layer, g, b):
                wait(dve, summed[layer], g - 1)
                v.tensor_tensor(oh[:, b, :, 0:T - 1], loc[:, bass.ds(g * GT, GT)].unsqueeze(2).to_broadcast([T, GT, T - 1]),
                                iota_b[:, 0:T - 1].unsqueeze(1).to_broadcast([T, GT, T - 1]), ALU.is_equal)
                v.tensor_copy(oh[:, b, :, T - 1], lastm[:, bass.ds(g * GT, GT)]).then_inc(oh_set[layer], 1)

            def windows(b, rows):
                return ps_s[0:rows, b, :].rearrange("p (t n) -> p t n", n=T)

            def carry_lasts(layer, w, b, rows):
                dve.wait_ge(summed[layer], w + 1)
                v.tensor_copy(lastsum[0:rows, b, 1:GT + 1], windows(b, rows)[:, :, T - 1])
                v.tensor_copy(lastsum[0:rows, b, 0:1], lastsum[0:rows, 1 - b, GT:GT + 1]).then_inc(lastsum_set[layer], 1)

            def carry_wide(layer, w, b, rows):
                dve.wait_ge(lastsum_set[layer], w + 1)
                v.tensor_tensor(windows(b, rows)[:, :, T - 1], windows(b, rows)[:, :, T - 1], wide[0:rows, bass.ds(w * GT, GT)],
                                ALU.mult).then_inc(firsts_set[layer], 1)

            def carry_drop(layer, w, b, rows):
                dve.wait_ge(drop_set[layer], w + 1)
                dve.wait_ge(lastsum_set[layer], w + 1)
                v.tensor_tensor(joined[0:rows, :], keep[0:rows, b, 1, :], lastsum[0:rows, b, 0:GT],
                                ALU.mult).then_inc(prior_set[layer], 1)

            def carry_own(layer, w, b, rows):
                dve.wait_ge(prior_set[layer], w + 1)
                v.tensor_tensor(joined[0:rows, :], joined[0:rows, :], windows(b, rows)[:, :, 0], ALU.add).then_inc(joined_set[layer], 1)

            def carry_scan(layer, w, b, rows):
                dve.wait_ge(joined_set[layer], w + 1)
                wait(dve, firsts_sb[layer], w)
                v.tensor_tensor_scan(firsts[0:rows, b, :], keep[0:rows, b, 0, :], joined[0:rows, :],
                                     firsts[0:rows, 1 - b, GT - 1:GT], ALU.mult, ALU.add).then_inc(firsts_sb[layer], 1)

            def carry_firsts(layer, w, b, rows):
                dve.wait_ge(firsts_sb[layer], w + 1)
                v.tensor_copy(windows(b, rows)[:, :, 0], firsts[0:rows, b, :]).then_inc(firsts_set[layer], 1)

            def layer0(i, s):
                n, w = behind(i, s, 0), behind(i, s, 1)
                if n is not None:
                    onehot(0, n[0], s % 2)
                if w is not None:
                    w, b = w[0], w[1] % 2
                    at = bass.ds(w * GT, GT)
                    v.scalar_tensor_tensor(keep[0:C, b, 0, :], cont[0:C, at], 0.0, single_prev[0:C, at],
                                           ALU.is_gt, ALU.mult).then_inc(keep_set[0], 1)
                    carry_lasts(0, w, b, C)
                    dve.wait_ge(keep_set[0], w + 1)
                    v.scalar_tensor_tensor(keep[0:C, b, 1, :], cont[0:C, at], 0.0, keep[0:C, b, 0, :],
                                           ALU.is_gt, ALU.subtract).then_inc(drop_set[0], 1)
                    carry_wide(0, w, b, C)
                    carry_drop(0, w, b, C)
                    carry_own(0, w, b, C)
                    carry_scan(0, w, b, C)
                    carry_firsts(0, w, b, C)

            each_body(dve, lambda i: [layer0(i, s) for s in range(SLOTS)])
            layer0(BODIES, 0)

            def add_sums(q):
                for c in chunks_of(q):
                    dve.wait_ge(acc_t, c + 1)
                    for k in range(JC):
                        j = c * JC + k
                        last = v.scalar_tensor_tensor(xs3[:, j, :], acc_to(c)[:, k * C:(k + 1) * C], dinv[:, j:j + 1],
                                                      xs3[:, j, :], ALU.mult, ALU.add)
                    last.then_inc(x1_set, 1)

            def centre(q):
                at = slice(q * JP, (q + 1) * JP)
                dve.wait_ge(x1_set, (q + 1) * JP // JC)
                link(v.tensor_reduce(mean[:, at], xs3[:, at, :], AX.X, ALU.add))
                link(v.tensor_scalar(mean[:, at], mean[:, at], 1.0 / C, None, ALU.mult))
                v.tensor_tensor(hs3[:, at, :], xs3[:, at, :], mean[:, at].unsqueeze(2).to_broadcast([NP, JP, C]),
                                ALU.subtract).then_inc(cent1_set, 1)

            def variance(q):
                at = slice(q * JP, (q + 1) * JP)
                dve.wait_ge(sq1_set, q + 1)
                link(v.tensor_reduce(rstd[:, at], squares1[:, q % 2], AX.X, ALU.add))
                v.tensor_scalar(rstd[:, at], rstd[:, at], 1.0 / C, None, ALU.mult).then_inc(var_set, 1)

            def normed(q):
                at = slice(q * JP, (q + 1) * JP)
                dve.wait_ge(std_set, q + 2)
                link(v.reciprocal(rstd[:, at], rstd[:, at]))
                dve.wait_ge(cent1_set, q + 1)
                v.scalar_tensor_tensor(hs3[:, at, :], hs3[:, at, :], 0.0, rstd[:, at].unsqueeze(2).to_broadcast([NP, JP, C]),
                                       ALU.max, ALU.mult).then_inc(h_set, 1)

            def split_xr(c):
                b = c % 2
                xr_ps = ps_g[0:NP, b, :].rearrange("p (j k) -> p j k", j=JC)[:, :, C:2 * C]
                dve.wait_ge(parts_set, 3 * c + 2)
                v.tensor_tensor(xr_rest[:, b], xr_ps, xr_parts[:, b, :, 0, :], ALU.subtract).then_inc(rest_set, 1)
                dve.wait_ge(parts_set, 3 * c + 3)
                dve.wait_ge(rest_set, c + 1)
                v.tensor_tensor(xr_parts[:, b, :, 2, :], xr_rest[:, b], xr_parts[:, b, :, 1, :],
                                ALU.subtract).then_inc(xr_kept, 1)

            for q in range(PARTS + 2):
                if q < PARTS:
                    add_sums(q)
                    centre(q)
                if 1 <= q <= PARTS:
                    variance(q - 1)
                    normed(q - 1)
                for c in chunks_of(q - 2):
                    if c > 0:
                        split_xr(c - 1)
            split_xr(CHUNKS - 1)

            def one_hot_t(n, s, rnd):
                dve.wait_ge(edge_in[s], 48 * (rnd + 1))
                wait(dve, g_made, n - 1)
                v.tensor_scalar(oht[:, s % 2, :], locr[:, s, :], part_f[:, 0:1], None, ALU.is_equal).then_inc(oht_set, 1)

            v.memset(start[:, :, T:T + 1], 0.0).then_inc(consts_f, 1)
            dve.wait_ge(consts_f, 2)
            one_hot_t(0, 0, 0)

            def layer1(i, s):
                n, y, z, w, ahead = (behind(i, s, lag) for lag in (0, 1, 2, 3, -1))
                if y is not None:
                    y, ys, yr = y
                    dve.wait_ge(edge_in[ys], 48 * (yr + 1))
                    dve.wait_ge(lt_made, y + 1)
                    v.tensor_tensor_scan(fwd[:], start[0:GT * H, ys, 0:T], lt_ps, -BIG, ALU.add, ALU.max).then_inc(fwd_set, 1)
                if w is not None:
                    w, wb = w[0], w[1] % 2
                    carry_lasts(1, w, wb, CD)
                if z is not None:
                    z, zs, zr = z
                    zb = zs % 2
                    dve.wait_ge(exp_set, z + 1)
                    v.tensor_scalar(resc[:], by_tile[:], expt[:, T:T + 1], None, ALU.mult).then_inc(resc_set, 1)
                if y is not None:
                    dve.wait_ge(fwd_set, y + 1)
                    v.tensor_scalar(tails[:], by_tile[:], fwd[:, T - 1:T], None, ALU.mult).then_inc(tails_set, 1)
                if w is not None:
                    carry_wide(1, w, wb, CD)
                    carry_drop(1, w, wb, CD)
                if z is not None:
                    at = bass.ds(z * GT, GT)
                    dve.wait_ge(ext_made, 2 * z + 2)
                    wait(dve, summed[1], z - 1)
                    v.tensor_tensor(keep[:, zb, 0, :], resc_ps, single_prev[:, at], ALU.mult).then_inc(keep_set[1], 1)
                    w8 = ext_ps.rearrange("p (t h) -> p t h", t=GT)
                    v.tensor_copy(msg[:, zb, :, C:CD], w8)
                    dve.wait_ge(keep_set[1], z + 1)
                    v.tensor_tensor(keep[:, zb, 1, :], resc_ps, keep[:, zb, 0, :], ALU.subtract).then_inc(drop_set[1], 1)
                    v.tensor_tensor(msg[:, zb, :, 0:C].rearrange("p t (h c) -> p t h c", h=H),
                                    gbuf[:, zs].rearrange("p t (h c) -> p t h c", h=H),
                                    w8.unsqueeze(3).to_broadcast([T, GT, H, HC]), ALU.mult).then_inc(msg_set, 1)
                if w is not None:
                    carry_own(1, w, wb, CD)
                if y is not None:
                    wait(dve, before_set, y)
                    v.tensor_copy(runmax[:, 0:1], runmax[:, GT:GT + 1]).then_inc(carry_set, 1)
                if w is not None:
                    carry_scan(1, w, wb, CD)
                if y is not None:
                    dve.wait_ge(carry_set, y + 1)
                    dve.wait_ge(tails_made, y + 1)
                    v.tensor_tensor_scan(runmax[:, 1:GT + 1], chain[:, bass.ds(y * GT, GT)], tails_ps, runmax[:, 0:1],
                                         ALU.min, ALU.max).then_inc(runmax_set, 1)
                if w is not None:
                    carry_firsts(1, w, wb, CD)
                if y is not None:
                    dve.wait_ge(runmax_set, y + 1)
                    v.tensor_tensor(before[:], runmax[:, 0:GT], cont[0:H, bass.ds(y * GT, GT)], ALU.min).then_inc(before_set, 1)
                    dve.wait_ge(before_set, y + 1)
                    v.tensor_tensor(beforex[:].rearrange("k (t h) -> k t h", h=H), before[:].unsqueeze(2).to_broadcast([H, GT, H]),
                                    ident[0:H, 0:H].unsqueeze(1).to_broadcast([H, GT, H]), ALU.mult).then_inc(beforex_set, 1)
                    onehot(1, y, ys % 2)
                if n is not None:
                    n = n[0]
                    dve.wait_ge(gathered[1][s], 16 * GT * (i + 1))
                    dve.wait_ge(g_made, n + 1)
                    v.tensor_tensor(lr, rows_to, gbuf[:, s].rearrange("p t c -> p (t c)"), ALU.add).then_inc(row_set, 1)
                if y is not None:
                    dve.wait_ge(hist_made, y + 1)
                    v.tensor_copy(hist[:], hist_ps).then_inc(hist_set, 1)
                if n is not None:
                    dve.wait_ge(row_set, n + 1)
                    v.scalar_tensor_tensor(lr, lr, SLOPE, lr, ALU.mult, ALU.max).then_inc(leaky_set, 1)
                if y is not None:
                    dve.wait_ge(hist_set, y + 1)
                    v.tensor_tensor_scan(fwd[:], start[0:GT * H, ys, 0:T], lt_ps, hist[:, 0:1], ALU.add, ALU.max).then_inc(fwdh_set, 1)
                if n is not None:
                    dve.wait_ge(leaky_set, n + 1)
                    v.tensor_tensor(lr.rearrange("p (t c) -> p t c", t=GT), lr.rearrange("p (t c) -> p t c", t=GT),
                                    att_s[:].unsqueeze(1).to_broadcast([T, GT, C]), ALU.mult).then_inc(prod_set, 1)
                if y is not None:
                    dve.wait_ge(fwdh_set, y + 1)
                    v.tensor_tensor_scan(segmax[:, ::-1], start[0:GT * H, ys, 1:T + 1][:, ::-1], fwd[:, ::-1], -BIG,
                                         ALU.add, ALU.max).then_inc(segmax_set, 1)
                if ahead is not None:
                    one_hot_t(*ahead)
                if y is not None:
                    dve.wait_ge(segmax_set, y + 1)
                    v.tensor_tensor(diff[:, T:T + 1], hist[:], segmax[:, 0:1], ALU.subtract)
                    v.tensor_tensor(diff[:, 0:T], lt_ps, segmax[:], ALU.subtract).then_inc(diff_set, 1)
                if n is not None:
                    dve.wait_ge(prod_set, n + 1)
                    v.tensor_reduce(lg[:], lr.rearrange("p (k c) -> p k c", c=HC), AX.X, ALU.add).then_inc(logits_set, 1)

            each_body(dve, lambda i: [layer1(i, s) for s in range(SLOTS)])
            for s in range(3):
                layer1(BODIES, s)

            def num(c):
                return ps_s[0:NP, c % 2, :].rearrange("p (k e) -> p k e", k=2)[:, :, 0:JE // 2 * CD].rearrange(
                    "p k (j d) -> p k j d", d=CD)

            def rden_of(c):
                return rden[:, c % 2].rearrange("p (k j) h -> p k j h", k=2)

            for c in range(ENDS):
                at = slice(c * JE, (c + 1) * JE)
                dve.wait_ge(num_t, c + 1)
                for k in range(2):
                    last = v.tensor_scalar(rden_of(c)[:, k], num(c)[:, k, :, C:CD], DEN_EPS, None, ALU.add)
                link(last)
                link(v.reciprocal(rden[:, c % 2], rden[:, c % 2]))
                for k in range(2):
                    part = slice(c * JE + k * JE // 2, c * JE + (k + 1) * JE // 2)
                    last = v.tensor_tensor(y3[:, part, :].rearrange("p j (h c) -> p j h c", h=H),
                                           num(c)[:, k, :, 0:C].rearrange("p j (h c) -> p j h c", h=H),
                                           rden_of(c)[:, k].unsqueeze(3).to_broadcast([NP, JE // 2, H, HC]), ALU.mult)
                link(last)
                v.tensor_tensor(y3[:, at, :], y3[:, at, :], bias_s[:].unsqueeze(1).to_broadcast([NP, JE, C]),
                                ALU.add).then_inc(y_set, 1)
            v.tensor_tensor(hs3, hs3, bet_s[:].unsqueeze(1).to_broadcast([NP, NJ, C]), ALU.add)
            dve.wait_ge(sum_ps, 2 * ENDS)
            link(v.tensor_reduce(stat[:, 0, :], ps_g[0:NP, 0, 0:JE // 2 * C].rearrange("p (j c) -> p c j", c=C), AX.X, ALU.add))
            link(v.tensor_scalar(stat[:, 0, :], stat[:, 0, :], 1.0 / N, None, ALU.mult))

            def sum_squares(q):
                dve.wait_ge(sq_set, q + 1)
                v.tensor_reduce(sq_sum[:, q, :], sq[:, q % 2, :].rearrange("p (j c) -> p c j", c=C), AX.X,
                                ALU.add).then_inc(sqsum_set, 1)

            for q in range(PARTS):
                at = slice(q * JP, (q + 1) * JP)
                v.tensor_tensor(y3[:, at, :], y3[:, at, :], stat[:, 0, :].unsqueeze(1).to_broadcast([NP, JP, C]),
                                ALU.subtract).then_inc(cent_set, 1)
                if q > 0:
                    sum_squares(q - 1)
            sum_squares(PARTS - 1)
            dve.wait_ge(sqsum_ps, 1)
            v.tensor_scalar(stat[:, 2, :], ps_g[0:NP, 1, 0:C], 1.0 / N, None, ALU.mult).then_inc(var_set, 1)
            dve.wait_ge(std_set, PARTS + 2)
            link(v.reciprocal(stat[:, 2, :], stat[:, 2, :]))
            link(v.tensor_tensor(stat[:, 2, :], stat[:, 2, :], gam_s[:], ALU.mult))

            def finish(q):
                at = slice(q * JP, (q + 1) * JP)
                dve.wait_ge(gelu_set, q + 1)
                v.tensor_tensor(hs3[:, at, :], y3[:, at, :], xs3[:, at, :], ALU.add).then_inc(y_done, 1)

            for q in range(PARTS):
                at = slice(q * JP, (q + 1) * JP)
                link(v.tensor_tensor(y3[:, at, :], y3[:, at, :], stat[:, 2, :].unsqueeze(1).to_broadcast([NP, JP, C]), ALU.mult))
                v.tensor_tensor(y3[:, at, :], y3[:, at, :], hs3[:, at, :], ALU.add).then_inc(gelu_in, 1)
                if q > 0:
                    finish(q - 1)
            finish(PARTS - 1)

        @block.scalar
        def _(act):
            a = nc.scalar
            act.dma_start(w0_s[:], w0).then_inc(w_in, 16)
            act.dma_start(wlr[:, 0:C], w_l).then_inc(w_in, 16)
            act.dma_start(wlr[:, C:2 * C], w_r).then_inc(w_in, 16)
            act.dma_start(blr[:, 0:C], b_l.unsqueeze(0)).then_inc(w_in, 16)
            act.dma_start(blr[:, C:2 * C], b_r.unsqueeze(0)).then_inc(w_in, 16)
            for to, vec in ((b0_s, b0), (bias_s, bias), (gam_s, gamma), (bet_s, beta)):
                act.dma_start(to[:], vec.partition_broadcast(NP)).then_inc(w_in, 16)
            act.dma_start(att_s[:], att.rearrange("h c -> (h c)").partition_broadcast(T)).then_inc(w_in, 16)
            act.wait_ge(consts_set, N_CONST)
            for t in range(GT):
                act.dma_start(web[t * ED:(t + 1) * ED, t * C:(t + 1) * C], w_e).then_inc(w_in, 16)
            act.dma_start(xr_table[N:NW], zeros).then_inc(pad_out, 16)

            act.wait_ge(var_set, 1)
            a.activation(rstd[:], rstd[:], ACT.Sqrt, bias=eps_ln[:, 0:1]).then_inc(std_set, 1)
            for c in range(CHUNKS):
                act.wait_ge(h_t, c + 1)
                wait(act, lin_ps, c - 1)
                a.activation(h_turn[:, c % 2].rearrange("p k q -> p (k q)"), ps_s[0:C, c % 2, 0:JC * NP],
                             ACT.Copy).then_inc(ht_set, 1)
                if c > 0:
                    act.wait_ge(lin_ps, c)
                    a.activation(hs[:, (c - 1) * JC * C:c * JC * C], ps_g[0:NP, (c - 1) % 2, 0:JC * C], ACT.Copy).then_inc(lin_kept, 1)
            act.wait_ge(lin_ps, CHUNKS)
            a.activation(hs[:, (CHUNKS - 1) * JC * C:], ps_g[0:NP, (CHUNKS - 1) % 2, 0:JC * C], ACT.Copy).then_inc(lin_kept, 1)
            act.wait_ge(deg_set, 1)
            a.activation(dinv[:], dinv[:], ACT.Sqrt, bias=ones[0:NP, 0:1]).then_inc(root_set, 1)

            def keep_sums(layer, w, b, rows, acc):
                bases = tile_bases(ENG.Activation, w)
                act.wait_ge(firsts_set[layer], 2 * w + 2)
                for t in range(GT):
                    wait(act, acc_set[layer], w * GT + t)
                    act.wait_ge(flags_set, 1)
                    a.activation(acc[:, bass.ds(bases[t], T)], ps_s[0:rows, b, t * T:(t + 1) * T],
                                 ACT.Copy).then_inc(acc_set[layer], 1)

            act.wait_ge(flags_set, 1)

            def layer0(i, s):
                w = behind(i, s, 1)
                if w is not None:
                    keep_sums(0, w[0], w[1] % 2, C, acc0)

            each_body(act, lambda i: [layer0(i, s) for s in range(SLOTS)])
            layer0(BODIES, 0)

            def square(q):
                act.wait_ge(cent1_set, q + 1)
                wait(act, var_set, q)
                a.activation(squares1[:, q % 2].rearrange("p j c -> p (j c)"), hs[:, q * JP * C:(q + 1) * JP * C],
                             ACT.Square).then_inc(sq1_set, 1)

            def root(q):
                at = slice(q * JP, (q + 1) * JP)
                act.wait_ge(var_set, q + 2)
                a.activation(rstd[:, at], rstd[:, at], ACT.Sqrt, bias=eps_ln[:, 0:1]).then_inc(std_set, 1)

            def turned(c):
                act.wait_ge(h1_t, c + 1)
                wait(act, lr_ps, c - 1)
                a.activation(h_turn[:, c % 2].rearrange("p k q -> p (k q)"), ps_s[0:C, c % 2, 0:JC * NP],
                             ACT.Copy).then_inc(h1t_set, 1)

            def split(c):
                b = c % 2
                rows = ps_g[0:NP, b, :].rearrange("p (j k) -> p j k", j=JC)
                act.wait_ge(lr_ps, c + 1)
                wait(act, lr_out[b], 32 * (c // 2))
                a.activation(lr_keep[:, b], rows[:, :, 0:C], ACT.Copy).then_inc(xl_kept, 1)
                a.activation(xr_parts[:, b, :, 0, :], rows[:, :, C:2 * C], ACT.Copy).then_inc(parts_set, 2)
                act.wait_ge(rest_set, c + 1)
                a.activation(xr_parts[:, b, :, 1, :], xr_rest[:, b], ACT.Copy).then_inc(parts_set, 1)

            for q in range(PARTS + 2):
                if q < PARTS:
                    square(q)
                if 1 <= q <= PARTS:
                    root(q - 1)
                for c in chunks_of(q - 2):
                    turned(c)
                    if c > 0:
                        split(c - 1)
            split(CHUNKS - 1)

            def layer1(i, s):
                y, w = behind(i, s, 1), behind(i, s, 3)
                if w is not None:
                    keep_sums(1, w[0], w[1] % 2, CD, acc1)
                if y is not None:
                    y = y[0]
                    act.wait_ge(diff_set, y + 1)
                    wait(act, ext_made, 2 * y)
                    a.activation(expt[:], diff[:], ACT.Exp).then_inc(exp_set, 1)

            each_body(act, lambda i: [layer1(i, s) for s in range(SLOTS)])
            for s in range(3):
                layer1(BODIES, s)

            for q in range(PARTS):
                act.wait_ge(cent_set, q + 1)
                wait(act, sqsum_set, q - 1)
                a.activation(sq[:, q % 2, :], y[:, q * JP * C:(q + 1) * JP * C], ACT.Square).then_inc(sq_set, 1)
            act.wait_ge(var_set, PARTS + 2)
            a.activation(stat[:, 2, :], stat[:, 2, :], ACT.Sqrt, bias=eps_bn[:, 0:1]).then_inc(std_set, 1)
            for q in range(PARTS):
                at = slice(q * JP * C, (q + 1) * JP * C)
                act.wait_ge(gelu_in, q + 1)
                a.activation(y[:, at], y[:, at], ACT.Gelu).then_inc(gelu_set, 1)

        @block.tensor
        def _(pe):
            m = nc.tensor
            pe.wait_ge(consts_f, 1)
            pe.wait_ge(onehots_set, 1)
            for k in range(BLK):
                m.matmul(ps_g[0:NP, 0, 0:NJ + 1], in_b[:, k, :], jlt[:, k, :], start=(k == 0), stop=False)
                last = m.matmul(ps_g[0:NP, 0, 0:NJ + 1], ge_b[:, k, 0:NP], ones_b[:, 0:NJ + 1], start=False, stop=(k == BLK - 1))
            last.then_inc(rows_ps, 1)

            def turn_rows(c, to):
                for k in range(JC):
                    last = m.transpose(ps_s[0:C, c % 2, k * NP:(k + 1) * NP], hs3[:, c * JC + k, :], ident[0:NP, 0:NP])
                last.then_inc(to, 1)

            pe.wait_ge(rows_set, 1)
            pe.wait_ge(h_set, 1)
            for c in range(CHUNKS + 1):
                if c < CHUNKS:
                    wait(pe, ht_set, c - 1)
                    turn_rows(c, h_t)
                if c > 0:
                    d = c - 1
                    pe.wait_ge(ht_set, d + 1)
                    wait(pe, lin_kept, d - 1)
                    for k in range(JC):
                        last = m.matmul(ps_g[0:NP, d % 2, k * C:(k + 1) * C], h_turn[:, d % 2, k, :], w0_s[:], start=True, stop=True)
                    last.then_inc(lin_ps, 1)

            def sums(layer, g, b, rows, rows_of):
                pe.wait_ge(oh_set[layer], g + 1)
                wait(pe, acc_set[layer], (g - 1) * GT)
                for t in range(GT):
                    last = m.matmul(ps_s[0:rows, b, t * T:(t + 1) * T], rows_of(t), oh[:, b, t, :], start=True, stop=True)
                last.then_inc(summed[layer], 1)

            def layer0(i, s):
                pe.wait_ge(gathered[0][s], 16 * GT * (i + 1))
                sums(0, i * SLOTS + s, s % 2, C, lambda t: gbuf[:, s, t, :])

            each_body(pe, lambda i: [layer0(i, s) for s in range(SLOTS)])

            pe.wait_ge(acc_set[0], GROUPS * GT)
            def product(d):
                pe.wait_ge(h1t_set, d + 1)
                wait(pe, xl_kept, d - 1)
                wait(pe, xr_kept, d - 1)
                for k in range(JC):
                    to = ps_g[0:NP, d % 2, k * 2 * C:(k + 1) * 2 * C]
                    m.matmul(to, h_turn[:, d % 2, k, :], wlr[:], start=True, stop=False)
                    last = m.matmul(to, ones[0:1, 0:NP], blr[:], start=False, stop=True)
                last.then_inc(lr_ps, 1)

            for q in range(PARTS + 2):
                for c in chunks_of(q):
                    wait(pe, x1_set, c - 1)
                    for k in range(JC):
                        last = m.transpose(acc_to(c)[:, k * C:(k + 1) * C], acc0_n[:, c * JC + k, :], ident[0:C, 0:C])
                    last.then_inc(acc_t, 1)
                for c in chunks_of(q - 2):
                    pe.wait_ge(h_set, q)
                    wait(pe, h1t_set, c - 1)
                    turn_rows(c, h1_t)
                    if c > 0:
                        product(c - 1)
            product(CHUNKS - 1)
            pe.wait_ge(xl_kept, CHUNKS)
            pe.wait_ge(xr_kept, CHUNKS)

            def layer1(i, s):
                n, y, z = (behind(i, s, lag) for lag in (0, 1, 2))
                if y is not None:
                    y, ys, yr = y
                    pe.wait_ge(consts_f, 1)
                    pe.wait_ge(logits_set, y + 1)
                    wait(pe, diff_set, y)
                    m.transpose(lt_ps, lg[:], ident[:]).then_inc(lt_made, 1)
                if z is not None:
                    z, zs, zr = z
                    zb = zs % 2
                    pe.wait_ge(consts_f, 1)
                    pe.wait_ge(exp_set, z + 1)
                    m.transpose(ext_ps, expt[:, 0:T], ident[0:GT * H, 0:GT * H]).then_inc(ext_made, 1)
                    pe.wait_ge(consts_f, 1)
                    pe.wait_ge(resc_set, z + 1)
                    m.matmul(resc_ps, by_chan[:], resc[:], start=True, stop=True).then_inc(ext_made, 1)
                if n is not None:
                    n = n[0]
                    pe.wait_ge(consts_f, 1)
                    pe.wait_ge(edge_in[s], 48 * (i + 1))
                    wait(pe, row_set, n)
                    m.matmul(rows_to, eat[:, s, :], web[:], start=True, stop=False)
                if y is not None:
                    pe.wait_ge(consts_f, 1)
                    pe.wait_ge(tails_set, y + 1)
                    m.matmul(tails_ps, by_head[:], tails[:], start=True, stop=True).then_inc(tails_made, 1)
                if n is not None:
                    pe.wait_ge(consts_f, 1)
                    pe.wait_ge(oht_set, n + 1)
                    pe.wait_ge(xrw_in[s], 16 * GT * (i + 1))
                    for t in range(GT):
                        for k in range(3):
                            last = m.matmul(rows_to[:, t * C:(t + 1) * C], oht[:, s % 2, t * T:(t + 1) * T], xrw[:, s, t, k, :],
                                            start=False, stop=(t == GT - 1 and k == 2))
                    last.then_inc(g_made, 1)
                if y is not None:
                    pe.wait_ge(consts_f, 1)
                    pe.wait_ge(beforex_set, y + 1)
                    m.matmul(hist_ps, beforex[:], ones[0:H, 0:1], start=True, stop=True).then_inc(hist_made, 1)
                if z is not None:
                    pe.wait_ge(msg_set, z + 1)
                    sums(1, z, zb, CD, lambda t: msg[:, zb, t, :])

            each_body(pe, lambda i: [layer1(i, s) for s in range(SLOTS)])
            for s in range(2):
                layer1(BODIES, s)

            pe.wait_ge(acc_set[1], GROUPS * GT)
            for c in range(ENDS + 1):
                if c < ENDS:
                    wait(pe, y_set, c - 1)
                    for k in range(JE):
                        at = k // (JE // 2) * (GE // 2) + k % (JE // 2) * CD
                        last = m.transpose(ps_s[0:NP, c % 2, at:at + CD], acc1_n[:, c * JE + k, :], ident[0:CD, 0:CD])
                    last.then_inc(num_t, 1)
                if c > 0:
                    pe.wait_ge(y_set, c)
                    for k in range(2 * c - 2, 2 * c):
                        m.matmul(ps_g[0:NP, 0, 0:JE // 2 * C], ones[0:NP, 0:NP], y[:, k * JE // 2 * C:(k + 1) * JE // 2 * C],
                                 start=(k == 0), stop=(k == 2 * ENDS - 1)).then_inc(sum_ps, 1)
            pe.wait_ge(sqsum_set, PARTS)
            for q in range(PARTS):
                last = m.matmul(ps_g[0:NP, 1, 0:C], ones[0:NP, 0:NP], sq_sum[:, q, :], start=(q == 0), stop=(q == PARTS - 1))
            last.then_inc(sqsum_ps, 1)


_INS = ["x", "src_cols", "dst_rows", "dst_cols", "first_dst", "last_dst", "edge_rows", "L0_gnn_W", "L0_gnn_b", "L1_gnn_W_l",
        "L1_gnn_b_l", "L1_gnn_W_r", "L1_gnn_b_r", "L1_gnn_W_e", "L1_gnn_att", "L1_gnn_bias", "L1_gnn_gamma", "L1_gnn_beta"]


def lay_out(inputs):
    import numpy as _np

    def tiles(a, pad):
        padded = _np.full((TILES * T,) + a.shape[1:], pad, a.dtype)
        padded[:E] = a
        return padded.reshape((TILES, T) + a.shape[1:])

    arrays = {name: _np.ascontiguousarray(a) for name, a in inputs.items()}
    src, dst = tiles(arrays.pop("src"), 0), tiles(arrays.pop("dst"), N)
    edges = tiles(arrays.pop("edge_attr_16"), 0)
    arrays["src_cols"] = _np.ascontiguousarray(src.T)
    arrays["dst_rows"], arrays["dst_cols"] = dst, _np.ascontiguousarray(dst.T)
    arrays["first_dst"], arrays["last_dst"] = _np.ascontiguousarray(dst[:, 0]), _np.ascontiguousarray(dst[:, T - 1])
    arrays["edge_rows"] = _np.ascontiguousarray(edges.transpose(0, 2, 1)).reshape(TILES * ED, T)
    return arrays


def kernel(**inputs):
    import concourse.bacc as _bacc
    from concourse import mybir as _mybir
    from concourse.bass_utils import run_bass_kernel_spmd as _run

    laid = lay_out(inputs)
    nc = _bacc.Bacc("TRN2", target_bir_lowering=False, num_devices=1)
    arrays, args = {}, []
    for name in _INS:
        a = laid[name]
        arrays[f"in_{name}_dram"] = a
        args.append(nc.dram_tensor(f"in_{name}_dram", a.shape, _mybir.dt.from_np(a.dtype), kind="ExternalInput").ap())
    args.append(nc.dram_tensor("out_dram", (N, C), F32, kind="ExternalOutput").ap())
    gnn_kernel(nc, *args)
    r = _run(nc, [arrays], core_ids=[0])
    return r.results[0]["out_dram"]
```

```python
import concourse.bass as bass
from concourse import mybir
from contextlib import ExitStack

F32 = mybir.dt.float32
BF16 = mybir.dt.bfloat16
I32 = mybir.dt.int32
I16 = mybir.dt.int16
ALU = mybir.AluOpType
ACT = mybir.ActivationFunctionType
AX = mybir.AxisListType
ENG = mybir.EngineType

N = 12500
E = 412500
C = 64
H = 4
HC = C // H
ED = 16
T = 128
GT = 8
SLOTS = 4
GE = GT * T
BODIES = -(-E // (SLOTS * GE))
GROUPS = BODIES * SLOTS
BLK = -(-(GROUPS * GT) // T)
TILES = BLK * T
NP, NJ = 125, 100
JC = 4
CHUNKS = NJ // JC
NW = N + T
CD = C + H
BIG = 1.0e38
SLOPE = 0.2
LN_EPS = 1e-5
BN_EPS = 1e-5
DEN_EPS = 1e-16
PARTS = 5
JP = NJ // PARTS
JE = 10
ENDS = NJ // JE
REAL = -(-E // T)
FG = 2 * SLOTS
K = 29
DW = 6
PIECES = [range(k, min(k + 5, K)) for k in range(0, K, 5)]
HI = -(-N // T)
FAST = -(-REAL // (FG * GT + K))
DENSE0 = FAST * FG * GT
DENSE = FAST * K
assert DENSE0 + DENSE <= TILES


def gnn_kernel(nc, x, src_cols, dst_rows, dst_cols, first_dst, last_dst, edge_rows, w0, b0, w_l, b_l, w_r, b_r, w_e,
               att, bias, gamma, beta, out):
    ctx = ExitStack()
    with ctx:
        def sb(name, shape, dt=F32):
            return ctx.enter_context(nc.sbuf_tensor(name, shape, dt))

        def pb(name, shape, dt=F32):
            return ctx.enter_context(nc.psum_tensor(name, shape, dt))

        def sem(name):
            return ctx.enter_context(nc.semaphore(name))

        def dram(name, shape, dt=F32):
            return nc.dram_tensor(name, shape, dt, kind="Internal").ap()

        loc_rows = dram("loc_rows", [TILES, T], BF16)
        start_rows = dram("start_rows", [TILES, H, T], BF16)
        agg_table = dram("agg_table", [N, C])
        xl_table = dram("xl_table", [N, C])
        xr_table = dram("xr_table", [NW, 3, C], BF16)

        xs = sb("xs", [NP, NJ * C])
        hs_all = sb("hs", [T, NJ * C])
        hs = hs_all[0:NP, :]
        arena = sb("arena", [T, NW])
        acc0 = arena[0:C, :]
        acc1 = arena[0:CD, :]
        loc = sb("loc", [T, TILES], BF16)
        lastm = sb("lastm", [T, TILES], BF16)
        cont = sb("cont", [CD, TILES], BF16)
        single_prev = sb("single_prev", [CD, TILES], BF16)
        wide = sb("wide", [CD, TILES], BF16)
        by_tiles = sb("by_tiles", [C + 1, TILES], BF16)
        place_row = by_tiles[GT * H:GT * H + 1, :].bitcast(I16)
        chain = by_tiles[0:H, :]
        base_row = by_tiles[C:C + 1, :].bitcast(I16)

        sizes = dict(g=SLOTS * GT * C, oh=2 * GE, xrw=SLOTS * GT * 3 * C // 2, oht=GE, msg=2 * GT * CD,
                     lr=GT * C, locr=SLOTS * GE // 2, ea=SLOTS * T, start=SLOTS * (T + 2) // 2)
        RING = SLOTS * GT * C + 2 * GE + HI * 3 * C // 2
        assert RING >= sum(sizes.values())
        ring = sb("ring", [T, RING])
        offs, at = {}, 0
        for key, size in sizes.items():
            offs[key] = at
            at += size

        def piece(key):
            return ring[:, offs[key]:offs[key] + sizes[key]]

        gbuf = piece("g").rearrange("p (s t c) -> p s t c", s=SLOTS, t=GT)
        xrw = piece("xrw").bitcast(BF16).rearrange("p (s t k c) -> p s t k c", s=SLOTS, t=GT, k=3)
        oht = piece("oht").bitcast(BF16).rearrange("p (b e) -> p b e", b=2)
        oh = piece("oh").rearrange("p (b t n) -> p b t n", b=2, t=GT)
        msg = piece("msg").rearrange("p (b t c) -> p b t c", b=2, t=GT)
        lr = piece("lr")
        locr = piece("locr").bitcast(BF16).rearrange("p (s e) -> p s e", s=SLOTS)
        eat = piece("ea").rearrange("p (s e) -> p s e", s=SLOTS)
        start = piece("start").bitcast(BF16).rearrange("p (s e) -> p s e", s=SLOTS)

        idx = sb("idx", [T, SLOTS, GT], I32)
        lg = sb("lg", [T, GT * H])
        small = sb("small", [T, DW * HI])
        fwd = small[0:GT * H, 0:T]
        segmax = small[0:GT * H, T:2 * T]
        diff = small[0:GT * H, 2 * T:3 * T + 1]
        expt = small[0:GT * H, 3 * T + 1:4 * T + 2]
        tails = sb("tails", [GT * H, GT])
        resc = sb("resc", [GT * H, GT])
        hist = sb("hist", [GT * H, 1])
        runmax = sb("runmax", [H, GT + 1])
        before = sb("before", [H, GT])
        beforex = sb("beforex", [H, GT * H])
        keep = sb("keep", [CD, 2, 2, GT])
        lastsum = sb("lastsum", [CD, 2, GT + 1])
        joined = sb("joined", [CD, GT])
        firsts = sb("firsts", [CD, 2, GT])

        table3 = ring[:, RING - HI * 3 * C // 2:].bitcast(BF16).rearrange("p (h k c) -> p h k c", h=HI, k=3)
        stage = hs_all[:, 0:HI * C].rearrange("p (h c) -> p h c", h=HI)
        counts = hs_all[:, 0:T * HI // 2].bitcast(BF16)
        counts_w = hs_all[:, 0:T * HI // 2]
        lo_hot = hs_all[:, T * HI // 2:T * HI // 2 + T].bitcast(BF16).rearrange("p (b l) -> p b l", b=2)
        key_hot = small[:, :].bitcast(BF16).rearrange("p (b k) -> p b k", b=2)
        iota_k = sb("iota_k", [T, DW * HI], I16)
        src_d = sb("src_d", [T, K], I32)
        hi_i = sb("hi_i", [T, K], I32)
        lo_i = sb("lo_i", [T, K], I32)
        lo_f = sb("lo_f", [T, K])
        key_f = sb("key_f", [T, K])
        dsum = sb("dsum", [T, T])
        part3 = dsum[:, 0:C]
        flag = sb("flag", [1, 4])
        flag_i = sb("flag_i", [1, 1], I32)
        zero1 = sb("zero1", [T, 1])
        ident2 = sb("ident2", [T, C])
        acc0b = arena[C:2 * C, :]

        iota_f = sb("iota_f", [T, T])
        iota_b = sb("iota_b", [T, T], BF16)
        part_i = sb("part_i", [T, 1], I32)
        part_f = sb("part_f", [T, 1])
        ident = sb("ident", [T, T])
        ones = sb("ones", [T, T])
        ones_b = sb("ones_b", [T, T], BF16)
        node_f = sb("node_f", [NP, NJ + 1])
        head_i = sb("head_i", [GT * H, 1], I32)
        head_f = sb("head_f", [GT * H, 1])
        tile_i = sb("tile_i", [GT * H, 1], I32)
        tile_f = sb("tile_f", [GT * H, 1])
        chan_f = sb("chan_f", [GT * H, CD])
        by_tile = sb("by_tile", [GT * H, GT])
        by_head = sb("by_head", [GT * H, H])
        by_chan = sb("by_chan", [GT * H, CD])
        w0_s = sb("w0_s", [C, C])
        wlr = sb("wlr", [C + 1, 2 * C])
        web = sb("web", [T, GT * C])
        att_s = sb("att_s", [T, C])
        b0_s = sb("b0_s", [NP, C])
        bias_s = sb("bias_s", [NP, C])
        gam_s = sb("gam_s", [NP, C])
        bet_s = sb("bet_s", [NP, C])
        eps_ln = sb("eps_ln", [NP, 1])
        eps_bn = sb("eps_bn", [NP, 1])
        rowblk = sb("rowblk", [NP, NJ + 1])
        rowidx = sb("rowidx", [NP, NJ + 1], I32)
        below = sb("below", [NP, NJ + 1])
        dinv = sb("dinv", [NP, NJ])
        mean = sb("mean", [NP, NJ])
        rstd = sb("rstd", [NP, NJ])
        stat = sb("stat", [NP, 3, C])
        pa = sb("pa", [T, BLK])
        jb = sb("jb", [T, BLK])

        ps_g = pb("ps_g", [T, 2, GT * C])
        ps_s = pb("ps_s", [T, 2, GE])
        ps_x = pb("ps_x", [T, 2, 512])
        ps_e = ps_x[:, 0, :]
        built_to = [ps_x[:, :, 0:DW * HI // 2], ps_g[:, :, 0:DW * HI // 2]]
        dense_ps = ps_g[:, 0, 0:3 * C].rearrange("p (k c) -> p k c", k=3)
        dense_t = ps_g[:, 1, 0:T]
        rows_to = ps_g[:, 0, :]
        ext_ps = ps_g[:, 1, 0:GT * H]
        resc_ps = ps_g[0:CD, 1, T:T + GT]
        lt_ps = ps_e[0:GT * H, 0:T]
        tails_ps = ps_e[0:H, 2 * T:2 * T + GT]
        hist_ps = ps_e[0:GT * H, 3 * T:3 * T + 1]

        def blocks(ap):
            return ap.rearrange("p (b e) -> p b e", e=T)

        dst_i = arena[:, 0:TILES].bitcast(I32)
        dst_f = arena[:, 0:TILES]
        first_all = arena[:, TILES:2 * TILES].bitcast(I32)
        last_all = arena[:, 2 * TILES:3 * TILES].bitcast(I32)
        squares = arena[0:NP, 3 * TILES:3 * TILES + NJ * C // 4].rearrange("p (j c) -> p j c", c=C)
        found = ring[0:NP, 0:2 * GE].bitcast(I32).rearrange("p (b t e) -> p b t e", b=2, t=GT)
        less = ring[0:NP, 2 * GE:3 * GE].rearrange("p (t e) -> p t e", t=GT)
        h_turn = ring[0:C + 1, 3 * GE:3 * GE + 2 * JC * NP].rearrange("p (b k q) -> p b k q", b=2, k=JC)
        dst_t = ring[:, offs["xrw"]:offs["xrw"] + TILES].bitcast(I32)
        stages = RING - TILES
        loc_b = ring[:, stages:stages + TILES // 2].bitcast(BF16)
        start_b = ring[:, stages + TILES // 2:stages + TILES].bitcast(BF16)
        equal_all = ring[0:CD, offs["xrw"]:offs["xrw"] + TILES]
        ge_b = hs_all[:, 0:BLK * (NP + 1) // 2].bitcast(BF16).rearrange("p (b q) -> p b q", b=BLK)
        in_b = hs_all[:, 1700:1700 + BLK * NP // 2].bitcast(BF16).rearrange("p (b q) -> p b q", b=BLK)
        jlt = hs_all[:, 3400:3400 + BLK * (NJ + 1) // 2].bitcast(BF16).rearrange("p (b j) -> p b j", b=BLK)
        iota_i = hs_all[:, 4800:4800 + T].bitcast(I32)
        node_i = hs_all[0:NP, 4960:4960 + NJ + 1].bitcast(I32)
        hund_i = hs_all[:, 5100:5100 + NP + 1].bitcast(I32)
        chan_i = hs_all[0:GT * H, 5260:5260 + CD].bitcast(I32)
        hund_f = hs_all[:, 5360:5360 + NP + 1]
        zeros = hs_all[:, 5600:5600 + 3 * C // 2].bitcast(BF16)
        key_i = hs_all[:, 5700:5700 + DW * HI].bitcast(I32)

        def acc_to(c):
            return ps_s[0:NP, c % 2, GE // 2:GE // 2 + JC * C]

        lr_keep = ring[0:NP, offs["oht"]:offs["oht"] + 2 * JC * C].rearrange("p (b j c) -> p b j c", b=2, j=JC)
        xr_rest = ring[0:NP, offs["oht"] + 2 * JC * C:offs["oht"] + 4 * JC * C].rearrange("p (b j c) -> p b j c", b=2, j=JC)
        xr_parts = ring[0:NP, offs["oh"]:offs["oh"] + 3 * JC * C].bitcast(BF16).rearrange(
            "p (b j k c) -> p b j k c", b=2, j=JC, k=3)
        squares1 = ring[0:NP, offs["msg"]:offs["msg"] + 2 * JP * C].rearrange("p (b j c) -> p b j c", b=2, c=C)
        y = ring[0:NP, 0:NJ * C]
        y3 = y.rearrange("p (j c) -> p j c", c=C)
        rden = ring[0:NP, 6400:6400 + 2 * JE * H].rearrange("p (b j h) -> p b j h", b=2, j=JE)
        sq = ring[0:NP, 6656:6656 + 2 * JP * C].rearrange("p (b k) -> p b k", b=2)
        sq_sum = ring[0:NP, 9600:9600 + PARTS * C].rearrange("p (q c) -> p q c", c=C)

        xs3 = xs[:, :].rearrange("p (j c) -> p j c", c=C)
        hs3 = hs[:, :].rearrange("p (j c) -> p j c", c=C)
        acc0_n = arena[:, 0:N].rearrange("c (p j) -> c j p", j=NJ)
        acc1_n = acc1[:, 0:N].rearrange("c (p j) -> c j p", j=NJ)
        agg_n, xl_n, out_n = (t.rearrange("(p j) c -> p j c", j=NJ) for t in (agg_table, xl_table, out))
        xr_n = xr_table[0:N].rearrange("(p j) k c -> p j k c", j=NJ)

        dst_in, ends_in, dstt_in, x_in, w_in = sem("dst_in"), sem("ends_in"), sem("dstt_in"), sem("x_in"), sem("w_in")
        consts_set, consts_f = sem("consts_set"), sem("consts_f")
        v_step = sem("v_step")
        dstf_set, loc_set, start_set, flags_set = sem("dstf_set"), sem("loc_set"), sem("start_set"), sem("flags_set")
        loc_out, start_out, pad_out = sem("loc_out"), sem("start_out"), sem("pad_out")
        onehots_set, rows_ps, rows_set = sem("onehots_set"), sem("rows_ps"), sem("rows_set")
        found_in = [sem("found_in0"), sem("found_in1")]
        counted, deg_set, root_set, table_set, table_out = (
            sem("counted"), sem("deg_set"), sem("root_set"), sem("table_set"), sem("table_out"))
        var_set, std_set, h_set = sem("var_set"), sem("std_set"), sem("h_set")
        h_t, ht_set, lin_ps, lin_kept = sem("h_t"), sem("ht_set"), sem("lin_ps"), sem("lin_kept")
        idx_in = [[sem(f"idx{k}_in{s}") for s in range(SLOTS)] for k in range(2)]
        gathered = [[sem(f"gathered{k}_{s}") for s in range(SLOTS)] for k in range(2)]
        slot_free = sem("slot_free")
        oh_set = [sem("oh_set0"), sem("oh_set1")]
        summed = [sem("summed0"), sem("summed1")]
        lastsum_set, prior_set, joined_set, firsts_sb, firsts_set, acc_set = (
            [sem(f"{n}{k}") for k in range(2)] for n in
            ("lastsum_set", "prior_set", "joined_set", "firsts_sb", "firsts_set", "acc_set"))
        keep_set, drop_set = [sem("keep_set0"), sem("keep_set1")], [sem("drop_set0"), sem("drop_set1")]
        xsum_set, stage_in, split_a, split_v, acc_zero = (
            sem("xsum_set"), sem("stage_in"), sem("split_a"), sem("split_v"), sem("acc_zero"))
        src_in, low_set, keys_set, hot_set, built, zeroed, added = (
            sem("src_in"), sem("low_set"), sem("keys_set"), sem("hot_set"), sem("built"), sem("zeroed"), sem("added"))
        dense_made, part_set, half_set, dsum_set, dsum_t, dense_set = (
            sem("dense_made"), sem("part_set"), sem("half_set"), sem("dsum_set"), sem("dsum_t"), sem("dense_set"))
        gather_done, dense_done, ones_row = sem("gather_done"), sem("dense_done"), sem("ones_row")
        acc_t, x1_set, cent1_set, sq1_set = sem("acc_t"), sem("x1_set"), sem("cent1_set"), sem("sq1_set")
        h1_t, h1t_set, lr_ps, parts_set, rest_set, xl_kept, xr_kept = (
            sem("h1_t"), sem("h1t_set"), sem("lr_ps"), sem("parts_set"), sem("rest_set"), sem("xl_kept"), sem("xr_kept"))
        lr_out = [sem("lr_out0"), sem("lr_out1")]
        xrw_in = [sem(f"xrw_in{s}") for s in range(SLOTS)]
        edge_in = [sem(f"edge_in{s}") for s in range(SLOTS)]
        oht_set, g_made, row_set, leaky_set, prod_set, logits_set = (
            sem("oht_set"), sem("g_made"), sem("row_set"), sem("leaky_set"), sem("prod_set"), sem("logits_set"))
        lt_made, fwd_set, tails_set, tails_made, carry_set, runmax_set, before_set, beforex_set = (
            sem("lt_made"), sem("fwd_set"), sem("tails_set"), sem("tails_made"), sem("carry_set"),
            sem("runmax_set"), sem("before_set"), sem("beforex_set"))
        hist_made, hist_set, fwdh_set, segmax_set, diff_set, exp_set, ext_made, resc_set, msg_set = (
            sem("hist_made"), sem("hist_set"), sem("fwdh_set"), sem("segmax_set"), sem("diff_set"), sem("exp_set"),
            sem("ext_made"), sem("resc_set"), sem("msg_set"))
        num_t, y_set, sum_ps, cent_set, sq_set, sqsum_set, sqsum_ps, gelu_in, gelu_set, y_done, out_done = (
            sem("num_t"), sem("y_set"), sem("sum_ps"), sem("cent_set"), sem("sq_set"), sem("sqsum_set"),
            sem("sqsum_ps"), sem("gelu_in"), sem("gelu_set"), sem("y_done"), sem("out_done"))

        N_CONST = 14
        N_W = 10 + GT
        COUNTS = -(-(NJ + 1) // GT)

        def wait(eng, s, value):
            if not isinstance(value, int) or value > 0:
                eng.wait_ge(s, value)

        def each_body(eng, body):
            body(0)
            with eng.Fori(1, BODIES - 1) as i:
                body(i)
            body(BODIES - 1)

        def behind(i, s, lag):
            g = i * SLOTS + s - lag
            if isinstance(i, int) and not 0 <= g < GROUPS:
                return None
            return g, (s - lag) % SLOTS, i + (s - lag) // SLOTS

        def chunks_of(q):
            return range(q * JP // JC, (q + 1) * JP // JC) if 0 <= q < PARTS else ()

        def in_registers(engine, row, start, count, largest):
            return nc.values_load_multi_w_load_instructions(
                row[0:1, bass.ds(start, count)], engines=[engine], min_val=0, max_val=largest,
                skip_runtime_bounds_check_because="dst holds node numbers, and the flag bounds the rest")[1]

        def tile_bases(engine, g):
            return in_registers(engine, base_row, g * GT, GT, N)

        def either(eng, engine, fast, general):
            eng.wait_ge(flags_set, 1)
            allowed = nc.values_load_multi_w_load_instructions(
                flag_i[0:1, 0:1], engines=[engine], min_val=0, max_val=1,
                skip_runtime_bounds_check_because="the flag is 0 or 1")[1][0]
            with eng.If(allowed == 1):
                fast()
            with eng.Else():
                general()

        def fast_bodies(eng, body):
            body(0)
            with eng.Fori(1, FAST - 1) as i:
                body(i)
            body(FAST - 1)

        def before_group(i, s):
            return None if isinstance(i, int) and i * FG + s == 0 else i * FG + s - 1

        def rounds(i, s):
            return i * (FG // SLOTS) + s // SLOTS + 1

        block = ctx.enter_context(nc.Block())

        @block.sync
        def _(sp):
            sp.dma_start(blocks(dst_i), dst_rows.rearrange("(b p) e -> p b e", p=T)).then_inc(dst_in, 16)
            sp.dma_start(xs[:, :], x.rearrange("(p j) c -> p (j c)", j=NJ)).then_inc(x_in, 16)
            sp.dma_start(dst_t, dst_cols).then_inc(dstt_in, 16)
            sp.dma_start(first_all, first_dst.partition_broadcast(T)).then_inc(ends_in, 16)
            sp.dma_start(last_all, last_dst.partition_broadcast(T)).then_inc(ends_in, 16)

            def layer0(i):
                for s in range(SLOTS):
                    wait(sp, gathered[0][s], i * (16 * GT))
                    sp.dma_start(idx[:, s, :], src_cols[:, bass.ds((i * SLOTS + s) * GT, GT)]).then_inc(idx_in[0][s], 16)

            layer0(0)
            for q in range(PARTS):
                sp.wait_ge(table_set, q + 1)
                sp.dma_start(agg_n[:, q * JP:(q + 1) * JP, :], hs3[:, q * JP:(q + 1) * JP, :]).then_inc(table_out, 16)
            sp.wait_ge(loc_set, 1)
            sp.dma_start(loc_rows.rearrange("(b p) e -> p b e", p=T), blocks(loc_b)).then_inc(loc_out, 16)
            sp.wait_ge(start_set, 1)
            for h in range(H):
                sp.dma_start(start_rows[:, h, :].rearrange("(b p) e -> p b e", p=T), blocks(start_b)).then_inc(start_out, 16)
            sp.wait_ge(xsum_set, 1)
            sp.dma_start(stage[:, 0:HI - 1, :], agg_table[0:(HI - 1) * T, :].rearrange("(h l) c -> l h c", l=T)).then_inc(stage_in, 16)
            sp.dma_start(stage[0:N - (HI - 1) * T, HI - 1, :], agg_table[(HI - 1) * T:N, :]).then_inc(stage_in, 16)

            def fast0(i):
                for s in range(SLOTS if isinstance(i, int) and i == 0 else 0, FG):
                    wait(sp, gathered[0][s % SLOTS], (rounds(i, s) - 1) * (16 * GT))
                    sp.dma_start(idx[:, s % SLOTS, :], src_cols[:, bass.ds((i * FG + s) * GT, GT)]).then_inc(idx_in[0][s % SLOTS], 16)
                    if s == SLOTS:
                        wait(sp, keys_set, i)
                        sp.dma_start(src_d[:], src_cols[:, bass.ds(DENSE0 + i * K, K)]).then_inc(src_in, 16)

            def general0():
                with sp.Fori(1, BODIES - 1) as i:
                    layer0(i)
                layer0(BODIES - 1)

            either(sp, ENG.SP, lambda: fast_bodies(sp, fast0), general0)

            for c in range(CHUNKS):
                sp.wait_ge(xl_kept, c + 1)
                sp.wait_ge(xr_kept, c + 1)
                sp.dma_start(xl_n[:, c * JC:(c + 1) * JC, :], lr_keep[:, c % 2]).then_inc(lr_out[c % 2], 16)
                sp.dma_start(xr_n[:, c * JC:(c + 1) * JC], xr_parts[:, c % 2]).then_inc(lr_out[c % 2], 16)
            sp.wait_ge(pad_out, 16)
            sp.wait_ge(loc_out, 16)
            sp.wait_ge(start_out, 16 * H)
            for b in range(2):
                sp.wait_ge(lr_out[b], 32 * len(range(b, CHUNKS, 2)))

            def layer1(i):
                for s in range(SLOTS):
                    g = i * SLOTS + s
                    wait(sp, gathered[1][s], i * (16 * GT))
                    if isinstance(i, int) and i == 0:
                        sp.wait_ge(gather_done, 1)
                    sp.dma_start(idx[:, s, :], src_cols[:, bass.ds(g * GT, GT)]).then_inc(idx_in[1][s], 16)
                    bases = tile_bases(ENG.SP, g)
                    wait(sp, g_made, g - SLOTS + 1)
                    wait(sp, segmax_set, g - SLOTS + 1)
                    sp.dma_start(eat[:, s, :], edge_rows[bass.ds(g * T, T), :]).then_inc(edge_in[s], 16)
                    sp.dma_start(locr[:, s, :], loc_rows[bass.ds(g * GT, GT), :].rearrange(
                        "t e -> (t e)").partition_broadcast(T)).then_inc(edge_in[s], 16)
                    sp.dma_start(start[0:GT * H, s, 0:T], start_rows[bass.ds(g * GT, GT), :, :].rearrange(
                        "t h e -> (t h) e")).then_inc(edge_in[s], 16)
                    for t in range(GT):
                        sp.dma_start(xrw[:, s, t], xr_table[bass.ds(bases[t], T)]).then_inc(xrw_in[s], 16)

            each_body(sp, layer1)

            for q in range(PARTS):
                sp.wait_ge(y_done, q + 1)
                at = slice(q * JP, (q + 1) * JP)
                sp.dma_start(out_n[:, at, :], hs3[:, at, :]).then_inc(out_done, 16)
            sp.wait_ge(out_done, 16 * PARTS)

        @block.gpsimd
        def _(pool):
            g = nc.gpsimd
            g.iota(iota_i[:], [[1, T]], base=0, channel_multiplier=0).then_inc(consts_set, 1)
            g.iota(part_i[:], [[1, 1]], base=0, channel_multiplier=1).then_inc(consts_set, 1)
            g.iota(node_i[:], [[1, NJ + 1]], base=0, channel_multiplier=NJ).then_inc(consts_set, 1)
            g.iota(hund_i[:], [[NJ, NP + 1]], base=0, channel_multiplier=0).then_inc(consts_set, 1)
            g.iota(chan_i[:, 0:C], [[1, H], [0, HC]], base=0, channel_multiplier=0).then_inc(consts_set, 1)
            g.iota(chan_i[:, C:CD], [[1, H]], base=0, channel_multiplier=0).then_inc(consts_set, 1)
            g.memset(ones[:], 1.0).then_inc(consts_set, 1)
            g.memset(ones_b[:], 1.0).then_inc(consts_set, 1)
            g.memset(eps_ln[:], LN_EPS).then_inc(consts_set, 1)
            g.memset(eps_bn[:], BN_EPS).then_inc(consts_set, 1)
            g.memset(zeros, 0.0).then_inc(consts_set, 1)
            g.memset(web[:], 0.0).then_inc(consts_set, 1)
            g.iota(key_i[:], [[1, DW * HI]], base=0, channel_multiplier=0).then_inc(consts_set, 1)
            g.memset(zero1[:], 0.0).then_inc(consts_set, 1)

            pool.wait_ge(rows_set, 1)
            for k in range(COUNTS):
                wait(pool, counted, k - 1)
                for t in range(min(GT, NJ + 1 - k * GT)):
                    j = k * GT + t
                    g.indirect_dma_start(out=found[:, k % 2, t, :], out_offset=None, in_=dst_rows,
                                         in_offset=bass.IndirectOffsetOnAxis(ap=rowidx[:, j:j + 1], axis=0)
                                         ).then_inc(found_in[k % 2], 16)

            def gather(layer, n, s, rnd, table, ready, used):
                wait(pool, used, n - SLOTS + 1)
                pool.wait_ge(idx_in[layer][s], 16 * rnd)
                pool.wait_ge(*ready)
                pool.sem_inc(slot_free, 1)
                for t in range(GT):
                    g.indirect_dma_start(out=gbuf[:, s, t, :], out_offset=None, in_=table,
                                         in_offset=bass.IndirectOffsetOnAxis(ap=idx[:, s, t:t + 1], axis=0)
                                         ).then_inc(gathered[layer][s], 16)

            def gather0(n, s, rnd):
                gather(0, n, s, rnd, agg_table, (table_out, 16 * PARTS), summed[0])

            pool.wait_ge(counted, COUNTS)
            either(pool, ENG.Pool,
                   lambda: fast_bodies(pool, lambda i: [gather0(i * FG + s, s % SLOTS, rounds(i, s)) for s in range(FG)]),
                   lambda: each_body(pool, lambda i: [gather0(i * SLOTS + s, s, i + 1) for s in range(SLOTS)]))
            for b in range(2):
                pool.wait_ge(lr_out[b], 32 * len(range(b, CHUNKS, 2)))
            each_body(pool, lambda i: [gather(1, i * SLOTS + s, s, i + 1, xl_table, (lr_out[0], 32 * len(range(0, CHUNKS, 2))),
                                              msg_set) for s in range(SLOTS)])

        @block.vector
        def _(dve):
            v = nc.vector
            steps = [0]

            def link(ins):
                steps[0] += 1
                ins.then_inc(v_step, 1)
                dve.wait_ge(v_step, steps[0])

            dve.wait_ge(consts_set, N_CONST)
            v.tensor_copy(iota_f[:], iota_i[:])
            v.tensor_copy(iota_b[:], iota_i[:])
            v.tensor_copy(iota_k[:], key_i[:])
            v.tensor_copy(part_f[:], part_i[:])
            v.tensor_copy(node_f[:], node_i[:])
            v.tensor_copy(hund_f[:], hund_i[:])
            v.tensor_copy(chan_f[:], chan_i[:])
            v.tensor_scalar(head_i[:], part_i[0:GT * H, :], H - 1, None, ALU.bitwise_and)
            link(v.tensor_scalar(tile_i[:], part_i[0:GT * H, :], H.bit_length() - 1, None, ALU.arith_shift_right))
            v.tensor_copy(head_f[:], head_i[:])
            link(v.tensor_copy(tile_f[:], tile_i[:]))
            link(v.tensor_scalar(ident[:], iota_f[:], part_f[:, 0:1], None, ALU.is_equal))
            v.tensor_tensor(ident2[:], ident[:, 0:C], ident[:, C:2 * C], ALU.add)
            v.tensor_scalar(by_tile[:], iota_f[0:GT * H, 0:GT], tile_f[:, 0:1], None, ALU.is_equal)
            v.tensor_scalar(by_head[:], iota_f[0:GT * H, 0:H], head_f[:, 0:1], None, ALU.is_equal)
            v.tensor_scalar(by_chan[:], chan_f[:], head_f[:, 0:1], None, ALU.is_equal)
            v.memset(lastsum[:], 0.0)
            v.memset(firsts[:], 0.0)
            v.memset(runmax[:], -BIG).then_inc(consts_f, 1)

            dve.wait_ge(dst_in, 16)
            v.tensor_copy(dst_f, dst_i).then_inc(dstf_set, 1)
            dve.wait_ge(dstf_set, 1)
            base = blocks(dst_f)[:, :, 0]
            base_q = base.unsqueeze(2).to_broadcast([T, BLK, NP + 1])
            hund = hund_f[:].unsqueeze(1).to_broadcast([T, BLK, NP + 1])
            link(v.tensor_tensor(ge_b, base_q, hund, ALU.is_ge))
            link(v.tensor_reduce(pa[:], ge_b[:, :, 1:NP + 1], AX.X, ALU.add))
            v.tensor_tensor(in_b, ge_b[:, :, 0:NP], ge_b[:, :, 1:NP + 1], ALU.subtract)
            link(v.scalar_tensor_tensor(jb[:], pa[:], -float(NJ), base, ALU.mult, ALU.add))
            v.tensor_tensor(jlt, jb[:].unsqueeze(2).to_broadcast([T, BLK, NJ + 1]),
                            iota_f[:, 0:NJ + 1].unsqueeze(1).to_broadcast([T, BLK, NJ + 1]), ALU.is_lt)
            v.tensor_tensor(ge_b, base_q, hund, ALU.is_lt).then_inc(onehots_set, 1)
            dve.wait_ge(rows_ps, 1)
            link(v.tensor_scalar(rowblk[:], ps_g[0:NP, 0, 0:NJ + 1], -1.0, 0.0, ALU.add, ALU.max))
            v.tensor_copy(rowidx[:], rowblk[:]).then_inc(rows_set, 1)

            def count(k):
                n = min(GT, NJ + 1 - k * GT)
                at = slice(k * GT, k * GT + n)
                dve.wait_ge(found_in[k % 2], sum(16 * min(GT, NJ + 1 - r * GT) for r in range(k % 2, k + 1, 2)))
                wait(dve, counted, k)
                link(v.tensor_tensor(less[:, 0:n, :], found[:, k % 2, 0:n, :],
                                     node_f[:, at].unsqueeze(2).to_broadcast([NP, n, T]), ALU.is_lt))
                v.tensor_reduce(below[:, at], less[:, 0:n, :], AX.X, ALU.add).then_inc(counted, 1)

            dve.wait_ge(x_in, 16)
            dve.wait_ge(w_in, 16 * N_W)
            dve.wait_ge(pad_out, 16)
            link(v.tensor_reduce(mean[:], xs3, AX.X, ALU.add))
            link(v.tensor_scalar(mean[:], mean[:], 1.0 / C, None, ALU.mult))
            link(v.tensor_tensor(hs3, xs3, mean[:].unsqueeze(2).to_broadcast([NP, NJ, C]), ALU.subtract))
            for q in range(4):
                at = slice(q * NJ // 4, (q + 1) * NJ // 4)
                if q % 2 == 0:
                    count(q // 2)
                link(v.tensor_tensor(squares, hs3[:, at, :], hs3[:, at, :], ALU.mult))
                link(v.tensor_reduce(rstd[:, at], squares, AX.X, ALU.add))
            v.tensor_scalar(rstd[:], rstd[:], 1.0 / C, None, ALU.mult).then_inc(var_set, 1)
            count(2)
            dve.wait_ge(std_set, 1)
            link(v.reciprocal(rstd[:], rstd[:]))
            v.scalar_tensor_tensor(hs3, hs3, 0.0, rstd[:].unsqueeze(2).to_broadcast([NP, NJ, C]),
                                   ALU.max, ALU.mult).then_inc(h_set, 1)
            count(3)
            dve.wait_ge(dstt_in, 16)
            dve.wait_ge(ends_in, 32)
            v.tensor_tensor(loc[:], dst_t, first_all, ALU.subtract)
            v.tensor_tensor(lastm[:], dst_t, last_all, ALU.is_equal)
            count(4)
            v.tensor_copy(base_row, first_all[C:C + 1, :])
            v.tensor_tensor(blocks(loc_b), blocks(dst_f), base.unsqueeze(2).to_broadcast([T, BLK, T]),
                            ALU.subtract).then_inc(loc_set, 1)
            v.memset(blocks(start_b)[:, :, 0:1], 0.0)
            link(v.tensor_tensor(blocks(start_b)[:, :, 1:T], blocks(dst_f)[:, :, 1:T], blocks(dst_f)[:, :, 0:T - 1],
                                 ALU.not_equal))
            count(5)
            v.tensor_scalar(start_b, start_b, -BIG, None, ALU.mult).then_inc(start_set, 1)
            v.memset(cont[:, 0:1], -BIG)
            v.memset(single_prev[:, 0:1], 0.0)
            link(v.tensor_tensor(equal_all[:, 1:TILES], first_all[0:CD, 1:TILES], last_all[0:CD, 0:TILES - 1], ALU.is_equal))
            count(6)
            link(v.tensor_scalar(cont[:, 1:TILES], equal_all[:, 1:TILES], 2 * BIG, -BIG, ALU.mult, ALU.add))
            link(v.tensor_tensor(equal_all, last_all[0:CD, :], first_all[0:CD, :], ALU.subtract))
            supers = first_all[:, DENSE0:DENSE0 + DENSE].rearrange("p (b k) -> p b k", k=K)
            v.tensor_reduce(flag[:, 0:1], equal_all[0:1, DENSE0:DENSE0 + DENSE], AX.X, ALU.max)
            v.tensor_reduce(flag[:, 1:2], equal_all[0:1, DENSE0:REAL - 1], AX.X, ALU.min)
            link(v.tensor_tensor(mean[0:1, 0:FAST], supers[0:1, :, K - 1], supers[0:1, :, 0], ALU.subtract))
            link(v.tensor_reduce(flag[:, 2:3], mean[0:1, 0:FAST], AX.X, ALU.max))
            count(7)
            v.tensor_scalar(flag[:, 0:1], flag[:, 0:1], float(DW - 1), None, ALU.is_le)
            v.tensor_scalar(flag[:, 1:2], flag[:, 1:2], 1.0, None, ALU.is_ge)
            link(v.tensor_scalar(flag[:, 2:3], flag[:, 2:3], float(T - DW), None, ALU.is_le))
            link(v.tensor_reduce(flag[:, 3:4], flag[:, 0:3], AX.X, ALU.min))
            v.tensor_copy(flag_i[:], flag[:, 3:4])
            v.tensor_scalar(single_prev[:, 1:TILES], equal_all[:, 0:TILES - 1], 0.0, None, ALU.is_equal)
            link(v.tensor_scalar(wide[:], equal_all, float(T - 1), None, ALU.is_equal))
            count(8)
            place_f = equal_all[GT * H:GT * H + 1, 0:DENSE]
            link(v.tensor_tensor(place_f.rearrange("p (b k) -> p b k", k=K), supers[GT * H:GT * H + 1],
                                 supers[GT * H:GT * H + 1, :, 0:1].to_broadcast([1, FAST, K]), ALU.subtract))
            v.tensor_scalar(place_row[:, 0:DENSE], place_f, float(HI), None, ALU.mult)
            link(v.tensor_scalar(equal_all[0:H, :], equal_all[0:H, :], 0.0, None, ALU.is_equal))
            link(v.tensor_scalar(equal_all[0:H, :], equal_all[0:H, :], 2 * BIG, -BIG, ALU.mult, ALU.add))
            v.tensor_tensor(chain, cont[0:H, :], equal_all[0:H, :], ALU.min).then_inc(flags_set, 1)
            for k in range(9, COUNTS):
                count(k)

            dve.wait_ge(counted, COUNTS)
            link(v.scalar_tensor_tensor(below[:], rowblk[:], float(T), below[:], ALU.mult, ALU.add))
            v.tensor_tensor(dinv[:], below[:, 1:NJ + 1], below[:, 0:NJ], ALU.subtract).then_inc(deg_set, 1)
            dve.wait_ge(root_set, 1)
            link(v.reciprocal(dinv[:], dinv[:]))
            dve.wait_ge(lin_kept, CHUNKS)
            for q in range(PARTS):
                at = slice(q * JP, (q + 1) * JP)
                v.tensor_tensor(hs3[:, at, :], hs3[:, at, :], dinv[:, at].unsqueeze(2).to_broadcast([NP, JP, C]),
                                ALU.mult).then_inc(table_set, 1)
            link(v.tensor_tensor(xs3, xs3, b0_s[:].unsqueeze(1).to_broadcast([NP, NJ, C]), ALU.add))
            dve.wait_ge(table_out, 16 * PARTS)
            link(v.tensor_tensor(hs3, hs3, dinv[:].unsqueeze(2).to_broadcast([NP, NJ, C]), ALU.mult))
            link(v.tensor_tensor(xs3, xs3, hs3, ALU.add))
            v.memset(stage[:, HI - 1, :], 0.0).then_inc(xsum_set, 1)
            dve.wait_ge(flags_set, 1)
            dve.wait_ge(loc_out, 16)
            dve.wait_ge(start_out, 16 * H)

            def onehot(layer, g, b):
                wait(dve, summed[layer], g - 1)
                v.tensor_tensor(oh[:, b, :, 0:T - 1], loc[:, bass.ds(g * GT, GT)].unsqueeze(2).to_broadcast([T, GT, T - 1]),
                                iota_b[:, 0:T - 1].unsqueeze(1).to_broadcast([T, GT, T - 1]), ALU.is_equal)
                v.tensor_copy(oh[:, b, :, T - 1], lastm[:, bass.ds(g * GT, GT)]).then_inc(oh_set[layer], 1)

            def windows(b, rows):
                return ps_s[0:rows, b, :].rearrange("p (t n) -> p t n", n=T)

            def carry_lasts(layer, w, b, rows):
                dve.wait_ge(summed[layer], w + 1)
                v.tensor_copy(lastsum[0:rows, b, 1:GT + 1], windows(b, rows)[:, :, T - 1])
                v.tensor_copy(lastsum[0:rows, b, 0:1], lastsum[0:rows, 1 - b, GT:GT + 1]).then_inc(lastsum_set[layer], 1)

            def carry_wide(layer, w, b, rows):
                dve.wait_ge(lastsum_set[layer], w + 1)
                v.tensor_tensor(windows(b, rows)[:, :, T - 1], windows(b, rows)[:, :, T - 1], wide[0:rows, bass.ds(w * GT, GT)],
                                ALU.mult).then_inc(firsts_set[layer], 1)

            def carry_drop(layer, w, b, rows):
                dve.wait_ge(drop_set[layer], w + 1)
                dve.wait_ge(lastsum_set[layer], w + 1)
                v.tensor_tensor(joined[0:rows, :], keep[0:rows, b, 1, :], lastsum[0:rows, b, 0:GT],
                                ALU.mult).then_inc(prior_set[layer], 1)

            def carry_own(layer, w, b, rows):
                dve.wait_ge(prior_set[layer], w + 1)
                v.tensor_tensor(joined[0:rows, :], joined[0:rows, :], windows(b, rows)[:, :, 0], ALU.add).then_inc(joined_set[layer], 1)

            def carry_scan(layer, w, b, rows):
                dve.wait_ge(joined_set[layer], w + 1)
                wait(dve, firsts_sb[layer], w)
                v.tensor_tensor_scan(firsts[0:rows, b, :], keep[0:rows, b, 0, :], joined[0:rows, :],
                                     firsts[0:rows, 1 - b, GT - 1:GT], ALU.mult, ALU.add).then_inc(firsts_sb[layer], 1)

            def carry_firsts(layer, w, b, rows):
                dve.wait_ge(firsts_sb[layer], w + 1)
                v.tensor_copy(windows(b, rows)[:, :, 0], firsts[0:rows, b, :]).then_inc(firsts_set[layer], 1)

            def carry0(w, b):
                at = bass.ds(w * GT, GT)
                v.scalar_tensor_tensor(keep[0:C, b, 0, :], cont[0:C, at], 0.0, single_prev[0:C, at],
                                       ALU.is_gt, ALU.mult).then_inc(keep_set[0], 1)
                carry_lasts(0, w, b, C)
                dve.wait_ge(keep_set[0], w + 1)
                v.scalar_tensor_tensor(keep[0:C, b, 1, :], cont[0:C, at], 0.0, keep[0:C, b, 0, :],
                                       ALU.is_gt, ALU.subtract).then_inc(drop_set[0], 1)
                carry_wide(0, w, b, C)
                carry_drop(0, w, b, C)
                carry_own(0, w, b, C)
                carry_scan(0, w, b, C)
                carry_firsts(0, w, b, C)

            def split_table():
                for h in range(2):
                    at = slice(h * HI // 2, (h + 1) * HI // 2)
                    dve.wait_ge(split_a, h + 1)
                    v.tensor_tensor(stage[:, at], stage[:, at], table3[:, at, 0, :], ALU.subtract).then_inc(split_v, 1)
                for h in range(2):
                    at = slice(h * HI // 2, (h + 1) * HI // 2)
                    dve.wait_ge(split_a, h + 3)
                    dve.wait_ge(split_v, h + 1)
                    v.tensor_tensor(table3[:, at, 2, :], stage[:, at], table3[:, at, 1, :], ALU.subtract).then_inc(split_v, 1)

            def keys(i):
                dve.wait_ge(src_in, 16 * (i + 1))
                v.tensor_scalar(lo_i[:], src_d[:], T - 1, None, ALU.bitwise_and).then_inc(low_set, 1)
                v.tensor_scalar(hi_i[:], src_d[:], T.bit_length() - 1, None, ALU.arith_shift_right).then_inc(low_set, 1)
                dve.wait_ge(low_set, 2 * i + 2)
                v.tensor_copy(lo_f[:], lo_i[:])
                v.scalar_tensor_tensor(key_f[:], loc[:, bass.ds(DENSE0 + i * K, K)], float(HI), hi_i[:],
                                       ALU.mult, ALU.add).then_inc(keys_set, 1)
                dve.wait_ge(keys_set, i + 1)

            def hot(i, k):
                wait(dve, built, i * K + k - (1 if k > 0 else 0))
                v.tensor_scalar(lo_hot[:, k % 2, :], iota_b[:], lo_f[:, k:k + 1], None, ALU.is_equal)
                v.tensor_scalar(key_hot[:, k % 2, :], iota_k[:], key_f[:, k:k + 1], None, ALU.is_equal).then_inc(hot_set, 1)

            def add_counts(i, k, place):
                to = counts[:, bass.ds(place, DW * HI)].rearrange("p (h e) -> p h e", h=2)
                dve.wait_ge(zeroed, 2 * i + 2)
                dve.wait_ge(built, i * K + k + 1)
                wait(dve, added, i * K + k)
                v.tensor_tensor(to, to, built_to[k % 2], ALU.add).then_inc(added, 1)

            def dense_rows(i):
                dve.wait_ge(part_set, i + 1)
                v.tensor_tensor(part3, dense_ps[:, 1, :], part3, ALU.add).then_inc(half_set, 1)
                dve.wait_ge(half_set, i + 1)
                wait(dve, dsum_t, i)
                v.tensor_tensor(dsum[:, C:2 * C], dense_ps[:, 0, :], part3, ALU.add).then_inc(dsum_set, 1)

            def dense_add(i):
                first = in_registers(ENG.DVE, base_row, DENSE0 + i * K, 1, N)[0]
                to = acc0b[:, bass.ds(first, T)]
                dve.wait_ge(acc_zero, 1)
                wait(dve, dense_set, i)
                dve.wait_ge(dsum_t, i + 1)
                v.tensor_tensor(to, to, dense_t[C:2 * C, :], ALU.add).then_inc(dense_set, 1)

            def fast0(i):
                first, last = (isinstance(i, int) and i == at for at in (0, FAST - 1))
                for s in range(FG):
                    onehot(0, i * FG + s, s % 2)
                    w = before_group(i, s)
                    if w is not None:
                        carry0(w, (s - 1) % 2)
                    if s == 0:
                        if first:
                            split_table()
                            keys(0)
                        else:
                            dense_rows(i - 1)
                    if s < len(PIECES):
                        piece = PIECES[s]
                        places = in_registers(ENG.DVE, place_row, i * K + piece[0], len(piece), (T - DW) * HI)
                        for k in piece:
                            hot(i, k)
                            if k == 1 and not first:
                                dense_add(i - 1)
                            if k > piece[0]:
                                add_counts(i, k - 1, places[k - 1 - piece[0]])
                        add_counts(i, piece[-1], places[-1])
                    elif s == len(PIECES) and not last:
                        keys(i + 1)

            def fast_loop():
                fast_bodies(dve, fast0)
                carry0(FAST * FG - 1, 1)
                dense_rows(FAST - 1)
                dense_add(FAST - 1)
                dve.wait_ge(dense_set, FAST)
                dve.sem_inc(dense_done, 1)

            def layer0(i, s):
                n, w = behind(i, s, 0), behind(i, s, 1)
                if n is not None:
                    onehot(0, n[0], s % 2)
                if w is not None:
                    carry0(w[0], w[1] % 2)

            def general_loop():
                each_body(dve, lambda i: [layer0(i, s) for s in range(SLOTS)])
                layer0(BODIES, 0)
                dve.sem_inc(dense_done, 1)

            either(dve, ENG.DVE, fast_loop, general_loop)
            dve.wait_ge(gather_done, 1)
            v.memset(h_turn[C:C + 1], 1.0).then_inc(ones_row, 1)

            def add_sums(q):
                for c in chunks_of(q):
                    dve.wait_ge(acc_t, c + 1)
                    for k in range(JC):
                        j = c * JC + k
                        last = v.scalar_tensor_tensor(xs3[:, j, :], acc_to(c)[:, k * C:(k + 1) * C], dinv[:, j:j + 1],
                                                      xs3[:, j, :], ALU.mult, ALU.add)
                    last.then_inc(x1_set, 1)

            def centre(q):
                at = slice(q * JP, (q + 1) * JP)
                dve.wait_ge(x1_set, (q + 1) * JP // JC)
                link(v.tensor_reduce(mean[:, at], xs3[:, at, :], AX.X, ALU.add))
                link(v.tensor_scalar(mean[:, at], mean[:, at], 1.0 / C, None, ALU.mult))
                v.tensor_tensor(hs3[:, at, :], xs3[:, at, :], mean[:, at].unsqueeze(2).to_broadcast([NP, JP, C]),
                                ALU.subtract).then_inc(cent1_set, 1)

            def variance(q):
                at = slice(q * JP, (q + 1) * JP)
                dve.wait_ge(sq1_set, q + 1)
                link(v.tensor_reduce(rstd[:, at], squares1[:, q % 2], AX.X, ALU.add))
                v.tensor_scalar(rstd[:, at], rstd[:, at], 1.0 / C, None, ALU.mult).then_inc(var_set, 1)

            def normed(q):
                at = slice(q * JP, (q + 1) * JP)
                dve.wait_ge(std_set, q + 2)
                link(v.reciprocal(rstd[:, at], rstd[:, at]))
                dve.wait_ge(cent1_set, q + 1)
                v.scalar_tensor_tensor(hs3[:, at, :], hs3[:, at, :], 0.0, rstd[:, at].unsqueeze(2).to_broadcast([NP, JP, C]),
                                       ALU.max, ALU.mult).then_inc(h_set, 1)

            def split_xr(c):
                b = c % 2
                xr_ps = ps_g[0:NP, b, :].rearrange("p (j k) -> p j k", j=JC)[:, :, C:2 * C]
                dve.wait_ge(parts_set, 3 * c + 2)
                v.tensor_tensor(xr_rest[:, b], xr_ps, xr_parts[:, b, :, 0, :], ALU.subtract).then_inc(rest_set, 1)
                dve.wait_ge(parts_set, 3 * c + 3)
                dve.wait_ge(rest_set, c + 1)
                v.tensor_tensor(xr_parts[:, b, :, 2, :], xr_rest[:, b], xr_parts[:, b, :, 1, :],
                                ALU.subtract).then_inc(xr_kept, 1)

            for q in range(PARTS + 2):
                if q < PARTS:
                    add_sums(q)
                    centre(q)
                if 1 <= q <= PARTS:
                    variance(q - 1)
                    normed(q - 1)
                for c in chunks_of(q - 2):
                    if c > 0:
                        split_xr(c - 1)
            split_xr(CHUNKS - 1)

            def one_hot_t(n, s, rnd):
                dve.wait_ge(edge_in[s], 48 * (rnd + 1))
                wait(dve, g_made, n - 1)
                v.tensor_scalar(oht[:, s % 2, :], locr[:, s, :], part_f[:, 0:1], None, ALU.is_equal).then_inc(oht_set, 1)

            v.memset(start[:, :, T:T + 1], 0.0).then_inc(consts_f, 1)
            dve.wait_ge(consts_f, 2)
            one_hot_t(0, 0, 0)

            def layer1(i, s):
                n, y, z, w, ahead = (behind(i, s, lag) for lag in (0, 1, 2, 3, -1))
                if y is not None:
                    y, ys, yr = y
                    dve.wait_ge(edge_in[ys], 48 * (yr + 1))
                    dve.wait_ge(lt_made, y + 1)
                    v.tensor_tensor_scan(fwd[:], start[0:GT * H, ys, 0:T], lt_ps, -BIG, ALU.add, ALU.max).then_inc(fwd_set, 1)
                if w is not None:
                    w, wb = w[0], w[1] % 2
                    carry_lasts(1, w, wb, CD)
                if z is not None:
                    z, zs, zr = z
                    zb = zs % 2
                    dve.wait_ge(exp_set, z + 1)
                    v.tensor_scalar(resc[:], by_tile[:], expt[:, T:T + 1], None, ALU.mult).then_inc(resc_set, 1)
                if y is not None:
                    dve.wait_ge(fwd_set, y + 1)
                    v.tensor_scalar(tails[:], by_tile[:], fwd[:, T - 1:T], None, ALU.mult).then_inc(tails_set, 1)
                if w is not None:
                    carry_wide(1, w, wb, CD)
                    carry_drop(1, w, wb, CD)
                if z is not None:
                    at = bass.ds(z * GT, GT)
                    dve.wait_ge(ext_made, 2 * z + 2)
                    wait(dve, summed[1], z - 1)
                    v.tensor_tensor(keep[:, zb, 0, :], resc_ps, single_prev[:, at], ALU.mult).then_inc(keep_set[1], 1)
                    w8 = ext_ps.rearrange("p (t h) -> p t h", t=GT)
                    v.tensor_copy(msg[:, zb, :, C:CD], w8)
                    dve.wait_ge(keep_set[1], z + 1)
                    v.tensor_tensor(keep[:, zb, 1, :], resc_ps, keep[:, zb, 0, :], ALU.subtract).then_inc(drop_set[1], 1)
                    v.tensor_tensor(msg[:, zb, :, 0:C].rearrange("p t (h c) -> p t h c", h=H),
                                    gbuf[:, zs].rearrange("p t (h c) -> p t h c", h=H),
                                    w8.unsqueeze(3).to_broadcast([T, GT, H, HC]), ALU.mult).then_inc(msg_set, 1)
                if w is not None:
                    carry_own(1, w, wb, CD)
                if y is not None:
                    wait(dve, before_set, y)
                    v.tensor_copy(runmax[:, 0:1], runmax[:, GT:GT + 1]).then_inc(carry_set, 1)
                if w is not None:
                    carry_scan(1, w, wb, CD)
                if y is not None:
                    dve.wait_ge(carry_set, y + 1)
                    dve.wait_ge(tails_made, y + 1)
                    v.tensor_tensor_scan(runmax[:, 1:GT + 1], chain[:, bass.ds(y * GT, GT)], tails_ps, runmax[:, 0:1],
                                         ALU.min, ALU.max).then_inc(runmax_set, 1)
                if w is not None:
                    carry_firsts(1, w, wb, CD)
                if y is not None:
                    dve.wait_ge(runmax_set, y + 1)
                    v.tensor_tensor(before[:], runmax[:, 0:GT], cont[0:H, bass.ds(y * GT, GT)], ALU.min).then_inc(before_set, 1)
                    dve.wait_ge(before_set, y + 1)
                    v.tensor_tensor(beforex[:].rearrange("k (t h) -> k t h", h=H), before[:].unsqueeze(2).to_broadcast([H, GT, H]),
                                    ident[0:H, 0:H].unsqueeze(1).to_broadcast([H, GT, H]), ALU.mult).then_inc(beforex_set, 1)
                    onehot(1, y, ys % 2)
                if n is not None:
                    n = n[0]
                    dve.wait_ge(gathered[1][s], 16 * GT * (i + 1))
                    dve.wait_ge(g_made, n + 1)
                    v.tensor_tensor(lr, rows_to, gbuf[:, s].rearrange("p t c -> p (t c)"), ALU.add).then_inc(row_set, 1)
                if y is not None:
                    dve.wait_ge(hist_made, y + 1)
                    v.tensor_copy(hist[:], hist_ps).then_inc(hist_set, 1)
                if n is not None:
                    dve.wait_ge(row_set, n + 1)
                    v.scalar_tensor_tensor(lr, lr, SLOPE, lr, ALU.mult, ALU.max).then_inc(leaky_set, 1)
                if y is not None:
                    dve.wait_ge(hist_set, y + 1)
                    v.tensor_tensor_scan(fwd[:], start[0:GT * H, ys, 0:T], lt_ps, hist[:, 0:1], ALU.add, ALU.max).then_inc(fwdh_set, 1)
                if n is not None:
                    dve.wait_ge(leaky_set, n + 1)
                    v.tensor_tensor(lr.rearrange("p (t c) -> p t c", t=GT), lr.rearrange("p (t c) -> p t c", t=GT),
                                    att_s[:].unsqueeze(1).to_broadcast([T, GT, C]), ALU.mult).then_inc(prod_set, 1)
                if y is not None:
                    dve.wait_ge(fwdh_set, y + 1)
                    v.tensor_tensor_scan(segmax[:, ::-1], start[0:GT * H, ys, 1:T + 1][:, ::-1], fwd[:, ::-1], -BIG,
                                         ALU.add, ALU.max).then_inc(segmax_set, 1)
                if ahead is not None:
                    one_hot_t(*ahead)
                if y is not None:
                    dve.wait_ge(segmax_set, y + 1)
                    v.tensor_tensor(diff[:, T:T + 1], hist[:], segmax[:, 0:1], ALU.subtract)
                    v.tensor_tensor(diff[:, 0:T], lt_ps, segmax[:], ALU.subtract).then_inc(diff_set, 1)
                if n is not None:
                    dve.wait_ge(prod_set, n + 1)
                    v.tensor_reduce(lg[:], lr.rearrange("p (k c) -> p k c", c=HC), AX.X, ALU.add).then_inc(logits_set, 1)

            each_body(dve, lambda i: [layer1(i, s) for s in range(SLOTS)])
            for s in range(3):
                layer1(BODIES, s)

            def num(c):
                return ps_s[0:NP, c % 2, :].rearrange("p (k e) -> p k e", k=2)[:, :, 0:JE // 2 * CD].rearrange(
                    "p k (j d) -> p k j d", d=CD)

            def rden_of(c):
                return rden[:, c % 2].rearrange("p (k j) h -> p k j h", k=2)

            for c in range(ENDS):
                at = slice(c * JE, (c + 1) * JE)
                dve.wait_ge(num_t, c + 1)
                for k in range(2):
                    last = v.tensor_scalar(rden_of(c)[:, k], num(c)[:, k, :, C:CD], DEN_EPS, None, ALU.add)
                link(last)
                link(v.reciprocal(rden[:, c % 2], rden[:, c % 2]))
                for k in range(2):
                    part = slice(c * JE + k * JE // 2, c * JE + (k + 1) * JE // 2)
                    last = v.tensor_tensor(y3[:, part, :].rearrange("p j (h c) -> p j h c", h=H),
                                           num(c)[:, k, :, 0:C].rearrange("p j (h c) -> p j h c", h=H),
                                           rden_of(c)[:, k].unsqueeze(3).to_broadcast([NP, JE // 2, H, HC]), ALU.mult)
                link(last)
                v.tensor_tensor(y3[:, at, :], y3[:, at, :], bias_s[:].unsqueeze(1).to_broadcast([NP, JE, C]),
                                ALU.add).then_inc(y_set, 1)
            v.tensor_tensor(hs3, hs3, bet_s[:].unsqueeze(1).to_broadcast([NP, NJ, C]), ALU.add)
            dve.wait_ge(sum_ps, 2 * ENDS)
            link(v.tensor_reduce(stat[:, 0, :], ps_g[0:NP, 0, 0:JE // 2 * C].rearrange("p (j c) -> p c j", c=C), AX.X, ALU.add))
            link(v.tensor_scalar(stat[:, 0, :], stat[:, 0, :], 1.0 / N, None, ALU.mult))

            def sum_squares(q):
                dve.wait_ge(sq_set, q + 1)
                v.tensor_reduce(sq_sum[:, q, :], sq[:, q % 2, :].rearrange("p (j c) -> p c j", c=C), AX.X,
                                ALU.add).then_inc(sqsum_set, 1)

            for q in range(PARTS):
                at = slice(q * JP, (q + 1) * JP)
                v.tensor_tensor(y3[:, at, :], y3[:, at, :], stat[:, 0, :].unsqueeze(1).to_broadcast([NP, JP, C]),
                                ALU.subtract).then_inc(cent_set, 1)
                if q > 0:
                    sum_squares(q - 1)
            sum_squares(PARTS - 1)
            dve.wait_ge(sqsum_ps, 1)
            v.tensor_scalar(stat[:, 2, :], ps_g[0:NP, 1, 0:C], 1.0 / N, None, ALU.mult).then_inc(var_set, 1)
            dve.wait_ge(std_set, PARTS + 2)
            link(v.reciprocal(stat[:, 2, :], stat[:, 2, :]))
            link(v.tensor_tensor(stat[:, 2, :], stat[:, 2, :], gam_s[:], ALU.mult))

            def finish(q):
                at = slice(q * JP, (q + 1) * JP)
                dve.wait_ge(gelu_set, q + 1)
                v.tensor_tensor(hs3[:, at, :], y3[:, at, :], xs3[:, at, :], ALU.add).then_inc(y_done, 1)

            for q in range(PARTS):
                at = slice(q * JP, (q + 1) * JP)
                link(v.tensor_tensor(y3[:, at, :], y3[:, at, :], stat[:, 2, :].unsqueeze(1).to_broadcast([NP, JP, C]), ALU.mult))
                v.tensor_tensor(y3[:, at, :], y3[:, at, :], hs3[:, at, :], ALU.add).then_inc(gelu_in, 1)
                if q > 0:
                    finish(q - 1)
            finish(PARTS - 1)

        @block.scalar
        def _(act):
            a = nc.scalar
            act.dma_start(w0_s[:], w0).then_inc(w_in, 16)
            act.dma_start(wlr[0:C, 0:C], w_l).then_inc(w_in, 16)
            act.dma_start(wlr[0:C, C:2 * C], w_r).then_inc(w_in, 16)
            act.dma_start(wlr[C:C + 1, 0:C], b_l.unsqueeze(0)).then_inc(w_in, 16)
            act.dma_start(wlr[C:C + 1, C:2 * C], b_r.unsqueeze(0)).then_inc(w_in, 16)
            for to, vec in ((b0_s, b0), (bias_s, bias), (gam_s, gamma), (bet_s, beta)):
                act.dma_start(to[:], vec.partition_broadcast(NP)).then_inc(w_in, 16)
            act.dma_start(att_s[:], att.rearrange("h c -> (h c)").partition_broadcast(T)).then_inc(w_in, 16)
            act.wait_ge(consts_set, N_CONST)
            for t in range(GT):
                act.dma_start(web[t * ED:(t + 1) * ED, t * C:(t + 1) * C], w_e).then_inc(w_in, 16)
            act.dma_start(xr_table[N:NW], zeros).then_inc(pad_out, 16)

            act.wait_ge(var_set, 1)
            a.activation(rstd[:], rstd[:], ACT.Sqrt, bias=eps_ln[:, 0:1]).then_inc(std_set, 1)
            for c in range(CHUNKS):
                act.wait_ge(h_t, c + 1)
                wait(act, lin_ps, c - 1)
                a.activation(h_turn[0:C, c % 2].rearrange("p k q -> p (k q)"), ps_s[0:C, c % 2, 0:JC * NP],
                             ACT.Copy).then_inc(ht_set, 1)
                if c > 0:
                    act.wait_ge(lin_ps, c)
                    a.activation(hs[:, (c - 1) * JC * C:c * JC * C], ps_g[0:NP, (c - 1) % 2, 0:JC * C], ACT.Copy).then_inc(lin_kept, 1)
            act.wait_ge(lin_ps, CHUNKS)
            a.activation(hs[:, (CHUNKS - 1) * JC * C:], ps_g[0:NP, (CHUNKS - 1) % 2, 0:JC * C], ACT.Copy).then_inc(lin_kept, 1)
            act.wait_ge(deg_set, 1)
            a.activation(dinv[:], dinv[:], ACT.Sqrt, bias=ones[0:NP, 0:1]).then_inc(root_set, 1)

            def keep_sums(layer, w, b, rows, acc):
                bases = tile_bases(ENG.Activation, w)
                act.wait_ge(firsts_set[layer], 2 * w + 2)
                for t in range(GT):
                    wait(act, acc_set[layer], w * GT + t)
                    act.wait_ge(flags_set, 1)
                    a.activation(acc[:, bass.ds(bases[t], T)], ps_s[0:rows, b, t * T:(t + 1) * T],
                                 ACT.Copy).then_inc(acc_set[layer], 1)

            act.wait_ge(flags_set, 1)
            a.activation(arena[:, :], zero1[:, 0:1].to_broadcast([T, NW]), ACT.Copy).then_inc(acc_zero, 1)
            act.wait_ge(acc_zero, 1)

            def split_table():
                act.wait_ge(stage_in, 32)
                act.wait_ge(loc_out, 16)
                act.wait_ge(start_out, 16 * H)
                for k in range(2):
                    for h in range(2):
                        at = slice(h * HI // 2, (h + 1) * HI // 2)
                        wait(act, split_v, h + 1 if k == 1 else 0)
                        a.activation(table3[:, at, k, :], stage[:, at], ACT.Copy).then_inc(split_a, 1)

            def clear(h):
                half = slice(h * T * HI // 4, (h + 1) * T * HI // 4)
                a.activation(counts_w[:, half], zero1[:, 0:1].to_broadcast([T, T * HI // 4]), ACT.Copy).then_inc(zeroed, 1)

            def dense_part(i):
                act.wait_ge(dense_made, i + 1)
                wait(act, dsum_t, i)
                a.activation(part3, dense_ps[:, 2, :], ACT.Copy).then_inc(part_set, 1)

            def fast0(i):
                first = isinstance(i, int) and i == 0
                for s in range(FG):
                    if s == 0:
                        if first:
                            split_table()
                            act.wait_ge(split_v, 4)
                        else:
                            dense_part(i - 1)
                        clear(0)
                    w = before_group(i, s)
                    if w is not None:
                        keep_sums(0, w, (s - 1) % 2, C, acc0)
                    if s == 0:
                        clear(1)

            def fast_loop():
                fast_bodies(act, fast0)
                keep_sums(0, FAST * FG - 1, 1, C, acc0)
                dense_part(FAST - 1)
                act.wait_ge(acc_set[0], FAST * FG * GT)
                act.sem_inc(gather_done, 1)

            def layer0(i, s):
                w = behind(i, s, 1)
                if w is not None:
                    keep_sums(0, w[0], w[1] % 2, C, acc0)

            def general_loop():
                each_body(act, lambda i: [layer0(i, s) for s in range(SLOTS)])
                layer0(BODIES, 0)
                act.wait_ge(acc_set[0], GROUPS * GT)
                act.sem_inc(gather_done, 1)

            either(act, ENG.Activation, fast_loop, general_loop)

            def square(q):
                act.wait_ge(cent1_set, q + 1)
                wait(act, var_set, q)
                a.activation(squares1[:, q % 2].rearrange("p j c -> p (j c)"), hs[:, q * JP * C:(q + 1) * JP * C],
                             ACT.Square).then_inc(sq1_set, 1)

            def root(q):
                at = slice(q * JP, (q + 1) * JP)
                act.wait_ge(var_set, q + 2)
                a.activation(rstd[:, at], rstd[:, at], ACT.Sqrt, bias=eps_ln[:, 0:1]).then_inc(std_set, 1)

            def turned(c):
                act.wait_ge(h1_t, c + 1)
                wait(act, lr_ps, c - 1)
                a.activation(h_turn[0:C, c % 2].rearrange("p k q -> p (k q)"), ps_s[0:C, c % 2, 0:JC * NP],
                             ACT.Copy).then_inc(h1t_set, 1)

            def split(c):
                b = c % 2
                rows = ps_g[0:NP, b, :].rearrange("p (j k) -> p j k", j=JC)
                act.wait_ge(lr_ps, c + 1)
                wait(act, lr_out[b], 32 * (c // 2))
                a.activation(lr_keep[:, b], rows[:, :, 0:C], ACT.Copy).then_inc(xl_kept, 1)
                a.activation(xr_parts[:, b, :, 0, :], rows[:, :, C:2 * C], ACT.Copy).then_inc(parts_set, 2)
                act.wait_ge(rest_set, c + 1)
                a.activation(xr_parts[:, b, :, 1, :], xr_rest[:, b], ACT.Copy).then_inc(parts_set, 1)

            for q in range(PARTS + 2):
                if q < PARTS:
                    square(q)
                if 1 <= q <= PARTS:
                    root(q - 1)
                for c in chunks_of(q - 2):
                    turned(c)
                    if c > 0:
                        split(c - 1)
            split(CHUNKS - 1)

            def layer1(i, s):
                y, w = behind(i, s, 1), behind(i, s, 3)
                if w is not None:
                    keep_sums(1, w[0], w[1] % 2, CD, acc1)
                if y is not None:
                    y = y[0]
                    act.wait_ge(diff_set, y + 1)
                    wait(act, ext_made, 2 * y)
                    a.activation(expt[:], diff[:], ACT.Exp).then_inc(exp_set, 1)

            each_body(act, lambda i: [layer1(i, s) for s in range(SLOTS)])
            for s in range(3):
                layer1(BODIES, s)

            for q in range(PARTS):
                act.wait_ge(cent_set, q + 1)
                wait(act, sqsum_set, q - 1)
                a.activation(sq[:, q % 2, :], y[:, q * JP * C:(q + 1) * JP * C], ACT.Square).then_inc(sq_set, 1)
            act.wait_ge(var_set, PARTS + 2)
            a.activation(stat[:, 2, :], stat[:, 2, :], ACT.Sqrt, bias=eps_bn[:, 0:1]).then_inc(std_set, 1)
            for q in range(PARTS):
                at = slice(q * JP * C, (q + 1) * JP * C)
                act.wait_ge(gelu_in, q + 1)
                a.activation(y[:, at], y[:, at], ACT.Gelu).then_inc(gelu_set, 1)

        @block.tensor
        def _(pe):
            m = nc.tensor
            pe.wait_ge(consts_f, 1)
            pe.wait_ge(onehots_set, 1)
            for k in range(BLK):
                m.matmul(ps_g[0:NP, 0, 0:NJ + 1], in_b[:, k, :], jlt[:, k, :], start=(k == 0), stop=False)
                last = m.matmul(ps_g[0:NP, 0, 0:NJ + 1], ge_b[:, k, 0:NP], ones_b[:, 0:NJ + 1], start=False, stop=(k == BLK - 1))
            last.then_inc(rows_ps, 1)

            def turn_rows(c, to):
                for k in range(JC):
                    last = m.transpose(ps_s[0:C, c % 2, k * NP:(k + 1) * NP], hs3[:, c * JC + k, :], ident[0:NP, 0:NP])
                last.then_inc(to, 1)

            pe.wait_ge(rows_set, 1)
            pe.wait_ge(h_set, 1)
            for c in range(CHUNKS + 1):
                if c < CHUNKS:
                    wait(pe, ht_set, c - 1)
                    turn_rows(c, h_t)
                if c > 0:
                    d = c - 1
                    pe.wait_ge(ht_set, d + 1)
                    wait(pe, lin_kept, d - 1)
                    for k in range(JC):
                        last = m.matmul(ps_g[0:NP, d % 2, k * C:(k + 1) * C], h_turn[0:C, d % 2, k, :], w0_s[:], start=True, stop=True)
                    last.then_inc(lin_ps, 1)

            def sums(layer, g, b, rows, rows_of):
                pe.wait_ge(oh_set[layer], g + 1)
                wait(pe, acc_set[layer], (g - 1) * GT)
                for t in range(GT):
                    last = m.matmul(ps_s[0:rows, b, t * T:(t + 1) * T], rows_of(t), oh[:, b, t, :], start=True, stop=True)
                last.then_inc(summed[layer], 1)

            def layer0(i, s):
                pe.wait_ge(gathered[0][s], 16 * GT * (i + 1))
                sums(0, i * SLOTS + s, s % 2, C, lambda t: gbuf[:, s, t, :])

            def build(i, k):
                pe.wait_ge(hot_set, i * K + k + 1)
                wait(pe, added, i * K + k - (1 if k > 0 else 0))
                if k == 1:
                    wait(pe, dense_set, i)
                for h in range(2):
                    last = m.matmul(built_to[k % 2][:, h, :], lo_hot[:, k % 2, :],
                                    key_hot[:, k % 2, h * DW * HI // 2:(h + 1) * DW * HI // 2], start=True, stop=True)
                last.then_inc(built, 1)

            def dense(i, part):
                by_hi = counts.rearrange("p (d h) -> p h d", h=HI)
                pe.wait_ge(added, i * K + K)
                for h in range(part * HI // 2, (part + 1) * HI // 2):
                    last = m.matmul(dense_ps.rearrange("p k c -> p (k c)"), by_hi[:, h, :], table3[:, h].rearrange("p k c -> p (k c)"),
                                    start=(h == 0), stop=(h == HI - 1))
                if part == 1:
                    last.then_inc(dense_made, 1)

            def dense_turn(i):
                pe.wait_ge(consts_f, 1)
                pe.wait_ge(dsum_set, i + 1)
                m.transpose(dense_t, dsum[:], ident[:]).then_inc(dsum_t, 1)

            def fast0(i):
                first = isinstance(i, int) and i == 0
                for s in range(FG):
                    pe.wait_ge(gathered[0][s % SLOTS], 16 * GT * rounds(i, s))
                    sums(0, i * FG + s, s % 2, C, lambda t: gbuf[:, s % SLOTS, t, :])
                    if s == 0 and not first:
                        dense_turn(i - 1)
                    if s < len(PIECES):
                        for k in PIECES[s]:
                            build(i, k)
                    else:
                        dense(i, s - len(PIECES))

            def fast_loop():
                fast_bodies(pe, fast0)
                dense_turn(FAST - 1)

            either(pe, ENG.PE, fast_loop, lambda: each_body(pe, lambda i: [layer0(i, s) for s in range(SLOTS)]))

            pe.wait_ge(gather_done, 1)
            pe.wait_ge(dense_done, 1)
            def product(d):
                pe.wait_ge(h1t_set, d + 1)
                wait(pe, xl_kept, d - 1)
                wait(pe, xr_kept, d - 1)
                for k in range(JC):
                    last = m.matmul(ps_g[0:NP, d % 2, k * 2 * C:(k + 1) * 2 * C], h_turn[:, d % 2, k, :], wlr[:], start=True, stop=True)
                last.then_inc(lr_ps, 1)

            pe.wait_ge(ones_row, 1)
            for q in range(PARTS + 2):
                for c in chunks_of(q):
                    wait(pe, x1_set, c - 1)
                    for k in range(JC):
                        last = m.matmul(acc_to(c)[:, k * C:(k + 1) * C], acc0_n[:, c * JC + k, :], ident2[:], start=True, stop=True)
                    last.then_inc(acc_t, 1)
                for c in chunks_of(q - 2):
                    pe.wait_ge(h_set, q)
                    wait(pe, h1t_set, c - 1)
                    turn_rows(c, h1_t)
                    if c > 0:
                        product(c - 1)
            product(CHUNKS - 1)
            pe.wait_ge(xl_kept, CHUNKS)
            pe.wait_ge(xr_kept, CHUNKS)

            def layer1(i, s):
                n, y, z = (behind(i, s, lag) for lag in (0, 1, 2))
                if y is not None:
                    y, ys, yr = y
                    pe.wait_ge(consts_f, 1)
                    pe.wait_ge(logits_set, y + 1)
                    wait(pe, diff_set, y)
                    m.transpose(lt_ps, lg[:], ident[:]).then_inc(lt_made, 1)
                if z is not None:
                    z, zs, zr = z
                    zb = zs % 2
                    pe.wait_ge(consts_f, 1)
                    pe.wait_ge(exp_set, z + 1)
                    m.transpose(ext_ps, expt[:, 0:T], ident[0:GT * H, 0:GT * H]).then_inc(ext_made, 1)
                    pe.wait_ge(consts_f, 1)
                    pe.wait_ge(resc_set, z + 1)
                    m.matmul(resc_ps, by_chan[:], resc[:], start=True, stop=True).then_inc(ext_made, 1)
                if n is not None:
                    n = n[0]
                    pe.wait_ge(consts_f, 1)
                    pe.wait_ge(edge_in[s], 48 * (i + 1))
                    wait(pe, row_set, n)
                    m.matmul(rows_to, eat[:, s, :], web[:], start=True, stop=False)
                if y is not None:
                    pe.wait_ge(consts_f, 1)
                    pe.wait_ge(tails_set, y + 1)
                    m.matmul(tails_ps, by_head[:], tails[:], start=True, stop=True).then_inc(tails_made, 1)
                if n is not None:
                    pe.wait_ge(consts_f, 1)
                    pe.wait_ge(oht_set, n + 1)
                    pe.wait_ge(xrw_in[s], 16 * GT * (i + 1))
                    for t in range(GT):
                        for k in range(3):
                            last = m.matmul(rows_to[:, t * C:(t + 1) * C], oht[:, s % 2, t * T:(t + 1) * T], xrw[:, s, t, k, :],
                                            start=False, stop=(t == GT - 1 and k == 2))
                    last.then_inc(g_made, 1)
                if y is not None:
                    pe.wait_ge(consts_f, 1)
                    pe.wait_ge(beforex_set, y + 1)
                    m.matmul(hist_ps, beforex[:], ones[0:H, 0:1], start=True, stop=True).then_inc(hist_made, 1)
                if z is not None:
                    pe.wait_ge(msg_set, z + 1)
                    sums(1, z, zb, CD, lambda t: msg[:, zb, t, :])

            each_body(pe, lambda i: [layer1(i, s) for s in range(SLOTS)])
            for s in range(2):
                layer1(BODIES, s)

            pe.wait_ge(acc_set[1], GROUPS * GT)
            for c in range(ENDS + 1):
                if c < ENDS:
                    wait(pe, y_set, c - 1)
                    for k in range(JE):
                        at = k // (JE // 2) * (GE // 2) + k % (JE // 2) * CD
                        last = m.transpose(ps_s[0:NP, c % 2, at:at + CD], acc1_n[:, c * JE + k, :], ident[0:CD, 0:CD])
                    last.then_inc(num_t, 1)
                if c > 0:
                    pe.wait_ge(y_set, c)
                    for k in range(2 * c - 2, 2 * c):
                        m.matmul(ps_g[0:NP, 0, 0:JE // 2 * C], ones[0:NP, 0:NP], y[:, k * JE // 2 * C:(k + 1) * JE // 2 * C],
                                 start=(k == 0), stop=(k == 2 * ENDS - 1)).then_inc(sum_ps, 1)
            pe.wait_ge(sqsum_set, PARTS)
            for q in range(PARTS):
                last = m.matmul(ps_g[0:NP, 1, 0:C], ones[0:NP, 0:NP], sq_sum[:, q, :], start=(q == 0), stop=(q == PARTS - 1))
            last.then_inc(sqsum_ps, 1)


_INS = ["x", "src_cols", "dst_rows", "dst_cols", "first_dst", "last_dst", "edge_rows", "L0_gnn_W", "L0_gnn_b", "L1_gnn_W_l",
        "L1_gnn_b_l", "L1_gnn_W_r", "L1_gnn_b_r", "L1_gnn_W_e", "L1_gnn_att", "L1_gnn_bias", "L1_gnn_gamma", "L1_gnn_beta"]


def lay_out(inputs):
    import numpy as _np

    def tiles(a, pad):
        padded = _np.full((TILES * T,) + a.shape[1:], pad, a.dtype)
        padded[:E] = a
        return padded.reshape((TILES, T) + a.shape[1:])

    arrays = {name: _np.ascontiguousarray(a) for name, a in inputs.items()}
    src, dst = tiles(arrays.pop("src"), 0), tiles(arrays.pop("dst"), N)
    edges = tiles(arrays.pop("edge_attr_16"), 0)
    arrays["src_cols"] = _np.ascontiguousarray(src.T)
    arrays["dst_rows"], arrays["dst_cols"] = dst, _np.ascontiguousarray(dst.T)
    arrays["first_dst"], arrays["last_dst"] = _np.ascontiguousarray(dst[:, 0]), _np.ascontiguousarray(dst[:, T - 1])
    arrays["edge_rows"] = _np.ascontiguousarray(edges.transpose(0, 2, 1)).reshape(TILES * ED, T)
    return arrays


def kernel(**inputs):
    import concourse.bacc as _bacc
    from concourse import mybir as _mybir
    from concourse.bass_utils import run_bass_kernel_spmd as _run

    laid = lay_out(inputs)
    nc = _bacc.Bacc("TRN2", target_bir_lowering=False, num_devices=1)
    arrays, args = {}, []
    for name in _INS:
        a = laid[name]
        arrays[f"in_{name}_dram"] = a
        args.append(nc.dram_tensor(f"in_{name}_dram", a.shape, _mybir.dt.from_np(a.dtype), kind="ExternalInput").ap())
    args.append(nc.dram_tensor("out_dram", (N, C), F32, kind="ExternalOutput").ap())
    gnn_kernel(nc, *args)
    r = _run(nc, [arrays], core_ids=[0])
    return r.results[0]["out_dram"]
```

```python
import concourse.bass as bass
from concourse import mybir
from contextlib import ExitStack

F32 = mybir.dt.float32
BF16 = mybir.dt.bfloat16
I32 = mybir.dt.int32
I16 = mybir.dt.int16
ALU = mybir.AluOpType
ACT = mybir.ActivationFunctionType
AX = mybir.AxisListType
ENG = mybir.EngineType

N = 12500
E = 412500
C = 64
H = 4
HC = C // H
ED = 16
T = 128
GT = 8
SLOTS = 4
GE = GT * T
BODIES = -(-E // (SLOTS * GE))
GROUPS = BODIES * SLOTS
BLK = -(-(GROUPS * GT) // T)
TILES = BLK * T
NP, NJ = 125, 100
JC = 4
CHUNKS = NJ // JC
NW = N + T
CD = C + H
BIG = 1.0e38
SLOPE = 0.2
LN_EPS = 1e-5
BN_EPS = 1e-5
DEN_EPS = 1e-16
PARTS = 5
JP = NJ // PARTS
JE = 10
ENDS = NJ // JE
REAL = -(-E // T)
SLOTS0 = 3
FG = 2 * SLOTS0
K = 29
DW = 6
COUNTED = 4
PIECES = [range(K * s // COUNTED, K * (s + 1) // COUNTED) for s in range(COUNTED)]
LATE = 3
HI = -(-N // T)
FAST = -(-REAL // (FG * GT + K))
DENSE0 = FAST * FG * GT
DENSE = FAST * K
assert DENSE0 + DENSE <= TILES


def gnn_kernel(nc, x, src_cols, dst_rows, dst_cols, first_dst, last_dst, edge_rows, w0, b0, w_l, b_l, w_r, b_r, w_e,
               att, bias, gamma, beta, out):
    ctx = ExitStack()
    with ctx:
        def sb(name, shape, dt=F32):
            return ctx.enter_context(nc.sbuf_tensor(name, shape, dt))

        def pb(name, shape, dt=F32):
            return ctx.enter_context(nc.psum_tensor(name, shape, dt))

        def sem(name):
            return ctx.enter_context(nc.semaphore(name))

        def dram(name, shape, dt=F32):
            return nc.dram_tensor(name, shape, dt, kind="Internal").ap()

        loc_rows = dram("loc_rows", [TILES, T], BF16)
        start_rows = dram("start_rows", [TILES, H, T], BF16)
        agg_table = dram("agg_table", [N, C])
        xl_table = dram("xl_table", [N, C])
        xr_table = dram("xr_table", [NW, 3, C], BF16)

        xs = sb("xs", [NP, NJ * C])
        hs_all = sb("hs", [T, NJ * C])
        hs = hs_all[0:NP, :]
        arena = sb("arena", [T, NW])
        acc0 = arena[0:C, :]
        acc1 = arena[0:CD, :]
        loc = sb("loc", [T, TILES], BF16)
        lastm = sb("lastm", [T, TILES], BF16)
        alone = sb("alone", [CD, TILES], BF16)
        open_ = sb("open_", [CD, TILES], BF16)
        cont = open_[0:H, :]
        wide = sb("wide", [CD, TILES], BF16)
        by_tiles = sb("by_tiles", [C + 1, TILES], BF16)
        place_row = by_tiles[GT * H:GT * H + 1, :].bitcast(I16)
        chain = by_tiles[0:H, :]
        base_row = by_tiles[C:C + 1, :].bitcast(I16)

        sizes = dict(g=SLOTS * GT * C, oh=2 * GE, xrw=SLOTS * GT * 3 * C // 2, oht=GE, msg=2 * GT * CD,
                     lr=GT * C, locr=SLOTS * GE // 2, ea=SLOTS * T, start=SLOTS * (T + 2) // 2)
        RING = SLOTS * GT * C + 2 * GE + HI * 3 * C // 2
        assert RING >= sum(sizes.values())
        ring = sb("ring", [T, RING])
        offs, at = {}, 0
        for key, size in sizes.items():
            offs[key] = at
            at += size

        def piece(key):
            return ring[:, offs[key]:offs[key] + sizes[key]]

        gbuf = piece("g").rearrange("p (s t c) -> p s t c", s=SLOTS, t=GT)
        xrw = piece("xrw").bitcast(BF16).rearrange("p (s t k c) -> p s t k c", s=SLOTS, t=GT, k=3)
        oht = piece("oht").bitcast(BF16).rearrange("p (b e) -> p b e", b=2)
        oh = piece("oh").rearrange("p (b t n) -> p b t n", b=2, t=GT)
        msg = piece("msg").rearrange("p (b t c) -> p b t c", b=2, t=GT)
        lr = piece("lr")
        locr = piece("locr").bitcast(BF16).rearrange("p (s e) -> p s e", s=SLOTS)
        eat = piece("ea").rearrange("p (s e) -> p s e", s=SLOTS)
        start = piece("start").bitcast(BF16).rearrange("p (s e) -> p s e", s=SLOTS)

        idx = sb("idx", [T, SLOTS, GT], I32)
        lg = sb("lg", [T, GT * H])
        small = sb("small", [T, DW * HI])
        fwd = small[0:GT * H, 0:T]
        segmax = small[0:GT * H, T:2 * T]
        diff = small[0:GT * H, 2 * T:3 * T + 1]
        expt = small[0:GT * H, 3 * T + 1:4 * T + 2]
        tails = sb("tails", [GT * H, GT])
        resc = sb("resc", [GT * H, GT])
        hist = sb("hist", [GT * H, 1])
        runmax = sb("runmax", [H, GT + 1])
        before = sb("before", [H, GT])
        beforex = sb("beforex", [H, GT * H])
        keep = sb("keep", [CD, 2, 2, GT])
        lastsum = sb("lastsum", [CD, 2, GT + 1])
        joined = sb("joined", [CD, GT])
        firsts = sb("firsts", [CD, 2, GT])

        table3 = ring[:, RING - HI * 3 * C // 2:].bitcast(BF16).rearrange("p (h k c) -> p h k c", h=HI, k=3)
        stage = hs_all[:, 0:HI * C].rearrange("p (h c) -> p h c", h=HI)
        counts = hs_all[:, 0:T * HI // 2].bitcast(BF16)
        counts_w = hs_all[:, 0:T * HI // 2]
        lo_hot = hs_all[:, T * HI // 2:T * HI // 2 + T].bitcast(BF16).rearrange("p (b l) -> p b l", b=2)
        key_hot = small[:, :].bitcast(BF16).rearrange("p (b k) -> p b k", b=2)
        iota_k = sb("iota_k", [T, DW * HI], I16)
        src_d = sb("src_d", [T, K], I32)
        hi_i = sb("hi_i", [T, K], I32)
        lo_i = sb("lo_i", [T, K], I32)
        lo_f = sb("lo_f", [T, K])
        key_f = sb("key_f", [T, K])
        dsum = sb("dsum", [T, T])
        part3 = dsum[:, 0:C]
        flag = sb("flag", [1, 4])
        flag_i = sb("flag_i", [1, 1], I32)
        zero1 = sb("zero1", [T, 1])
        ident2 = sb("ident2", [T, C])
        acc0b = arena[C:2 * C, :]

        iota_f = sb("iota_f", [T, T])
        iota_b = sb("iota_b", [T, T], BF16)
        part_i = sb("part_i", [T, 1], I32)
        part_f = sb("part_f", [T, 1])
        ident = sb("ident", [T, T])
        ones = sb("ones", [T, T])
        ones_b = sb("ones_b", [T, T], BF16)
        node_f = sb("node_f", [NP, NJ + 1])
        head_i = sb("head_i", [GT * H, 1], I32)
        head_f = sb("head_f", [GT * H, 1])
        tile_i = sb("tile_i", [GT * H, 1], I32)
        tile_f = sb("tile_f", [GT * H, 1])
        chan_f = sb("chan_f", [GT * H, CD])
        by_tile = sb("by_tile", [GT * H, GT])
        by_head = sb("by_head", [GT * H, H])
        by_chan = sb("by_chan", [GT * H, CD])
        w0_s = sb("w0_s", [C, C])
        wlr = sb("wlr", [C + 1, 2 * C])
        web = sb("web", [T, GT * C])
        att_s = sb("att_s", [T, C])
        b0_s = sb("b0_s", [NP, C])
        bias_s = sb("bias_s", [NP, C])
        gam_s = sb("gam_s", [NP, C])
        bet_s = sb("bet_s", [NP, C])
        eps_ln = sb("eps_ln", [NP, 1])
        eps_bn = sb("eps_bn", [NP, 1])
        rowblk = sb("rowblk", [NP, NJ + 1])
        rowidx = sb("rowidx", [NP, NJ + 1], I32)
        below = sb("below", [NP, NJ + 1])
        dinv = sb("dinv", [NP, NJ])
        mean = sb("mean", [NP, NJ])
        rstd = sb("rstd", [NP, NJ])
        stat = sb("stat", [NP, 3, C])
        pa = sb("pa", [T, BLK])
        jb = sb("jb", [T, BLK])

        ps_g = pb("ps_g", [T, 2, GT * C])
        ps_s = pb("ps_s", [T, 2, GE])
        ps_x = pb("ps_x", [T, 2, 512])
        ps_e = ps_x[:, 0, :]
        built_to = [ps_x, ps_g]
        dense_ps = ps_g[:, 0, 0:3 * C].rearrange("p (k c) -> p k c", k=3)
        dense_t = ps_g[:, 1, 0:T]
        rows_to = ps_g[:, 0, :]
        ext_ps = ps_g[:, 1, 0:GT * H]
        resc_ps = ps_g[0:CD, 1, T:T + GT]
        lt_ps = ps_e[0:GT * H, 0:T]
        tails_ps = ps_e[0:H, 2 * T:2 * T + GT]
        hist_ps = ps_e[0:GT * H, 3 * T:3 * T + 1]

        def blocks(ap):
            return ap.rearrange("p (b e) -> p b e", e=T)

        dst_i = arena[:, 0:TILES].bitcast(I32)
        dst_f = arena[:, 0:TILES]
        first_all = arena[:, TILES:2 * TILES].bitcast(I32)
        last_all = arena[:, 2 * TILES:3 * TILES].bitcast(I32)
        squares = arena[0:NP, 3 * TILES:3 * TILES + NJ * C // 4].rearrange("p (j c) -> p j c", c=C)
        found = ring[0:NP, 0:2 * GE].bitcast(I32).rearrange("p (b t e) -> p b t e", b=2, t=GT)
        less = ring[0:NP, 2 * GE:3 * GE].rearrange("p (t e) -> p t e", t=GT)
        h_turn = ring[0:C + 1, 3 * GE:3 * GE + 2 * JC * NP].rearrange("p (b k q) -> p b k q", b=2, k=JC)
        dst_t = ring[:, offs["xrw"]:offs["xrw"] + TILES].bitcast(I32)
        stages = RING - TILES
        loc_b = ring[:, stages:stages + TILES // 2].bitcast(BF16)
        start_b = ring[:, stages + TILES // 2:stages + TILES].bitcast(BF16)
        equal_all = ring[0:CD, offs["xrw"]:offs["xrw"] + TILES]
        ge_b = hs_all[:, 0:BLK * (NP + 1) // 2].bitcast(BF16).rearrange("p (b q) -> p b q", b=BLK)
        in_b = hs_all[:, 1700:1700 + BLK * NP // 2].bitcast(BF16).rearrange("p (b q) -> p b q", b=BLK)
        jlt = hs_all[:, 3400:3400 + BLK * (NJ + 1) // 2].bitcast(BF16).rearrange("p (b j) -> p b j", b=BLK)
        iota_i = hs_all[:, 4800:4800 + T].bitcast(I32)
        node_i = hs_all[0:NP, 4960:4960 + NJ + 1].bitcast(I32)
        hund_i = hs_all[:, 5100:5100 + NP + 1].bitcast(I32)
        chan_i = hs_all[0:GT * H, 5260:5260 + CD].bitcast(I32)
        hund_f = hs_all[:, 5360:5360 + NP + 1]
        zeros = hs_all[:, 5600:5600 + 3 * C // 2].bitcast(BF16)
        key_i = hs_all[:, 5700:5700 + DW * HI].bitcast(I32)

        def acc_to(c):
            return ps_s[0:NP, c % 2, GE // 2:GE // 2 + JC * C]

        lr_keep = ring[0:NP, offs["oht"]:offs["oht"] + 2 * JC * C].rearrange("p (b j c) -> p b j c", b=2, j=JC)
        xr_rest = ring[0:NP, offs["oht"] + 2 * JC * C:offs["oht"] + 4 * JC * C].rearrange("p (b j c) -> p b j c", b=2, j=JC)
        xr_parts = ring[0:NP, offs["oh"]:offs["oh"] + 3 * JC * C].bitcast(BF16).rearrange(
            "p (b j k c) -> p b j k c", b=2, j=JC, k=3)
        squares1 = ring[0:NP, offs["msg"]:offs["msg"] + 2 * JP * C].rearrange("p (b j c) -> p b j c", b=2, c=C)
        y = ring[0:NP, 0:NJ * C]
        y3 = y.rearrange("p (j c) -> p j c", c=C)
        rden = ring[0:NP, 6400:6400 + 2 * JE * H].rearrange("p (b j h) -> p b j h", b=2, j=JE)
        sq = ring[0:NP, 6656:6656 + 2 * JP * C].rearrange("p (b k) -> p b k", b=2)
        sq_sum = ring[0:NP, 9600:9600 + PARTS * C].rearrange("p (q c) -> p q c", c=C)

        xs3 = xs[:, :].rearrange("p (j c) -> p j c", c=C)
        hs3 = hs[:, :].rearrange("p (j c) -> p j c", c=C)
        acc0_n = arena[:, 0:N].rearrange("c (p j) -> c j p", j=NJ)
        acc1_n = acc1[:, 0:N].rearrange("c (p j) -> c j p", j=NJ)
        agg_n, xl_n, out_n = (t.rearrange("(p j) c -> p j c", j=NJ) for t in (agg_table, xl_table, out))
        xr_n = xr_table[0:N].rearrange("(p j) k c -> p j k c", j=NJ)

        dst_in, ends_in, dstt_in, x_in, w_in = sem("dst_in"), sem("ends_in"), sem("dstt_in"), sem("x_in"), sem("w_in")
        consts_set, consts_f = sem("consts_set"), sem("consts_f")
        v_step = sem("v_step")
        dstf_set, loc_set, start_set, flags_set = sem("dstf_set"), sem("loc_set"), sem("start_set"), sem("flags_set")
        loc_out, start_out, pad_out = sem("loc_out"), sem("start_out"), sem("pad_out")
        onehots_set, rows_ps, rows_set = sem("onehots_set"), sem("rows_ps"), sem("rows_set")
        found_in = [sem("found_in0"), sem("found_in1")]
        counted, deg_set, root_set, table_set, table_out = (
            sem("counted"), sem("deg_set"), sem("root_set"), sem("table_set"), sem("table_out"))
        var_set, std_set, h_set = sem("var_set"), sem("std_set"), sem("h_set")
        h_t, ht_set, lin_ps, lin_kept = sem("h_t"), sem("ht_set"), sem("lin_ps"), sem("lin_kept")
        idx_in = [[sem(f"idx{k}_in{s}") for s in range(SLOTS)] for k in range(2)]
        gathered = [[sem(f"gathered{k}_{s}") for s in range(SLOTS)] for k in range(2)]
        slot_free = sem("slot_free")
        oh_set = [sem("oh_set0"), sem("oh_set1")]
        summed = [sem("summed0"), sem("summed1")]
        lastsum_set, prior_set, joined_set, firsts_sb, firsts_set, acc_set = (
            [sem(f"{n}{k}") for k in range(2)] for n in
            ("lastsum_set", "prior_set", "joined_set", "firsts_sb", "firsts_set", "acc_set"))
        keep_set, drop_set = sem("keep_set"), sem("drop_set")
        xsum_set, stage_in, split_a, split_v, acc_zero = (
            sem("xsum_set"), sem("stage_in"), sem("split_a"), sem("split_v"), sem("acc_zero"))
        src_in, low_set, keys_set, hot_set, built, zeroed, zeroed_v, added, kept = (
            sem("src_in"), sem("low_set"), sem("keys_set"), sem("hot_set"), sem("built"), sem("zeroed"), sem("zeroed_v"), sem("added"), sem("kept"))
        dense_made, part_set, half_set, dsum_set, dsum_t, dense_set = (
            sem("dense_made"), sem("part_set"), sem("half_set"), sem("dsum_set"), sem("dsum_t"), sem("dense_set"))
        gather_done, dense_done, ones_row = sem("gather_done"), sem("dense_done"), sem("ones_row")
        acc_t, x1_set, cent1_set, sq1_set = sem("acc_t"), sem("x1_set"), sem("cent1_set"), sem("sq1_set")
        h1_t, h1t_set, lr_ps, parts_set, rest_set, xl_kept, xr_kept = (
            sem("h1_t"), sem("h1t_set"), sem("lr_ps"), sem("parts_set"), sem("rest_set"), sem("xl_kept"), sem("xr_kept"))
        xl_out, xr_out = [[sem(f"{k}_out{b}") for b in range(2)] for k in ("xl", "xr")]
        xrw_in = [sem(f"xrw_in{s}") for s in range(SLOTS)]
        edge_in = [sem(f"edge_in{s}") for s in range(SLOTS)]
        oht_set, g_made, row_set, leaky_set, prod_set, logits_set = (
            sem("oht_set"), sem("g_made"), sem("row_set"), sem("leaky_set"), sem("prod_set"), sem("logits_set"))
        lt_made, fwd_set, tails_set, tails_made, carry_set, runmax_set, before_set, beforex_set = (
            sem("lt_made"), sem("fwd_set"), sem("tails_set"), sem("tails_made"), sem("carry_set"),
            sem("runmax_set"), sem("before_set"), sem("beforex_set"))
        hist_made, hist_set, fwdh_set, segmax_set, diff_set, exp_set, ext_made, resc_set, msg_set = (
            sem("hist_made"), sem("hist_set"), sem("fwdh_set"), sem("segmax_set"), sem("diff_set"), sem("exp_set"),
            sem("ext_made"), sem("resc_set"), sem("msg_set"))
        num_t, y_set, sum_ps, cent_set, sq_set, sqsum_set, sqsum_ps, gelu_in, gelu_set, y_done, out_done = (
            sem("num_t"), sem("y_set"), sem("sum_ps"), sem("cent_set"), sem("sq_set"), sem("sqsum_set"),
            sem("sqsum_ps"), sem("gelu_in"), sem("gelu_set"), sem("y_done"), sem("out_done"))

        N_CONST = 14
        N_W = 10 + GT
        COUNTS = -(-(NJ + 1) // GT)

        def wait(eng, s, value):
            if not isinstance(value, int) or value > 0:
                eng.wait_ge(s, value)

        def each_body(eng, body):
            body(0)
            with eng.Fori(1, BODIES - 1) as i:
                body(i)
            body(BODIES - 1)

        def behind(i, s, lag):
            g = i * SLOTS + s - lag
            if isinstance(i, int) and not 0 <= g < GROUPS:
                return None
            return g, (s - lag) % SLOTS, i + (s - lag) // SLOTS

        def chunks_of(q):
            return range(q * JP // JC, (q + 1) * JP // JC) if 0 <= q < PARTS else ()

        def in_registers(engine, row, start, count, largest):
            return nc.values_load_multi_w_load_instructions(
                row[0:1, bass.ds(start, count)], engines=[engine], min_val=0, max_val=largest,
                skip_runtime_bounds_check_because="dst holds node numbers, and the flag bounds the rest")[1]

        def tile_bases(engine, g):
            return in_registers(engine, base_row, g * GT, GT, N)

        def either(eng, engine, fast, general):
            eng.wait_ge(flags_set, 1)
            allowed = nc.values_load_multi_w_load_instructions(
                flag_i[0:1, 0:1], engines=[engine], min_val=0, max_val=1,
                skip_runtime_bounds_check_because="the flag is 0 or 1")[1][0]
            with eng.If(allowed == 1):
                fast()
            with eng.Else():
                general()

        def fast_bodies(eng, body):
            body(0)
            with eng.Fori(1, FAST - 1) as i:
                body(i)
            body(FAST - 1)

        def before_group(i, s):
            return None if isinstance(i, int) and i * FG + s == 0 else i * FG + s - 1

        def rounds(i, s):
            return i * (FG // SLOTS0) + s // SLOTS0 + 1

        block = ctx.enter_context(nc.Block())

        @block.sync
        def _(sp):
            sp.dma_start(blocks(dst_i), dst_rows.rearrange("(b p) e -> p b e", p=T)).then_inc(dst_in, 16)
            sp.dma_start(xs[:, :], x.rearrange("(p j) c -> p (j c)", j=NJ)).then_inc(x_in, 16)
            sp.dma_start(dst_t, dst_cols).then_inc(dstt_in, 16)
            sp.dma_start(first_all, first_dst.partition_broadcast(T)).then_inc(ends_in, 16)
            sp.dma_start(last_all, last_dst.partition_broadcast(T)).then_inc(ends_in, 16)

            def layer0(i, slots=range(SLOTS)):
                for s in slots:
                    wait(sp, gathered[0][s], i * (16 * GT))
                    sp.dma_start(idx[:, s, :], src_cols[:, bass.ds((i * SLOTS + s) * GT, GT)]).then_inc(idx_in[0][s], 16)

            layer0(0, range(SLOTS0))
            sp.dma_start(src_d[:], src_cols[:, DENSE0:DENSE0 + K]).then_inc(src_in, 16)
            for q in range(PARTS):
                sp.wait_ge(table_set, q + 1)
                sp.dma_start(agg_n[:, q * JP:(q + 1) * JP, :], hs3[:, q * JP:(q + 1) * JP, :]).then_inc(table_out, 16)
            sp.wait_ge(loc_set, 1)
            sp.dma_start(loc_rows.rearrange("(b p) e -> p b e", p=T), blocks(loc_b)).then_inc(loc_out, 16)
            sp.wait_ge(start_set, 1)
            for h in range(H):
                sp.dma_start(start_rows[:, h, :].rearrange("(b p) e -> p b e", p=T), blocks(start_b)).then_inc(start_out, 16)
            sp.wait_ge(xsum_set, 1)
            sp.dma_start(stage[:, 0:HI - 1, :], agg_table[0:(HI - 1) * T, :].rearrange("(h l) c -> l h c", l=T)).then_inc(stage_in, 16)
            sp.dma_start(stage[0:N - (HI - 1) * T, HI - 1, :], agg_table[(HI - 1) * T:N, :]).then_inc(stage_in, 16)

            def fast0(i):
                first, last = (isinstance(i, int) and i == at for at in (0, FAST - 1))
                for s in range(SLOTS0 if first else 0, FG):
                    slot = s % SLOTS0
                    wait(sp, gathered[0][slot], (rounds(i, s) - 1) * (16 * GT))
                    sp.dma_start(idx[:, slot, :], src_cols[:, bass.ds((i * FG + s) * GT, GT)]).then_inc(idx_in[0][slot], 16)
                    if s == SLOTS0 and not last:
                        sp.wait_ge(keys_set, i + 1)
                        sp.dma_start(src_d[:], src_cols[:, bass.ds(DENSE0 + (i + 1) * K, K)]).then_inc(src_in, 16)

            def general0():
                layer0(0, range(SLOTS0, SLOTS))
                with sp.Fori(1, BODIES - 1) as i:
                    layer0(i)
                layer0(BODIES - 1)

            either(sp, ENG.SP, lambda: fast_bodies(sp, fast0), general0)

            sp.wait_ge(gather_done, 1)
            for s in range(SLOTS):
                sp.dma_start(idx[:, s, :], src_cols[:, s * GT:(s + 1) * GT]).then_inc(idx_in[1][s], 16)
            for c in range(CHUNKS):
                sp.wait_ge(xl_kept, c + 1)
                sp.dma_start(xl_n[:, c * JC:(c + 1) * JC, :], lr_keep[:, c % 2]).then_inc(xl_out[c % 2], 16)
                sp.wait_ge(xr_kept, c + 1)
                sp.dma_start(xr_n[:, c * JC:(c + 1) * JC], xr_parts[:, c % 2]).then_inc(xr_out[c % 2], 16)
            sp.wait_ge(pad_out, 16)
            sp.wait_ge(loc_out, 16)
            sp.wait_ge(start_out, 16 * H)
            for b in range(2):
                sp.wait_ge(xr_out[b], 16 * len(range(b, CHUNKS, 2)))

            def layer1(i):
                for s in range(SLOTS):
                    g = i * SLOTS + s
                    if not (isinstance(i, int) and i == 0):
                        sp.wait_ge(gathered[1][s], i * (16 * GT))
                        sp.dma_start(idx[:, s, :], src_cols[:, bass.ds(g * GT, GT)]).then_inc(idx_in[1][s], 16)
                    bases = tile_bases(ENG.SP, g)
                    wait(sp, g_made, g - SLOTS + 1)
                    wait(sp, segmax_set, g - SLOTS + 1)
                    sp.dma_start(eat[:, s, :], edge_rows[bass.ds(g * T, T), :]).then_inc(edge_in[s], 16)
                    sp.dma_start(locr[:, s, :], loc_rows[bass.ds(g * GT, GT), :].rearrange(
                        "t e -> (t e)").partition_broadcast(T)).then_inc(edge_in[s], 16)
                    sp.dma_start(start[0:GT * H, s, 0:T], start_rows[bass.ds(g * GT, GT), :, :].rearrange(
                        "t h e -> (t h) e")).then_inc(edge_in[s], 16)
                    for t in range(GT):
                        sp.dma_start(xrw[:, s, t], xr_table[bass.ds(bases[t], T)]).then_inc(xrw_in[s], 16)

            each_body(sp, layer1)

            for q in range(PARTS):
                sp.wait_ge(y_done, q + 1)
                at = slice(q * JP, (q + 1) * JP)
                sp.dma_start(out_n[:, at, :], hs3[:, at, :]).then_inc(out_done, 16)
            sp.wait_ge(out_done, 16 * PARTS)

        @block.gpsimd
        def _(pool):
            g = nc.gpsimd
            g.iota(iota_i[:], [[1, T]], base=0, channel_multiplier=0).then_inc(consts_set, 1)
            g.iota(part_i[:], [[1, 1]], base=0, channel_multiplier=1).then_inc(consts_set, 1)
            g.iota(node_i[:], [[1, NJ + 1]], base=0, channel_multiplier=NJ).then_inc(consts_set, 1)
            g.iota(hund_i[:], [[NJ, NP + 1]], base=0, channel_multiplier=0).then_inc(consts_set, 1)
            g.iota(chan_i[:, 0:C], [[1, H], [0, HC]], base=0, channel_multiplier=0).then_inc(consts_set, 1)
            g.iota(chan_i[:, C:CD], [[1, H]], base=0, channel_multiplier=0).then_inc(consts_set, 1)
            g.memset(ones[:], 1.0).then_inc(consts_set, 1)
            g.memset(ones_b[:], 1.0).then_inc(consts_set, 1)
            g.memset(eps_ln[:], LN_EPS).then_inc(consts_set, 1)
            g.memset(eps_bn[:], BN_EPS).then_inc(consts_set, 1)
            g.memset(zeros, 0.0).then_inc(consts_set, 1)
            g.memset(web[:], 0.0).then_inc(consts_set, 1)
            g.iota(key_i[:], [[1, DW * HI]], base=0, channel_multiplier=0).then_inc(consts_set, 1)
            g.memset(zero1[:], 0.0).then_inc(consts_set, 1)

            pool.wait_ge(rows_set, 1)
            for k in range(COUNTS):
                wait(pool, counted, k - 1)
                for t in range(min(GT, NJ + 1 - k * GT)):
                    j = k * GT + t
                    g.indirect_dma_start(out=found[:, k % 2, t, :], out_offset=None, in_=dst_rows,
                                         in_offset=bass.IndirectOffsetOnAxis(ap=rowidx[:, j:j + 1], axis=0)
                                         ).then_inc(found_in[k % 2], 16)

            def gather(layer, n, s, rnd, table, ready, used, slots=SLOTS):
                wait(pool, used, n - slots + 1)
                pool.wait_ge(idx_in[layer][s], 16 * rnd)
                pool.wait_ge(*ready)
                pool.sem_inc(slot_free, 1)
                for t in range(GT):
                    g.indirect_dma_start(out=gbuf[:, s, t, :], out_offset=None, in_=table,
                                         in_offset=bass.IndirectOffsetOnAxis(ap=idx[:, s, t:t + 1], axis=0)
                                         ).then_inc(gathered[layer][s], 16)

            def gather0(n, s, rnd, slots):
                gather(0, n, s, rnd, agg_table, (table_out, 16 * PARTS), summed[0], slots)

            pool.wait_ge(counted, COUNTS)
            either(pool, ENG.Pool,
                   lambda: fast_bodies(pool, lambda i: [gather0(i * FG + s, s % SLOTS0, rounds(i, s), SLOTS0) for s in range(FG)]),
                   lambda: each_body(pool, lambda i: [gather0(i * SLOTS + s, s, i + 1, SLOTS) for s in range(SLOTS)]))
            for b in range(2):
                pool.wait_ge(xl_out[b], 16 * len(range(b, CHUNKS, 2)))
            each_body(pool, lambda i: [gather(1, i * SLOTS + s, s, i + 1, xl_table, (xl_out[0], 16 * len(range(0, CHUNKS, 2))),
                                              msg_set) for s in range(SLOTS)])

        @block.vector
        def _(dve):
            v = nc.vector
            steps = [0]

            def link(ins):
                steps[0] += 1
                ins.then_inc(v_step, 1)
                dve.wait_ge(v_step, steps[0])

            dve.wait_ge(consts_set, N_CONST)
            v.tensor_copy(iota_f[:], iota_i[:])
            v.tensor_copy(iota_b[:], iota_i[:])
            v.tensor_copy(iota_k[:], key_i[:])
            v.tensor_copy(part_f[:], part_i[:])
            v.tensor_copy(node_f[:], node_i[:])
            v.tensor_copy(hund_f[:], hund_i[:])
            v.tensor_copy(chan_f[:], chan_i[:])
            v.tensor_scalar(head_i[:], part_i[0:GT * H, :], H - 1, None, ALU.bitwise_and)
            link(v.tensor_scalar(tile_i[:], part_i[0:GT * H, :], H.bit_length() - 1, None, ALU.arith_shift_right))
            v.tensor_copy(head_f[:], head_i[:])
            link(v.tensor_copy(tile_f[:], tile_i[:]))
            link(v.tensor_scalar(ident[:], iota_f[:], part_f[:, 0:1], None, ALU.is_equal))
            v.tensor_tensor(ident2[:], ident[:, 0:C], ident[:, C:2 * C], ALU.add)
            v.tensor_scalar(by_tile[:], iota_f[0:GT * H, 0:GT], tile_f[:, 0:1], None, ALU.is_equal)
            v.tensor_scalar(by_head[:], iota_f[0:GT * H, 0:H], head_f[:, 0:1], None, ALU.is_equal)
            v.tensor_scalar(by_chan[:], chan_f[:], head_f[:, 0:1], None, ALU.is_equal)
            v.memset(lastsum[:], 0.0)
            v.memset(firsts[:], 0.0)
            v.memset(runmax[:], -BIG).then_inc(consts_f, 1)

            dve.wait_ge(dst_in, 16)
            v.tensor_copy(dst_f, dst_i).then_inc(dstf_set, 1)
            dve.wait_ge(dstf_set, 1)
            base = blocks(dst_f)[:, :, 0]
            base_q = base.unsqueeze(2).to_broadcast([T, BLK, NP + 1])
            hund = hund_f[:].unsqueeze(1).to_broadcast([T, BLK, NP + 1])
            link(v.tensor_tensor(ge_b, base_q, hund, ALU.is_ge))
            link(v.tensor_reduce(pa[:], ge_b[:, :, 1:NP + 1], AX.X, ALU.add))
            v.tensor_tensor(in_b, ge_b[:, :, 0:NP], ge_b[:, :, 1:NP + 1], ALU.subtract)
            link(v.scalar_tensor_tensor(jb[:], pa[:], -float(NJ), base, ALU.mult, ALU.add))
            v.tensor_tensor(jlt, jb[:].unsqueeze(2).to_broadcast([T, BLK, NJ + 1]),
                            iota_f[:, 0:NJ + 1].unsqueeze(1).to_broadcast([T, BLK, NJ + 1]), ALU.is_lt)
            v.tensor_tensor(ge_b, base_q, hund, ALU.is_lt).then_inc(onehots_set, 1)
            dve.wait_ge(rows_ps, 1)
            link(v.tensor_scalar(rowblk[:], ps_g[0:NP, 0, 0:NJ + 1], -1.0, 0.0, ALU.add, ALU.max))
            v.tensor_copy(rowidx[:], rowblk[:]).then_inc(rows_set, 1)

            def count(k):
                n = min(GT, NJ + 1 - k * GT)
                at = slice(k * GT, k * GT + n)
                dve.wait_ge(found_in[k % 2], sum(16 * min(GT, NJ + 1 - r * GT) for r in range(k % 2, k + 1, 2)))
                wait(dve, counted, k)
                link(v.tensor_tensor(less[:, 0:n, :], found[:, k % 2, 0:n, :],
                                     node_f[:, at].unsqueeze(2).to_broadcast([NP, n, T]), ALU.is_lt))
                v.tensor_reduce(below[:, at], less[:, 0:n, :], AX.X, ALU.add).then_inc(counted, 1)

            dve.wait_ge(x_in, 16)
            dve.wait_ge(w_in, 16 * N_W)
            dve.wait_ge(pad_out, 16)
            link(v.tensor_reduce(mean[:], xs3, AX.X, ALU.add))
            link(v.tensor_scalar(mean[:], mean[:], 1.0 / C, None, ALU.mult))
            link(v.tensor_tensor(hs3, xs3, mean[:].unsqueeze(2).to_broadcast([NP, NJ, C]), ALU.subtract))
            for q in range(4):
                at = slice(q * NJ // 4, (q + 1) * NJ // 4)
                if q % 2 == 0:
                    count(q // 2)
                link(v.tensor_tensor(squares, hs3[:, at, :], hs3[:, at, :], ALU.mult))
                link(v.tensor_reduce(rstd[:, at], squares, AX.X, ALU.add))
            v.tensor_scalar(rstd[:], rstd[:], 1.0 / C, None, ALU.mult).then_inc(var_set, 1)
            count(2)
            dve.wait_ge(std_set, 1)
            link(v.reciprocal(rstd[:], rstd[:]))
            v.scalar_tensor_tensor(hs3, hs3, 0.0, rstd[:].unsqueeze(2).to_broadcast([NP, NJ, C]),
                                   ALU.max, ALU.mult).then_inc(h_set, 1)
            count(3)
            dve.wait_ge(dstt_in, 16)
            dve.wait_ge(ends_in, 32)
            v.tensor_tensor(loc[:], dst_t, first_all, ALU.subtract)
            v.tensor_tensor(lastm[:], dst_t, last_all, ALU.is_equal)
            count(4)
            v.tensor_copy(base_row, first_all[C:C + 1, :])
            v.tensor_tensor(blocks(loc_b), blocks(dst_f), base.unsqueeze(2).to_broadcast([T, BLK, T]),
                            ALU.subtract).then_inc(loc_set, 1)
            v.memset(blocks(start_b)[:, :, 0:1], 0.0)
            link(v.tensor_tensor(blocks(start_b)[:, :, 1:T], blocks(dst_f)[:, :, 1:T], blocks(dst_f)[:, :, 0:T - 1],
                                 ALU.not_equal))
            count(5)
            v.tensor_scalar(start_b, start_b, -BIG, None, ALU.mult).then_inc(start_set, 1)
            v.memset(open_[:, 0:1], 0.0)
            v.memset(alone[:, 0:1], 0.0)
            link(v.tensor_tensor(open_[:, 1:TILES], first_all[0:CD, 1:TILES], last_all[0:CD, 0:TILES - 1], ALU.is_equal))
            count(6)
            link(v.tensor_tensor(equal_all, last_all[0:CD, :], first_all[0:CD, :], ALU.subtract))
            supers = first_all[:, DENSE0:DENSE0 + DENSE].rearrange("p (b k) -> p b k", k=K)
            v.tensor_reduce(flag[:, 0:1], equal_all[0:1, DENSE0:DENSE0 + DENSE], AX.X, ALU.max)
            v.tensor_reduce(flag[:, 1:2], equal_all[0:1, DENSE0:REAL - 1], AX.X, ALU.min)
            link(v.tensor_tensor(mean[0:1, 0:FAST], supers[0:1, :, K - 1], supers[0:1, :, 0], ALU.subtract))
            link(v.tensor_reduce(flag[:, 2:3], mean[0:1, 0:FAST], AX.X, ALU.max))
            count(7)
            v.tensor_scalar(flag[:, 0:1], flag[:, 0:1], float(DW - 1), None, ALU.is_le)
            v.tensor_scalar(flag[:, 1:2], flag[:, 1:2], 1.0, None, ALU.is_ge)
            link(v.tensor_scalar(flag[:, 2:3], flag[:, 2:3], float(T - DW), None, ALU.is_le))
            link(v.tensor_reduce(flag[:, 3:4], flag[:, 0:3], AX.X, ALU.min))
            v.tensor_copy(flag_i[:], flag[:, 3:4])
            link(v.scalar_tensor_tensor(alone[:, 1:TILES], equal_all[:, 0:TILES - 1], 0.0, open_[:, 1:TILES],
                                        ALU.is_equal, ALU.mult))
            link(v.tensor_tensor(open_[:], open_[:], alone[:], ALU.subtract))
            link(v.tensor_scalar(wide[:], equal_all, float(T - 1), None, ALU.is_equal))
            count(8)
            place_f = equal_all[GT * H:GT * H + 1, 0:DENSE]
            link(v.tensor_tensor(place_f.rearrange("p (b k) -> p b k", k=K), supers[GT * H:GT * H + 1],
                                 supers[GT * H:GT * H + 1, :, 0:1].to_broadcast([1, FAST, K]), ALU.subtract))
            v.tensor_scalar(place_row[:, 0:DENSE], place_f, float(HI), None, ALU.mult)
            link(v.tensor_scalar(equal_all[0:H, :], equal_all[0:H, :], 0.0, None, ALU.is_equal))
            link(v.tensor_tensor(chain, open_[0:H, :], alone[0:H, :], ALU.add))
            link(v.tensor_tensor(chain, chain, equal_all[0:H, :], ALU.mult))
            v.tensor_scalar(chain, chain, 2 * BIG, -BIG, ALU.mult, ALU.add).then_inc(flags_set, 1)
            for k in range(9, COUNTS):
                count(k)

            dve.wait_ge(counted, COUNTS)
            link(v.scalar_tensor_tensor(below[:], rowblk[:], float(T), below[:], ALU.mult, ALU.add))
            v.tensor_tensor(dinv[:], below[:, 1:NJ + 1], below[:, 0:NJ], ALU.subtract).then_inc(deg_set, 1)
            dve.wait_ge(root_set, 1)
            link(v.reciprocal(dinv[:], dinv[:]))
            dve.wait_ge(lin_kept, CHUNKS)
            for q in range(PARTS):
                at = slice(q * JP, (q + 1) * JP)
                v.tensor_tensor(hs3[:, at, :], hs3[:, at, :], dinv[:, at].unsqueeze(2).to_broadcast([NP, JP, C]),
                                ALU.mult).then_inc(table_set, 1)
            link(v.tensor_tensor(xs3, xs3, b0_s[:].unsqueeze(1).to_broadcast([NP, NJ, C]), ALU.add))
            dve.wait_ge(table_out, 16 * PARTS)
            link(v.tensor_tensor(hs3, hs3, dinv[:].unsqueeze(2).to_broadcast([NP, NJ, C]), ALU.mult))
            link(v.tensor_tensor(xs3, xs3, hs3, ALU.add))
            v.memset(stage[:, HI - 1, :], 0.0).then_inc(xsum_set, 1)
            dve.wait_ge(flags_set, 1)
            dve.wait_ge(loc_out, 16)
            dve.wait_ge(start_out, 16 * H)

            def onehot(layer, g, b, start=0, size=GT):
                if start == 0:
                    wait(dve, summed[layer], g - 1)
                at, tiles = bass.ds(g * GT + start, size), slice(start, start + size)
                v.tensor_tensor(oh[:, b, tiles, 0:T - 1], loc[:, at].unsqueeze(2).to_broadcast([T, size, T - 1]),
                                iota_b[:, 0:T - 1].unsqueeze(1).to_broadcast([T, size, T - 1]), ALU.is_equal)
                last = v.tensor_copy(oh[:, b, tiles, T - 1], lastm[:, at])
                if start + size == GT:
                    last.then_inc(oh_set[layer], 1)

            def windows(b, rows):
                return ps_s[0:rows, b, :].rearrange("p (t n) -> p t n", n=T)

            def carry_lasts(layer, w, b, rows):
                dve.wait_ge(summed[layer], w + 1)
                v.tensor_copy(lastsum[0:rows, b, 1:GT + 1], windows(b, rows)[:, :, T - 1])
                v.tensor_copy(lastsum[0:rows, b, 0:1], lastsum[0:rows, 1 - b, GT:GT + 1]).then_inc(lastsum_set[layer], 1)

            def carry_wide(layer, w, b, rows):
                dve.wait_ge(lastsum_set[layer], w + 1)
                v.tensor_tensor(windows(b, rows)[:, :, T - 1], windows(b, rows)[:, :, T - 1], wide[0:rows, bass.ds(w * GT, GT)],
                                ALU.mult).then_inc(firsts_set[layer], 1)

            def keeps(layer, w, b, rows, which):
                return (alone, open_)[which][0:rows, bass.ds(w * GT, GT)] if layer == 0 else keep[:, b, which, :]

            def carry_drop(layer, w, b, rows):
                if layer == 1:
                    dve.wait_ge(drop_set, w + 1)
                dve.wait_ge(lastsum_set[layer], w + 1)
                v.tensor_tensor(joined[0:rows, :], keeps(layer, w, b, rows, 1), lastsum[0:rows, b, 0:GT],
                                ALU.mult).then_inc(prior_set[layer], 1)

            def carry_own(layer, w, b, rows):
                dve.wait_ge(prior_set[layer], w + 1)
                v.tensor_tensor(joined[0:rows, :], joined[0:rows, :], windows(b, rows)[:, :, 0], ALU.add).then_inc(joined_set[layer], 1)

            def carry_scan(layer, w, b, rows):
                dve.wait_ge(joined_set[layer], w + 1)
                wait(dve, firsts_sb[layer], w)
                v.tensor_tensor_scan(firsts[0:rows, b, :], keeps(layer, w, b, rows, 0), joined[0:rows, :],
                                     firsts[0:rows, 1 - b, GT - 1:GT], ALU.mult, ALU.add).then_inc(firsts_sb[layer], 1)

            def carry_firsts(layer, w, b, rows):
                dve.wait_ge(firsts_sb[layer], w + 1)
                v.tensor_copy(windows(b, rows)[:, :, 0], firsts[0:rows, b, :]).then_inc(firsts_set[layer], 1)

            def carry0(w, b):
                def step1():
                    carry_lasts(0, w, b, C)
                    carry_wide(0, w, b, C)
                    carry_drop(0, w, b, C)

                return [step1, lambda: carry_own(0, w, b, C), lambda: carry_scan(0, w, b, C),
                        lambda: carry_firsts(0, w, b, C)]

            def split_table():
                for h in range(2):
                    at = slice(h * HI // 2, (h + 1) * HI // 2)
                    dve.wait_ge(split_a, h + 1)
                    v.tensor_tensor(stage[:, at], stage[:, at], table3[:, at, 0, :], ALU.subtract).then_inc(split_v, 1)
                for h in range(2):
                    at = slice(h * HI // 2, (h + 1) * HI // 2)
                    dve.wait_ge(split_a, h + 3)
                    dve.wait_ge(split_v, h + 1)
                    v.tensor_tensor(table3[:, at, 2, :], stage[:, at], table3[:, at, 1, :], ALU.subtract).then_inc(split_v, 1)

            def keys(i):
                dve.wait_ge(src_in, 16 * (i + 1))
                v.tensor_scalar(lo_i[:], src_d[:], T - 1, None, ALU.bitwise_and).then_inc(low_set, 1)
                v.tensor_scalar(hi_i[:], src_d[:], T.bit_length() - 1, None, ALU.arith_shift_right).then_inc(low_set, 1)
                dve.wait_ge(low_set, 2 * i + 2)
                v.tensor_copy(lo_f[:], lo_i[:])
                v.scalar_tensor_tensor(key_f[:], loc[:, bass.ds(DENSE0 + i * K, K)], float(HI), hi_i[:],
                                       ALU.mult, ALU.add).then_inc(keys_set, 1)
                dve.wait_ge(keys_set, i + 1)

            def hot(i, k):
                wait(dve, built, i * K + k - (1 if k > 0 else 0))
                v.tensor_scalar(lo_hot[:, k % 2, :], iota_b[:], lo_f[:, k:k + 1], None, ALU.is_equal)
                v.tensor_scalar(key_hot[:, k % 2, :], iota_k[:], key_f[:, k:k + 1], None, ALU.is_equal).then_inc(hot_set, 1)

            half = counts_w[:, T * HI // 4:].bitcast(BF16)

            def add_first(i, k, place):
                to = counts[:, bass.ds(place, HI)]
                if k == 0:
                    dve.wait_ge(zeroed, i + 1)
                    dve.wait_ge(zeroed_v, i + 1)
                dve.wait_ge(built, i * K + k + 1)
                wait(dve, kept, i * K + k)
                wait(dve, added, i * K + k)
                v.tensor_tensor(to, to, built_to[k % 2][:, 0, 0:HI], ALU.add).then_inc(added, 1)

            def dense_rows(i):
                dve.wait_ge(part_set, i + 1)
                v.tensor_tensor(part3, dense_ps[:, 1, :], part3, ALU.add).then_inc(half_set, 1)
                dve.wait_ge(half_set, i + 1)
                wait(dve, dsum_t, i)
                v.tensor_tensor(dsum[:, C:2 * C], dense_ps[:, 0, :], part3, ALU.add).then_inc(dsum_set, 1)

            def dense_add(i):
                first = in_registers(ENG.DVE, base_row, DENSE0 + i * K, 1, N)[0]
                to = acc0b[:, bass.ds(first, T)]
                dve.wait_ge(acc_zero, 1)
                wait(dve, dense_set, i)
                dve.wait_ge(dsum_t, i + 1)
                v.tensor_tensor(to, to, dense_t[C:2 * C, :], ALU.add).then_inc(dense_set, 1)

            def clear(first=False):
                if first:
                    v.memset(half, 0.0).then_inc(zeroed_v, 1)
                else:
                    v.tensor_scalar(half, half, 0.0, None, ALU.mult).then_inc(zeroed_v, 1)

            def fast0(i):
                last = isinstance(i, int) and i == FAST - 1
                for s in range(FG):
                    piece = PIECES[s] if s < len(PIECES) else ()
                    if piece:
                        places = in_registers(ENG.DVE, place_row, i * K + piece[0], len(piece), (T - DW) * HI)
                    w = before_group(i, s)
                    steps = carry0(w, (s - 1) % 2) if w is not None else []
                    for r in range(max(6, len(piece))):
                        if r < len(steps):
                            steps[r]()
                        if r in (4, 5) and not (last and s == FG - 1):
                            onehot(0, i * FG + s + 1, (s + 1) % 2, (r - 4) * GT // 2, GT // 2)
                        if r < len(piece):
                            add_first(i, piece[r], places[r])
                            if piece[r] + 2 < K:
                                hot(i, piece[r] + 2)
                    if s == len(PIECES) and not last:
                        keys(i + 1)
                        hot(i + 1, 0)
                        hot(i + 1, 1)
                dense_rows(i)
                if not last:
                    clear()
                dense_add(i)

            def fast_loop():
                split_table()
                keys(0)
                onehot(0, 0, 0)
                dve.wait_ge(split_v, 4)
                clear(first=True)
                hot(0, 0)
                hot(0, 1)
                fast_bodies(dve, fast0)
                for step in carry0(FAST * FG - 1, 1):
                    step()
                dve.wait_ge(dense_set, FAST)
                dve.sem_inc(dense_done, 1)

            def layer0(i, s):
                n, w = behind(i, s, 0), behind(i, s, 1)
                if n is not None:
                    onehot(0, n[0], s % 2)
                if w is not None:
                    for step in carry0(w[0], w[1] % 2):
                        step()

            def general_loop():
                each_body(dve, lambda i: [layer0(i, s) for s in range(SLOTS)])
                layer0(BODIES, 0)
                dve.sem_inc(dense_done, 1)

            either(dve, ENG.DVE, fast_loop, general_loop)
            dve.wait_ge(gather_done, 1)
            v.memset(h_turn[C:C + 1], 1.0).then_inc(ones_row, 1)

            def add_sums(q):
                for c in chunks_of(q):
                    dve.wait_ge(acc_t, c + 1)
                    for k in range(JC):
                        j = c * JC + k
                        last = v.scalar_tensor_tensor(xs3[:, j, :], acc_to(c)[:, k * C:(k + 1) * C], dinv[:, j:j + 1],
                                                      xs3[:, j, :], ALU.mult, ALU.add)
                    last.then_inc(x1_set, 1)

            def centre(q):
                at = slice(q * JP, (q + 1) * JP)
                dve.wait_ge(x1_set, (q + 1) * JP // JC)
                link(v.tensor_reduce(mean[:, at], xs3[:, at, :], AX.X, ALU.add))
                link(v.tensor_scalar(mean[:, at], mean[:, at], 1.0 / C, None, ALU.mult))
                v.tensor_tensor(hs3[:, at, :], xs3[:, at, :], mean[:, at].unsqueeze(2).to_broadcast([NP, JP, C]),
                                ALU.subtract).then_inc(cent1_set, 1)

            def variance(q):
                at = slice(q * JP, (q + 1) * JP)
                dve.wait_ge(sq1_set, q + 1)
                link(v.tensor_reduce(rstd[:, at], squares1[:, q % 2], AX.X, ALU.add))
                v.tensor_scalar(rstd[:, at], rstd[:, at], 1.0 / C, None, ALU.mult).then_inc(var_set, 1)

            def normed(q):
                at = slice(q * JP, (q + 1) * JP)
                dve.wait_ge(std_set, q + 2)
                link(v.reciprocal(rstd[:, at], rstd[:, at]))
                dve.wait_ge(cent1_set, q + 1)
                v.scalar_tensor_tensor(hs3[:, at, :], hs3[:, at, :], 0.0, rstd[:, at].unsqueeze(2).to_broadcast([NP, JP, C]),
                                       ALU.max, ALU.mult).then_inc(h_set, 1)

            def split_xr(c):
                b = c % 2
                xr_ps = ps_g[0:NP, b, :].rearrange("p (j k) -> p j k", j=JC)[:, :, C:2 * C]
                dve.wait_ge(parts_set, 3 * c + 2)
                v.tensor_tensor(xr_rest[:, b], xr_ps, xr_parts[:, b, :, 0, :], ALU.subtract).then_inc(rest_set, 1)
                dve.wait_ge(parts_set, 3 * c + 3)
                dve.wait_ge(rest_set, c + 1)
                v.tensor_tensor(xr_parts[:, b, :, 2, :], xr_rest[:, b], xr_parts[:, b, :, 1, :],
                                ALU.subtract).then_inc(xr_kept, 1)

            for q in range(PARTS + 2):
                if q < PARTS:
                    add_sums(q)
                    centre(q)
                if 1 <= q <= PARTS:
                    variance(q - 1)
                    normed(q - 1)
                for c in chunks_of(q - 2):
                    if c > 0:
                        split_xr(c - 1)
            split_xr(CHUNKS - 1)

            def one_hot_t(n, s, rnd):
                dve.wait_ge(edge_in[s], 48 * (rnd + 1))
                wait(dve, g_made, n - 1)
                v.tensor_scalar(oht[:, s % 2, :], locr[:, s, :], part_f[:, 0:1], None, ALU.is_equal).then_inc(oht_set, 1)

            link(v.tensor_tensor(cont, cont, alone[0:H, :], ALU.add))
            link(v.tensor_scalar(cont, cont, 2 * BIG, -BIG, ALU.mult, ALU.add))
            v.memset(start[:, :, T:T + 1], 0.0).then_inc(consts_f, 1)
            dve.wait_ge(consts_f, 2)
            one_hot_t(0, 0, 0)

            def layer1(i, s):
                n, y, z, w, ahead = (behind(i, s, lag) for lag in (0, 1, 2, 3, -1))
                if z is not None:
                    z, zs, zr = z
                    zb = zs % 2
                    dve.wait_ge(exp_set, z + 1)
                    v.tensor_scalar(resc[:], by_tile[:], expt[:, T:T + 1], None, ALU.mult).then_inc(resc_set, 1)
                if y is not None:
                    y, ys, yr = y
                    onehot(1, y, ys % 2)
                    dve.wait_ge(edge_in[ys], 48 * (yr + 1))
                    dve.wait_ge(lt_made, y + 1)
                    v.tensor_tensor_scan(fwd[:], start[0:GT * H, ys, 0:T], lt_ps, -BIG, ALU.add, ALU.max).then_inc(fwd_set, 1)
                if w is not None:
                    w, wb = w[0], w[1] % 2
                    carry_lasts(1, w, wb, CD)
                if y is not None:
                    dve.wait_ge(fwd_set, y + 1)
                    v.tensor_scalar(tails[:], by_tile[:], fwd[:, T - 1:T], None, ALU.mult).then_inc(tails_set, 1)
                if w is not None:
                    carry_wide(1, w, wb, CD)
                    carry_drop(1, w, wb, CD)
                if z is not None:
                    at = bass.ds(z * GT, GT)
                    dve.wait_ge(ext_made, 2 * z + 2)
                    wait(dve, summed[1], z - 1)
                    v.tensor_tensor(keep[:, zb, 0, :], resc_ps, alone[:, at], ALU.mult).then_inc(keep_set, 1)
                    w8 = ext_ps.rearrange("p (t h) -> p t h", t=GT)
                    v.tensor_copy(msg[:, zb, :, C:CD], w8)
                    dve.wait_ge(keep_set, z + 1)
                    v.tensor_tensor(keep[:, zb, 1, :], resc_ps, keep[:, zb, 0, :], ALU.subtract).then_inc(drop_set, 1)
                    v.tensor_tensor(msg[:, zb, :, 0:C].rearrange("p t (h c) -> p t h c", h=H),
                                    gbuf[:, zs].rearrange("p t (h c) -> p t h c", h=H),
                                    w8.unsqueeze(3).to_broadcast([T, GT, H, HC]), ALU.mult).then_inc(msg_set, 1)
                if w is not None:
                    carry_own(1, w, wb, CD)
                if y is not None:
                    wait(dve, before_set, y)
                    v.tensor_copy(runmax[:, 0:1], runmax[:, GT:GT + 1]).then_inc(carry_set, 1)
                if w is not None:
                    carry_scan(1, w, wb, CD)
                if y is not None:
                    dve.wait_ge(carry_set, y + 1)
                    dve.wait_ge(tails_made, y + 1)
                    v.tensor_tensor_scan(runmax[:, 1:GT + 1], chain[:, bass.ds(y * GT, GT)], tails_ps, runmax[:, 0:1],
                                         ALU.min, ALU.max).then_inc(runmax_set, 1)
                if w is not None:
                    carry_firsts(1, w, wb, CD)
                if y is not None:
                    dve.wait_ge(runmax_set, y + 1)
                    v.tensor_tensor(before[:], runmax[:, 0:GT], cont[:, bass.ds(y * GT, GT)], ALU.min).then_inc(before_set, 1)
                    dve.wait_ge(before_set, y + 1)
                    v.tensor_tensor(beforex[:].rearrange("k (t h) -> k t h", h=H), before[:].unsqueeze(2).to_broadcast([H, GT, H]),
                                    ident[0:H, 0:H].unsqueeze(1).to_broadcast([H, GT, H]), ALU.mult).then_inc(beforex_set, 1)
                if n is not None:
                    n = n[0]
                    dve.wait_ge(gathered[1][s], 16 * GT * (i + 1))
                    dve.wait_ge(g_made, n + 1)
                    v.tensor_tensor(lr, rows_to, gbuf[:, s].rearrange("p t c -> p (t c)"), ALU.add).then_inc(row_set, 1)
                if y is not None:
                    dve.wait_ge(hist_made, y + 1)
                    v.tensor_copy(hist[:], hist_ps).then_inc(hist_set, 1)
                if n is not None:
                    dve.wait_ge(row_set, n + 1)
                    v.scalar_tensor_tensor(lr, lr, SLOPE, lr, ALU.mult, ALU.max).then_inc(leaky_set, 1)
                if y is not None:
                    dve.wait_ge(hist_set, y + 1)
                    v.tensor_tensor_scan(fwd[:], start[0:GT * H, ys, 0:T], lt_ps, hist[:, 0:1], ALU.add, ALU.max).then_inc(fwdh_set, 1)
                if n is not None:
                    dve.wait_ge(leaky_set, n + 1)
                    v.tensor_tensor(lr.rearrange("p (t c) -> p t c", t=GT), lr.rearrange("p (t c) -> p t c", t=GT),
                                    att_s[:].unsqueeze(1).to_broadcast([T, GT, C]), ALU.mult).then_inc(prod_set, 1)
                if y is not None:
                    dve.wait_ge(fwdh_set, y + 1)
                    v.tensor_tensor_scan(segmax[:, ::-1], start[0:GT * H, ys, 1:T + 1][:, ::-1], fwd[:, ::-1], -BIG,
                                         ALU.add, ALU.max).then_inc(segmax_set, 1)
                if ahead is not None:
                    one_hot_t(*ahead)
                if y is not None:
                    dve.wait_ge(segmax_set, y + 1)
                    v.tensor_tensor(diff[:, T:T + 1], hist[:], segmax[:, 0:1], ALU.subtract)
                    v.tensor_tensor(diff[:, 0:T], lt_ps, segmax[:], ALU.subtract).then_inc(diff_set, 1)
                if n is not None:
                    dve.wait_ge(prod_set, n + 1)
                    v.tensor_reduce(lg[:], lr.rearrange("p (k c) -> p k c", c=HC), AX.X, ALU.add).then_inc(logits_set, 1)

            each_body(dve, lambda i: [layer1(i, s) for s in range(SLOTS)])
            for s in range(3):
                layer1(BODIES, s)

            def num(c):
                return ps_s[0:NP, c % 2, :].rearrange("p (k e) -> p k e", k=2)[:, :, 0:JE // 2 * CD].rearrange(
                    "p k (j d) -> p k j d", d=CD)

            def rden_of(c):
                return rden[:, c % 2].rearrange("p (k j) h -> p k j h", k=2)

            for c in range(ENDS):
                at = slice(c * JE, (c + 1) * JE)
                dve.wait_ge(num_t, c + 1)
                for k in range(2):
                    last = v.tensor_scalar(rden_of(c)[:, k], num(c)[:, k, :, C:CD], DEN_EPS, None, ALU.add)
                link(last)
                link(v.reciprocal(rden[:, c % 2], rden[:, c % 2]))
                for k in range(2):
                    part = slice(c * JE + k * JE // 2, c * JE + (k + 1) * JE // 2)
                    last = v.tensor_tensor(y3[:, part, :].rearrange("p j (h c) -> p j h c", h=H),
                                           num(c)[:, k, :, 0:C].rearrange("p j (h c) -> p j h c", h=H),
                                           rden_of(c)[:, k].unsqueeze(3).to_broadcast([NP, JE // 2, H, HC]), ALU.mult)
                link(last)
                v.tensor_tensor(y3[:, at, :], y3[:, at, :], bias_s[:].unsqueeze(1).to_broadcast([NP, JE, C]),
                                ALU.add).then_inc(y_set, 1)
            v.tensor_tensor(hs3, hs3, bet_s[:].unsqueeze(1).to_broadcast([NP, NJ, C]), ALU.add)
            dve.wait_ge(sum_ps, 2 * ENDS)
            link(v.tensor_reduce(stat[:, 0, :], ps_g[0:NP, 0, 0:JE // 2 * C].rearrange("p (j c) -> p c j", c=C), AX.X, ALU.add))
            link(v.tensor_scalar(stat[:, 0, :], stat[:, 0, :], 1.0 / N, None, ALU.mult))

            def sum_squares(q):
                dve.wait_ge(sq_set, q + 1)
                v.tensor_reduce(sq_sum[:, q, :], sq[:, q % 2, :].rearrange("p (j c) -> p c j", c=C), AX.X,
                                ALU.add).then_inc(sqsum_set, 1)

            for q in range(PARTS):
                at = slice(q * JP, (q + 1) * JP)
                v.tensor_tensor(y3[:, at, :], y3[:, at, :], stat[:, 0, :].unsqueeze(1).to_broadcast([NP, JP, C]),
                                ALU.subtract).then_inc(cent_set, 1)
                if q > 0:
                    sum_squares(q - 1)
            sum_squares(PARTS - 1)
            dve.wait_ge(sqsum_ps, 1)
            v.tensor_scalar(stat[:, 2, :], ps_g[0:NP, 1, 0:C], 1.0 / N, None, ALU.mult).then_inc(var_set, 1)
            dve.wait_ge(std_set, PARTS + 2)
            link(v.reciprocal(stat[:, 2, :], stat[:, 2, :]))
            link(v.tensor_tensor(stat[:, 2, :], stat[:, 2, :], gam_s[:], ALU.mult))

            def finish(q):
                at = slice(q * JP, (q + 1) * JP)
                dve.wait_ge(gelu_set, q + 1)
                v.tensor_tensor(hs3[:, at, :], y3[:, at, :], xs3[:, at, :], ALU.add).then_inc(y_done, 1)

            for q in range(PARTS):
                at = slice(q * JP, (q + 1) * JP)
                link(v.tensor_tensor(y3[:, at, :], y3[:, at, :], stat[:, 2, :].unsqueeze(1).to_broadcast([NP, JP, C]), ALU.mult))
                v.tensor_tensor(y3[:, at, :], y3[:, at, :], hs3[:, at, :], ALU.add).then_inc(gelu_in, 1)
                if q > 0:
                    finish(q - 1)
            finish(PARTS - 1)

        @block.scalar
        def _(act):
            a = nc.scalar
            act.dma_start(w0_s[:], w0).then_inc(w_in, 16)
            act.dma_start(wlr[0:C, 0:C], w_l).then_inc(w_in, 16)
            act.dma_start(wlr[0:C, C:2 * C], w_r).then_inc(w_in, 16)
            act.dma_start(wlr[C:C + 1, 0:C], b_l.unsqueeze(0)).then_inc(w_in, 16)
            act.dma_start(wlr[C:C + 1, C:2 * C], b_r.unsqueeze(0)).then_inc(w_in, 16)
            for to, vec in ((b0_s, b0), (bias_s, bias), (gam_s, gamma), (bet_s, beta)):
                act.dma_start(to[:], vec.partition_broadcast(NP)).then_inc(w_in, 16)
            act.dma_start(att_s[:], att.rearrange("h c -> (h c)").partition_broadcast(T)).then_inc(w_in, 16)
            act.wait_ge(consts_set, N_CONST)
            for t in range(GT):
                act.dma_start(web[t * ED:(t + 1) * ED, t * C:(t + 1) * C], w_e).then_inc(w_in, 16)
            act.dma_start(xr_table[N:NW], zeros).then_inc(pad_out, 16)

            act.wait_ge(var_set, 1)
            a.activation(rstd[:], rstd[:], ACT.Sqrt, bias=eps_ln[:, 0:1]).then_inc(std_set, 1)
            for c in range(CHUNKS):
                act.wait_ge(h_t, c + 1)
                wait(act, lin_ps, c - 1)
                a.activation(h_turn[0:C, c % 2].rearrange("p k q -> p (k q)"), ps_s[0:C, c % 2, 0:JC * NP],
                             ACT.Copy).then_inc(ht_set, 1)
                if c > 0:
                    act.wait_ge(lin_ps, c)
                    a.activation(hs[:, (c - 1) * JC * C:c * JC * C], ps_g[0:NP, (c - 1) % 2, 0:JC * C], ACT.Copy).then_inc(lin_kept, 1)
            act.wait_ge(lin_ps, CHUNKS)
            a.activation(hs[:, (CHUNKS - 1) * JC * C:], ps_g[0:NP, (CHUNKS - 1) % 2, 0:JC * C], ACT.Copy).then_inc(lin_kept, 1)
            act.wait_ge(deg_set, 1)
            a.activation(dinv[:], dinv[:], ACT.Sqrt, bias=ones[0:NP, 0:1]).then_inc(root_set, 1)

            def keep_sums(layer, w, b, rows, acc, tiles=range(GT), bases=None):
                if bases is None:
                    bases = tile_bases(ENG.Activation, w)
                act.wait_ge(firsts_set[layer], 2 * w + 2)
                for t in tiles:
                    wait(act, acc_set[layer], w * GT + t)
                    act.wait_ge(flags_set, 1)
                    a.activation(acc[:, bass.ds(bases[t], T)], ps_s[0:rows, b, t * T:(t + 1) * T],
                                 ACT.Copy).then_inc(acc_set[layer], 1)

            act.wait_ge(flags_set, 1)
            a.activation(arena[:, :], zero1[:, 0:1].to_broadcast([T, NW]), ACT.Copy).then_inc(acc_zero, 1)
            act.wait_ge(acc_zero, 1)

            def split_table():
                act.wait_ge(stage_in, 32)
                act.wait_ge(loc_out, 16)
                act.wait_ge(start_out, 16 * H)
                for k in range(2):
                    for h in range(2):
                        at = slice(h * HI // 2, (h + 1) * HI // 2)
                        wait(act, split_v, h + 1 if k == 1 else 0)
                        a.activation(table3[:, at, k, :], stage[:, at], ACT.Copy).then_inc(split_a, 1)

            def clear():
                a.activation(counts_w[:, 0:T * HI // 4], zero1[:, 0:1].to_broadcast([T, T * HI // 4]), ACT.Copy).then_inc(zeroed, 1)

            def keep_counts(i, k, place):
                if k == 0:
                    act.wait_ge(zeroed, i + 1)
                    act.wait_ge(zeroed_v, i + 1)
                wait(act, kept, i * K + k)
                act.wait_ge(built, i * K + k + 1)
                act.wait_ge(flags_set, 1)
                a.activation(counts[:, bass.ds(place + HI, (DW - 1) * HI)], built_to[k % 2][:, 1, 0:(DW - 1) * HI],
                             ACT.Copy).then_inc(kept, 1)

            def dense_part(i):
                act.wait_ge(dense_made, i + 1)
                wait(act, dsum_t, i)
                a.activation(part3, dense_ps[:, 2, :], ACT.Copy).then_inc(part_set, 1)

            def fast0(i):
                last = isinstance(i, int) and i == FAST - 1
                for s in range(FG):
                    w = before_group(i, s)
                    piece = PIECES[s] if s < len(PIECES) else ()
                    if piece:
                        places = in_registers(ENG.Activation, place_row, i * K + piece[0], len(piece), (T - DW) * HI)
                    none_left = s == 0 or s > COUNTED or (isinstance(w, int) and w == 0)
                    late = 0 if none_left else LATE
                    turn = []
                    if w is not None:
                        turn += [(w - 1, s % 2, t) for t in range(GT - late, GT)]
                        turn += [(w, (s - 1) % 2, t) for t in range(GT if s >= COUNTED else GT - LATE)]
                        bases = in_registers(ENG.Activation, base_row, w * GT - late, len(turn), N)
                    for r in range(max(len(piece), late, len(turn) - late + 3)):
                        if r < len(piece):
                            keep_counts(i, piece[r], places[r])
                        at = r if r < late else r - 3 + late
                        if (r < late or r >= 3) and at < len(turn):
                            g, b, t = turn[at]
                            keep_sums(0, g, b, C, acc0, [t], {t: bases[at]})
                dense_part(i)
                if not last:
                    clear()

            def fast_loop():
                split_table()
                act.wait_ge(split_v, 4)
                clear()
                fast_bodies(act, fast0)
                keep_sums(0, FAST * FG - 1, 1, C, acc0)
                act.wait_ge(acc_set[0], FAST * FG * GT)
                act.sem_inc(gather_done, 1)

            def layer0(i, s):
                w = behind(i, s, 1)
                if w is not None:
                    keep_sums(0, w[0], w[1] % 2, C, acc0)

            def general_loop():
                each_body(act, lambda i: [layer0(i, s) for s in range(SLOTS)])
                layer0(BODIES, 0)
                act.wait_ge(acc_set[0], GROUPS * GT)
                act.wait_ge(stage_in, 32)
                act.sem_inc(gather_done, 1)

            either(act, ENG.Activation, fast_loop, general_loop)

            def square(q):
                act.wait_ge(cent1_set, q + 1)
                wait(act, var_set, q)
                a.activation(squares1[:, q % 2].rearrange("p j c -> p (j c)"), hs[:, q * JP * C:(q + 1) * JP * C],
                             ACT.Square).then_inc(sq1_set, 1)

            def root(q):
                at = slice(q * JP, (q + 1) * JP)
                act.wait_ge(var_set, q + 2)
                a.activation(rstd[:, at], rstd[:, at], ACT.Sqrt, bias=eps_ln[:, 0:1]).then_inc(std_set, 1)

            def turned(c):
                act.wait_ge(h1_t, c + 1)
                wait(act, lr_ps, c - 1)
                a.activation(h_turn[0:C, c % 2].rearrange("p k q -> p (k q)"), ps_s[0:C, c % 2, 0:JC * NP],
                             ACT.Copy).then_inc(h1t_set, 1)

            def split(c):
                b = c % 2
                rows = ps_g[0:NP, b, :].rearrange("p (j k) -> p j k", j=JC)
                act.wait_ge(lr_ps, c + 1)
                for stored in (xl_out, xr_out):
                    wait(act, stored[b], 16 * (c // 2))
                a.activation(lr_keep[:, b], rows[:, :, 0:C], ACT.Copy).then_inc(xl_kept, 1)
                a.activation(xr_parts[:, b, :, 0, :], rows[:, :, C:2 * C], ACT.Copy).then_inc(parts_set, 2)
                act.wait_ge(rest_set, c + 1)
                a.activation(xr_parts[:, b, :, 1, :], xr_rest[:, b], ACT.Copy).then_inc(parts_set, 1)

            for q in range(PARTS + 2):
                if q < PARTS:
                    square(q)
                if 1 <= q <= PARTS:
                    root(q - 1)
                for c in chunks_of(q - 2):
                    turned(c)
                    if c > 0:
                        split(c - 1)
            split(CHUNKS - 1)

            def layer1(i, s):
                y, w = behind(i, s, 1), behind(i, s, 3)
                if w is not None:
                    keep_sums(1, w[0], w[1] % 2, CD, acc1)
                if y is not None:
                    y = y[0]
                    act.wait_ge(diff_set, y + 1)
                    wait(act, ext_made, 2 * y)
                    a.activation(expt[:], diff[:], ACT.Exp).then_inc(exp_set, 1)

            each_body(act, lambda i: [layer1(i, s) for s in range(SLOTS)])
            for s in range(3):
                layer1(BODIES, s)

            for q in range(PARTS):
                act.wait_ge(cent_set, q + 1)
                wait(act, sqsum_set, q - 1)
                a.activation(sq[:, q % 2, :], y[:, q * JP * C:(q + 1) * JP * C], ACT.Square).then_inc(sq_set, 1)
            act.wait_ge(var_set, PARTS + 2)
            a.activation(stat[:, 2, :], stat[:, 2, :], ACT.Sqrt, bias=eps_bn[:, 0:1]).then_inc(std_set, 1)
            for q in range(PARTS):
                at = slice(q * JP * C, (q + 1) * JP * C)
                act.wait_ge(gelu_in, q + 1)
                a.activation(y[:, at], y[:, at], ACT.Gelu).then_inc(gelu_set, 1)

        @block.tensor
        def _(pe):
            m = nc.tensor
            pe.wait_ge(consts_f, 1)
            pe.wait_ge(onehots_set, 1)
            for k in range(BLK):
                m.matmul(ps_g[0:NP, 0, 0:NJ + 1], in_b[:, k, :], jlt[:, k, :], start=(k == 0), stop=False)
                last = m.matmul(ps_g[0:NP, 0, 0:NJ + 1], ge_b[:, k, 0:NP], ones_b[:, 0:NJ + 1], start=False, stop=(k == BLK - 1))
            last.then_inc(rows_ps, 1)

            def turn_rows(c, to):
                for k in range(JC):
                    last = m.transpose(ps_s[0:C, c % 2, k * NP:(k + 1) * NP], hs3[:, c * JC + k, :], ident[0:NP, 0:NP])
                last.then_inc(to, 1)

            pe.wait_ge(rows_set, 1)
            pe.wait_ge(h_set, 1)
            for c in range(CHUNKS + 1):
                if c < CHUNKS:
                    wait(pe, ht_set, c - 1)
                    turn_rows(c, h_t)
                if c > 0:
                    d = c - 1
                    pe.wait_ge(ht_set, d + 1)
                    wait(pe, lin_kept, d - 1)
                    for k in range(JC):
                        last = m.matmul(ps_g[0:NP, d % 2, k * C:(k + 1) * C], h_turn[0:C, d % 2, k, :], w0_s[:], start=True, stop=True)
                    last.then_inc(lin_ps, 1)

            def sums(layer, g, b, rows, rows_of, tiles=range(GT)):
                if tiles[0] == 0:
                    pe.wait_ge(oh_set[layer], g + 1)
                    wait(pe, acc_set[layer], (g - 1) * GT)
                for t in tiles:
                    last = m.matmul(ps_s[0:rows, b, t * T:(t + 1) * T], rows_of(t), oh[:, b, t, :], start=True, stop=True)
                if tiles[-1] == GT - 1:
                    last.then_inc(summed[layer], 1)

            def layer0(i, s):
                pe.wait_ge(gathered[0][s], 16 * GT * (i + 1))
                sums(0, i * SLOTS + s, s % 2, C, lambda t: gbuf[:, s, t, :])

            def build(i, k):
                pe.wait_ge(hot_set, i * K + k + 1)
                for s in (added, kept):
                    wait(pe, s, i * K + k - (1 if k > 0 else 0))
                if k == 1:
                    wait(pe, dense_set, i)
                m.matmul(built_to[k % 2][:, 0, 0:HI], lo_hot[:, k % 2, :], key_hot[:, k % 2, 0:HI], start=True, stop=True)
                m.matmul(built_to[k % 2][:, 1, 0:(DW - 1) * HI], lo_hot[:, k % 2, :], key_hot[:, k % 2, HI:DW * HI],
                         start=True, stop=True).then_inc(built, 1)

            def dense(i, between):
                by_hi = counts.rearrange("p (d h) -> p h d", h=HI)
                pe.wait_ge(added, i * K + K)
                pe.wait_ge(kept, i * K + K)
                for h in range(HI):
                    if h == HI // 4:
                        between()
                    last = m.matmul(dense_ps.rearrange("p k c -> p (k c)"), by_hi[:, h, :], table3[:, h].rearrange("p k c -> p (k c)"),
                                    start=(h == 0), stop=(h == HI - 1))
                last.then_inc(dense_made, 1)

            def dense_turn(i):
                pe.wait_ge(consts_f, 1)
                pe.wait_ge(dsum_set, i + 1)
                m.transpose(dense_t, dsum[:], ident[:]).then_inc(dsum_t, 1)

            def gathered_sums(i, s, tiles):
                if tiles[0] == 0:
                    pe.wait_ge(gathered[0][s % SLOTS0], 16 * GT * rounds(i, s))
                sums(0, i * FG + s, s % 2, C, lambda t: gbuf[:, s % SLOTS0, t, :], tiles)

            def fast0(i):
                for s, piece in enumerate(PIECES):
                    for r in range(max(LATE + GT // 2, len(piece))):
                        if r < len(piece):
                            build(i, piece[r])
                        if 0 <= r - LATE < GT // 2:
                            gathered_sums(i, s, range(2 * (r - LATE), 2 * (r - LATE) + 2))
                dense(i, lambda: gathered_sums(i, len(PIECES), range(GT)))
                dense_turn(i)
                for s in range(len(PIECES) + 1, FG):
                    gathered_sums(i, s, range(GT))

            either(pe, ENG.PE, lambda: fast_bodies(pe, fast0), lambda: each_body(pe, lambda i: [layer0(i, s) for s in range(SLOTS)]))

            pe.wait_ge(gather_done, 1)
            pe.wait_ge(dense_done, 1)
            def product(d):
                pe.wait_ge(h1t_set, d + 1)
                wait(pe, xl_kept, d - 1)
                wait(pe, xr_kept, d - 1)
                for k in range(JC):
                    last = m.matmul(ps_g[0:NP, d % 2, k * 2 * C:(k + 1) * 2 * C], h_turn[:, d % 2, k, :], wlr[:], start=True, stop=True)
                last.then_inc(lr_ps, 1)

            pe.wait_ge(ones_row, 1)
            for q in range(PARTS + 2):
                for c in chunks_of(q):
                    wait(pe, x1_set, c - 1)
                    for k in range(JC):
                        last = m.matmul(acc_to(c)[:, k * C:(k + 1) * C], acc0_n[:, c * JC + k, :], ident2[:], start=True, stop=True)
                    last.then_inc(acc_t, 1)
                for c in chunks_of(q - 2):
                    pe.wait_ge(h_set, q)
                    wait(pe, h1t_set, c - 1)
                    turn_rows(c, h1_t)
                    if c > 0:
                        product(c - 1)
            product(CHUNKS - 1)
            pe.wait_ge(xl_kept, CHUNKS)
            pe.wait_ge(xr_kept, CHUNKS)

            def layer1(i, s):
                n, y, z = (behind(i, s, lag) for lag in (0, 1, 2))
                if y is not None:
                    y, ys, yr = y
                    pe.wait_ge(consts_f, 1)
                    pe.wait_ge(logits_set, y + 1)
                    wait(pe, diff_set, y)
                    m.transpose(lt_ps, lg[:], ident[:]).then_inc(lt_made, 1)
                if z is not None:
                    z, zs, zr = z
                    zb = zs % 2
                    pe.wait_ge(consts_f, 1)
                    pe.wait_ge(exp_set, z + 1)
                    m.transpose(ext_ps, expt[:, 0:T], ident[0:GT * H, 0:GT * H]).then_inc(ext_made, 1)
                    pe.wait_ge(consts_f, 1)
                    pe.wait_ge(resc_set, z + 1)
                    m.matmul(resc_ps, by_chan[:], resc[:], start=True, stop=True).then_inc(ext_made, 1)
                if n is not None:
                    n = n[0]
                    pe.wait_ge(consts_f, 1)
                    pe.wait_ge(edge_in[s], 48 * (i + 1))
                    wait(pe, row_set, n)
                    m.matmul(rows_to, eat[:, s, :], web[:], start=True, stop=False)
                if y is not None:
                    pe.wait_ge(consts_f, 1)
                    pe.wait_ge(tails_set, y + 1)
                    m.matmul(tails_ps, by_head[:], tails[:], start=True, stop=True).then_inc(tails_made, 1)
                if n is not None:
                    pe.wait_ge(consts_f, 1)
                    pe.wait_ge(oht_set, n + 1)
                    pe.wait_ge(xrw_in[s], 16 * GT * (i + 1))
                    for t in range(GT):
                        for k in range(3):
                            last = m.matmul(rows_to[:, t * C:(t + 1) * C], oht[:, s % 2, t * T:(t + 1) * T], xrw[:, s, t, k, :],
                                            start=False, stop=(t == GT - 1 and k == 2))
                    last.then_inc(g_made, 1)
                if y is not None:
                    pe.wait_ge(consts_f, 1)
                    pe.wait_ge(beforex_set, y + 1)
                    m.matmul(hist_ps, beforex[:], ones[0:H, 0:1], start=True, stop=True).then_inc(hist_made, 1)
                if z is not None:
                    pe.wait_ge(msg_set, z + 1)
                    sums(1, z, zb, CD, lambda t: msg[:, zb, t, :])

            each_body(pe, lambda i: [layer1(i, s) for s in range(SLOTS)])
            for s in range(2):
                layer1(BODIES, s)

            pe.wait_ge(acc_set[1], GROUPS * GT)
            for c in range(ENDS + 1):
                if c < ENDS:
                    wait(pe, y_set, c - 1)
                    for k in range(JE):
                        at = k // (JE // 2) * (GE // 2) + k % (JE // 2) * CD
                        last = m.transpose(ps_s[0:NP, c % 2, at:at + CD], acc1_n[:, c * JE + k, :], ident[0:CD, 0:CD])
                    last.then_inc(num_t, 1)
                if c > 0:
                    pe.wait_ge(y_set, c)
                    for k in range(2 * c - 2, 2 * c):
                        m.matmul(ps_g[0:NP, 0, 0:JE // 2 * C], ones[0:NP, 0:NP], y[:, k * JE // 2 * C:(k + 1) * JE // 2 * C],
                                 start=(k == 0), stop=(k == 2 * ENDS - 1)).then_inc(sum_ps, 1)
            pe.wait_ge(sqsum_set, PARTS)
            for q in range(PARTS):
                last = m.matmul(ps_g[0:NP, 1, 0:C], ones[0:NP, 0:NP], sq_sum[:, q, :], start=(q == 0), stop=(q == PARTS - 1))
            last.then_inc(sqsum_ps, 1)


_INS = ["x", "src_cols", "dst_rows", "dst_cols", "first_dst", "last_dst", "edge_rows", "L0_gnn_W", "L0_gnn_b", "L1_gnn_W_l",
        "L1_gnn_b_l", "L1_gnn_W_r", "L1_gnn_b_r", "L1_gnn_W_e", "L1_gnn_att", "L1_gnn_bias", "L1_gnn_gamma", "L1_gnn_beta"]


def lay_out(inputs):
    import numpy as _np

    def tiles(a, pad):
        padded = _np.full((TILES * T,) + a.shape[1:], pad, a.dtype)
        padded[:E] = a
        return padded.reshape((TILES, T) + a.shape[1:])

    arrays = {name: _np.ascontiguousarray(a) for name, a in inputs.items()}
    src, dst = tiles(arrays.pop("src"), 0), tiles(arrays.pop("dst"), N)
    edges = tiles(arrays.pop("edge_attr_16"), 0)
    arrays["src_cols"] = _np.ascontiguousarray(src.T)
    arrays["dst_rows"], arrays["dst_cols"] = dst, _np.ascontiguousarray(dst.T)
    arrays["first_dst"], arrays["last_dst"] = _np.ascontiguousarray(dst[:, 0]), _np.ascontiguousarray(dst[:, T - 1])
    arrays["edge_rows"] = _np.ascontiguousarray(edges.transpose(0, 2, 1)).reshape(TILES * ED, T)
    return arrays


def kernel(**inputs):
    import concourse.bacc as _bacc
    from concourse import mybir as _mybir
    from concourse.bass_utils import run_bass_kernel_spmd as _run

    laid = lay_out(inputs)
    nc = _bacc.Bacc("TRN2", target_bir_lowering=False, num_devices=1)
    arrays, args = {}, []
    for name in _INS:
        a = laid[name]
        arrays[f"in_{name}_dram"] = a
        args.append(nc.dram_tensor(f"in_{name}_dram", a.shape, _mybir.dt.from_np(a.dtype), kind="ExternalInput").ap())
    args.append(nc.dram_tensor("out_dram", (N, C), F32, kind="ExternalOutput").ap())
    gnn_kernel(nc, *args)
    r = _run(nc, [arrays], core_ids=[0])
    return r.results[0]["out_dram"]
```
